# Optimizing a Trainium2 kernel written in Bass

```python
import numpy as np
import jax
import jax.numpy as jnp

def _softmax(x, axis=-1):
    return jax.nn.softmax(x, axis=axis)

def _gelu(x):
    return jax.nn.gelu(x, approximate=True)

def _silu(x):
    return jax.nn.silu(x)

def _sigmoid(x):
    return jax.nn.sigmoid(x)

def _layernorm(x, axis=-1, eps=1e-05):
    m = jnp.mean(x, axis=axis, keepdims=True)
    v = jnp.var(x, axis=axis, keepdims=True)
    return (x - m) / jnp.sqrt(v + eps)

def _scatter_add(tgt, idx, src, axis=0):
    return tgt.at[idx].add(src)

def _segment_sum(src, seg, n):
    return jax.ops.segment_sum(src, seg, n)
kernel_name = 'mk_macaron_d2_jaxref_r8_a12465'

def setup_inputs(seed: int=0):
    np.random.seed(seed)
    _w = jnp.asarray

    def _L0_attn_setup():
        import jax, jax.numpy as jnp
        import numpy as np
        D_MODEL = 128
        NUM_HEADS = 16
        D_HEAD = D_MODEL // NUM_HEADS
        LAMBDA_INIT = 0.8
        EPS = 1e-05
        key = jax.random.key(seed)
        ks = jax.random.split(key, 10)
        B, N = (2, 256)

        def xav(k, shape):
            fan_in, fan_out = (shape[0], shape[1])
            lim = np.sqrt(6.0 / (fan_in + fan_out))
            return jax.random.uniform(k, shape, jnp.float32, -lim, lim)
        return {'X': jax.random.normal(ks[0], (B, N, D_MODEL), jnp.float32), 'Wq': xav(ks[1], (D_MODEL, 2 * D_MODEL)), 'Wk': xav(ks[2], (D_MODEL, 2 * D_MODEL)), 'Wv': xav(ks[3], (D_MODEL, 2 * D_MODEL)), 'Wo': xav(ks[4], (2 * D_MODEL, D_MODEL)), 'lambda_q1': jax.random.normal(ks[5], (NUM_HEADS, D_HEAD), jnp.float32), 'lambda_k1': jax.random.normal(ks[6], (NUM_HEADS, D_HEAD), jnp.float32), 'lambda_q2': jax.random.normal(ks[7], (NUM_HEADS, D_HEAD), jnp.float32), 'lambda_k2': jax.random.normal(ks[8], (NUM_HEADS, D_HEAD), jnp.float32), 'rms_scale': jnp.ones((2 * D_HEAD,), jnp.float32)}
    _L0_attn_in = _L0_attn_setup()

    def _L0_ffn_setup():
        import jax, jax.numpy as jnp
        import numpy as np
        D_MODEL = 128
        D_FF = 512
        NUM_EXPERTS = 8
        key = jax.random.key(seed)
        ks = jax.random.split(key, 8)
        scale_in = 1.0 / np.sqrt(D_MODEL)
        scale_ff = 1.0 / np.sqrt(D_FF)
        x = jax.random.normal(ks[0], (4, 256, D_MODEL), dtype=jnp.float32)
        gate_w = jax.random.uniform(ks[1], (NUM_EXPERTS, D_MODEL), jnp.float32, -scale_in, scale_in)
        gate_b = jax.random.uniform(ks[2], (NUM_EXPERTS,), jnp.float32, -scale_in, scale_in)
        expert_bias = jnp.zeros((NUM_EXPERTS,), dtype=jnp.float32)
        w1 = jax.random.uniform(ks[3], (NUM_EXPERTS, D_MODEL, D_FF), jnp.float32, -scale_in, scale_in)
        b1 = jax.random.uniform(ks[4], (NUM_EXPERTS, D_FF), jnp.float32, -scale_in, scale_in)
        w2 = jax.random.uniform(ks[5], (NUM_EXPERTS, D_FF, D_MODEL), jnp.float32, -scale_ff, scale_ff)
        b2 = jax.random.uniform(ks[6], (NUM_EXPERTS, D_MODEL), jnp.float32, -scale_ff, scale_ff)
        return {'x': x, 'gate_w': gate_w, 'gate_b': gate_b, 'expert_bias': expert_bias, 'w1': w1, 'b1': b1, 'w2': w2, 'b2': b2}
    _L0_ffn_in = _L0_ffn_setup()

    def _L1_attn_setup():
        import jax, jax.numpy as jnp
        import numpy as np
        D_MODEL = 128
        N_HEADS = 16
        D_LATENT = 32
        HEAD_DIM = D_MODEL // N_HEADS

        def apply_rope(x):
            B, T, H, D = x.shape
            inv_freq = 1.0 / 10000.0 ** (jnp.arange(0, D, 2, dtype=jnp.float32) / D)
            t = jnp.arange(T, dtype=jnp.float32)
            freqs = t[:, None] * inv_freq[None, :]
            sin_f = jnp.sin(freqs)[None, :, None, :]
            cos_f = jnp.cos(freqs)[None, :, None, :]
            x1, x2 = jnp.split(x, 2, axis=-1)
            return jnp.concatenate([x1 * cos_f - x2 * sin_f, x1 * sin_f + x2 * cos_f], axis=-1)
        key = jax.random.key(seed)
        ks = jax.random.split(key, 10)
        B, T = (4, 512)
        s = lambda fan_in: 1.0 / np.sqrt(fan_in)
        return {'x': jax.random.normal(ks[0], (B, T, D_MODEL), dtype=jnp.float32), 'Wq': jax.random.normal(ks[1], (D_MODEL, D_MODEL), dtype=jnp.float32) * s(D_MODEL), 'bq': jnp.zeros((D_MODEL,), jnp.float32), 'Wdown': jax.random.normal(ks[2], (D_MODEL, D_LATENT), dtype=jnp.float32) * s(D_MODEL), 'bdown': jnp.zeros((D_LATENT,), jnp.float32), 'Wup': jax.random.normal(ks[3], (D_LATENT, 2 * D_MODEL), dtype=jnp.float32) * s(D_LATENT), 'bup': jnp.zeros((2 * D_MODEL,), jnp.float32), 'Wout': jax.random.normal(ks[4], (D_MODEL, D_MODEL), dtype=jnp.float32) * s(D_MODEL), 'bout': jnp.zeros((D_MODEL,), jnp.float32)}
    _L1_attn_in = _L1_attn_setup()

    def _L1_ffn_setup():
        import jax, jax.numpy as jnp
        import numpy as np
        DIM = 128
        MOE_HID = 64
        SHARED_HID = 256
        N_EXPERTS = 16
        TOP_K = 2
        NORM_TOPK_PROB = True
        key = jax.random.key(seed)
        ks = jax.random.split(key, 9)
        s = 0.02
        x = jax.random.normal(ks[0], (2, 128, DIM), dtype=jnp.float32)
        Wg = jax.random.normal(ks[1], (N_EXPERTS, DIM), dtype=jnp.float32) * s
        We_gate = jax.random.normal(ks[2], (N_EXPERTS, MOE_HID, DIM), dtype=jnp.float32) * s
        We_up = jax.random.normal(ks[3], (N_EXPERTS, MOE_HID, DIM), dtype=jnp.float32) * s
        We_down = jax.random.normal(ks[4], (N_EXPERTS, DIM, MOE_HID), dtype=jnp.float32) * s
        Ws_gate = jax.random.normal(ks[5], (SHARED_HID, DIM), dtype=jnp.float32) * s
        Ws_up = jax.random.normal(ks[6], (SHARED_HID, DIM), dtype=jnp.float32) * s
        Ws_down = jax.random.normal(ks[7], (DIM, SHARED_HID), dtype=jnp.float32) * s
        Wsg = jax.random.normal(ks[8], (1, DIM), dtype=jnp.float32) * s
        return {'x': x, 'Wg': Wg, 'We_gate': We_gate, 'We_up': We_up, 'We_down': We_down, 'Ws_gate': Ws_gate, 'Ws_up': Ws_up, 'Ws_down': Ws_down, 'Wsg': Wsg}
    _L1_ffn_in = _L1_ffn_setup()
    _d = {'L0_attn_X': _L0_attn_in['X'], 'L0_attn_Wq': _L0_attn_in['Wq'], 'L0_attn_Wk': _L0_attn_in['Wk'], 'L0_attn_Wv': _L0_attn_in['Wv'], 'L0_attn_Wo': _L0_attn_in['Wo'], 'L0_attn_lambda_q1': _L0_attn_in['lambda_q1'], 'L0_attn_lambda_k1': _L0_attn_in['lambda_k1'], 'L0_attn_lambda_q2': _L0_attn_in['lambda_q2'], 'L0_attn_lambda_k2': _L0_attn_in['lambda_k2'], 'L0_attn_rms_scale': _L0_attn_in['rms_scale'], 'L0_ffn_gate_w': _L0_ffn_in['gate_w'], 'L0_ffn_gate_b': _L0_ffn_in['gate_b'], 'L0_ffn_expert_bias': _L0_ffn_in['expert_bias'], 'L0_ffn_w1': _L0_ffn_in['w1'], 'L0_ffn_b1': _L0_ffn_in['b1'], 'L0_ffn_w2': _L0_ffn_in['w2'], 'L0_ffn_b2': _L0_ffn_in['b2'], 'L1_attn_Wq': _L1_attn_in['Wq'], 'L1_attn_bq': _L1_attn_in['bq'], 'L1_attn_Wdown': _L1_attn_in['Wdown'], 'L1_attn_bdown': _L1_attn_in['bdown'], 'L1_attn_Wup': _L1_attn_in['Wup'], 'L1_attn_bup': _L1_attn_in['bup'], 'L1_attn_Wout': _L1_attn_in['Wout'], 'L1_attn_bout': _L1_attn_in['bout'], 'L1_ffn_Wg': _L1_ffn_in['Wg'], 'L1_ffn_We_gate': _L1_ffn_in['We_gate'], 'L1_ffn_We_up': _L1_ffn_in['We_up'], 'L1_ffn_We_down': _L1_ffn_in['We_down'], 'L1_ffn_Ws_gate': _L1_ffn_in['Ws_gate'], 'L1_ffn_Ws_up': _L1_ffn_in['Ws_up'], 'L1_ffn_Ws_down': _L1_ffn_in['Ws_down'], 'L1_ffn_Wsg': _L1_ffn_in['Wsg']}
    _x0 = _d['L0_attn_X']
    _d['L0_attn_X'] = jax.random.normal(jax.random.fold_in(jax.random.key(seed), 1), (8, 512, 128), dtype=_x0.dtype)
    del _x0
    return _d

def reference(L0_attn_X, L0_attn_Wq, L0_attn_Wk, L0_attn_Wv, L0_attn_Wo, L0_attn_lambda_q1, L0_attn_lambda_k1, L0_attn_lambda_q2, L0_attn_lambda_k2, L0_attn_rms_scale, L0_ffn_gate_w, L0_ffn_gate_b, L0_ffn_expert_bias, L0_ffn_w1, L0_ffn_b1, L0_ffn_w2, L0_ffn_b2, L1_attn_Wq, L1_attn_bq, L1_attn_Wdown, L1_attn_bdown, L1_attn_Wup, L1_attn_bup, L1_attn_Wout, L1_attn_bout, L1_ffn_Wg, L1_ffn_We_gate, L1_ffn_We_up, L1_ffn_We_down, L1_ffn_Ws_gate, L1_ffn_Ws_up, L1_ffn_Ws_down, L1_ffn_Wsg):

    def _L0_attn_ref(X, Wq, Wk, Wv, Wo, lambda_q1, lambda_k1, lambda_q2, lambda_k2, rms_scale):
        import jax, jax.numpy as jnp
        import numpy as np
        D_MODEL = 128
        NUM_HEADS = 16
        D_HEAD = D_MODEL // NUM_HEADS
        LAMBDA_INIT = 0.8
        EPS = 1e-05
        B, N, _ = X.shape
        H, Dh = (NUM_HEADS, D_HEAD)
        Q = (X @ Wq).reshape(B, N, H, 2 * Dh).transpose(0, 2, 1, 3)
        K = (X @ Wk).reshape(B, N, H, 2 * Dh).transpose(0, 2, 1, 3)
        V = (X @ Wv).reshape(B, N, H, 2 * Dh).transpose(0, 2, 1, 3)
        Q1, Q2 = (Q[..., :Dh], Q[..., Dh:])
        K1, K2 = (K[..., :Dh], K[..., Dh:])
        lam = jnp.exp(jnp.sum(lambda_q1 * lambda_k1, -1)) - jnp.exp(jnp.sum(lambda_q2 * lambda_k2, -1)) + LAMBDA_INIT
        scaling = 1.0 / np.sqrt(Dh)
        causal = jnp.tril(jnp.ones((N, N), bool))
        neg_inf = jnp.float32(-jnp.inf)
        A1 = jnp.einsum('bhqd,bhkd->bhqk', Q1, K1) * scaling
        A2 = jnp.einsum('bhqd,bhkd->bhqk', Q2, K2) * scaling
        A1 = jnp.where(causal, A1, neg_inf)
        A2 = jnp.where(causal, A2, neg_inf)
        attn = jax.nn.softmax(A1, axis=-1) - lam[None, :, None, None] * jax.nn.softmax(A2, axis=-1)
        O = jnp.einsum('bhqk,bhkd->bhqd', attn, V)
        rms = jnp.sqrt(jnp.mean(O * O, axis=-1, keepdims=True) + EPS)
        O = O / rms * rms_scale
        O = O * (1.0 - LAMBDA_INIT)
        O = O.transpose(0, 2, 1, 3).reshape(B, N, H * 2 * Dh)
        return O @ Wo

    def _L0_ffn_ref(x, gate_w, gate_b, expert_bias, w1, b1, w2, b2):
        import jax, jax.numpy as jnp
        import numpy as np
        D_MODEL = 128
        D_FF = 512
        NUM_EXPERTS = 8
        gate_logits = jnp.einsum('bsd,ed->bse', x, gate_w) + gate_b + expert_bias
        top_idx = jnp.argmax(gate_logits, axis=-1)
        out = jnp.zeros_like(x)
        for e in range(NUM_EXPERTS):
            mask = (top_idx == e)[..., None].astype(x.dtype)
            h = jax.nn.relu(jnp.einsum('bsd,df->bsf', x, w1[e]) + b1[e])
            y = jnp.einsum('bsf,fd->bsd', h, w2[e]) + b2[e]
            out = out + mask * y
        return out

    def _L1_attn_ref(x, Wq, bq, Wdown, bdown, Wup, bup, Wout, bout):
        import jax, jax.numpy as jnp
        import numpy as np
        D_MODEL = 128
        N_HEADS = 16
        D_LATENT = 32
        HEAD_DIM = D_MODEL // N_HEADS

        def apply_rope(x):
            B, T, H, D = x.shape
            inv_freq = 1.0 / 10000.0 ** (jnp.arange(0, D, 2, dtype=jnp.float32) / D)
            t = jnp.arange(T, dtype=jnp.float32)
            freqs = t[:, None] * inv_freq[None, :]
            sin_f = jnp.sin(freqs)[None, :, None, :]
            cos_f = jnp.cos(freqs)[None, :, None, :]
            x1, x2 = jnp.split(x, 2, axis=-1)
            return jnp.concatenate([x1 * cos_f - x2 * sin_f, x1 * sin_f + x2 * cos_f], axis=-1)
        B, T, D = x.shape
        H, Dh = (N_HEADS, HEAD_DIM)
        q = x @ Wq + bq
        kv_latent = x @ Wdown + bdown
        kv = kv_latent @ Wup + bup
        q = q.reshape(B, T, H, Dh)
        kv = kv.reshape(B, T, H, 2 * Dh)
        k, v = jnp.split(kv, 2, axis=-1)
        q = apply_rope(q)
        k = apply_rope(k)
        att = jnp.einsum('bthd,btgd->bthg', q, k) / jnp.sqrt(jnp.float32(Dh))
        att = jax.nn.softmax(att, axis=-1)
        out = jnp.einsum('bthg,btgd->bthd', att, v)
        out = out.reshape(B, T, D)
        return out @ Wout + bout

    def _L1_ffn_ref(x, Wg, We_gate, We_up, We_down, Ws_gate, Ws_up, Ws_down, Wsg):
        import jax, jax.numpy as jnp
        import numpy as np
        DIM = 128
        MOE_HID = 64
        SHARED_HID = 256
        N_EXPERTS = 16
        TOP_K = 2
        NORM_TOPK_PROB = True
        B, S, D = x.shape
        xt = x.reshape(-1, D)
        gates = jax.nn.softmax(xt @ Wg.T, axis=-1)
        scores, inds = jax.lax.top_k(gates, TOP_K)
        if NORM_TOPK_PROB:
            scores = scores / jnp.sum(scores, axis=-1, keepdims=True)
        g = jnp.einsum('td,ehd->teh', xt, We_gate)
        u = jnp.einsum('td,ehd->teh', xt, We_up)
        h = jax.nn.silu(g) * u
        y_all = jnp.einsum('teh,edh->ted', h, We_down)
        y_sel = jnp.take_along_axis(y_all, inds[:, :, None], axis=1)
        y = jnp.sum(y_sel * scores[:, :, None], axis=1)
        shared = jax.nn.silu(xt @ Ws_gate.T) * (xt @ Ws_up.T) @ Ws_down.T
        y = y + jax.nn.sigmoid(xt @ Wsg.T) * shared
        return y.reshape(B, S, D)
    x = L0_attn_X
    x = x + 0.5 * _L0_ffn_ref(_layernorm(x, axis=-1), L0_ffn_gate_w, L0_ffn_gate_b, L0_ffn_expert_bias, L0_ffn_w1, L0_ffn_b1, L0_ffn_w2, L0_ffn_b2)
    x = x + _L0_attn_ref(_layernorm(x, axis=-1), L0_attn_Wq, L0_attn_Wk, L0_attn_Wv, L0_attn_Wo, L0_attn_lambda_q1, L0_attn_lambda_k1, L0_attn_lambda_q2, L0_attn_lambda_k2, L0_attn_rms_scale)
    x = x + 0.5 * _L0_ffn_ref(_layernorm(x, axis=-1), L0_ffn_gate_w, L0_ffn_gate_b, L0_ffn_expert_bias, L0_ffn_w1, L0_ffn_b1, L0_ffn_w2, L0_ffn_b2)
    x = x + 0.5 * _L1_ffn_ref(_layernorm(x, axis=-1), L1_ffn_Wg, L1_ffn_We_gate, L1_ffn_We_up, L1_ffn_We_down, L1_ffn_Ws_gate, L1_ffn_Ws_up, L1_ffn_Ws_down, L1_ffn_Wsg)
    x = x + _L1_attn_ref(_layernorm(x, axis=-1), L1_attn_Wq, L1_attn_bq, L1_attn_Wdown, L1_attn_bdown, L1_attn_Wup, L1_attn_bup, L1_attn_Wout, L1_attn_bout)
    x = x + 0.5 * _L1_ffn_ref(_layernorm(x, axis=-1), L1_ffn_Wg, L1_ffn_We_gate, L1_ffn_We_up, L1_ffn_We_down, L1_ffn_Ws_gate, L1_ffn_Ws_up, L1_ffn_Ws_down, L1_ffn_Wsg)
    return x

_drawn_inputs = setup_inputs


def setup_inputs(seed=0):
    import zlib

    import numpy as np

    out = dict(_drawn_inputs(seed))
    spreads = {'L0_attn_rms_scale': (1.0, 0.2),
     'L0_ffn_expert_bias': (0.0, 0.1),
     'L1_attn_bq': (0.0, 0.284),
     'L1_attn_bdown': (0.0, 0.1),
     'L1_attn_bup': (0.0, 0.1),
     'L1_attn_bout': (0.0, 0.1)}
    factors = {'L1_ffn_Wg': 8.0,
     'L1_ffn_We_gate': 8.0,
     'L1_ffn_We_up': 8.0,
     'L1_ffn_We_down': 8.0,
     'L1_ffn_Ws_gate': 8.0,
     'L1_ffn_Ws_up': 8.0,
     'L1_ffn_Ws_down': 8.0,
     'L1_ffn_Wsg': 8.0}
    for name, (base, spread) in spreads.items():
        noise = np.random.default_rng([zlib.crc32(name.encode()), seed]).standard_normal(out[name].shape)
        drawn = base * np.exp(spread * noise) if base else spread * noise
        out[name] = jnp.asarray(drawn.astype(out[name].dtype))
    for name, factor in factors.items():
        out[name] = (out[name] * factor).astype(out[name].dtype)
    return out
```

```python
from contextlib import ExitStack

import numpy as np

import concourse.bass as bass
from concourse import mybir

F32 = mybir.dt.float32
BF16 = mybir.dt.bfloat16
ALU = mybir.AluOpType
ACT = mybir.ActivationFunctionType
AX = mybir.AxisListType

P = 128
D = 128
T = 512
J = T // P
EPS = 1e-5
LAMBDA_INIT = 0.8


class Chain:

    def __init__(self, eng, sem, per):
        self.eng, self.sem, self.per, self.base, self.n = eng, sem, per, 0, 0

    def start(self, b):
        self.base, self.n = b * self.per, 0

    def mark(self, ins):
        self.n += 1
        return ins.then_inc(self.sem, 1)

    def after(self, ins):
        self.mark(ins)
        self.eng.wait_ge(self.sem, self.base + self.n)

    def end(self):
        assert self.n == self.per, (self.n, self.per)


def along(ap, n):
    return ap.rearrange("p (a o) -> p a o", o=1).broadcast_to([ap.shape[0], ap.shape[1], n])


def over(ap, n):
    return ap.rearrange("p (o a) -> p o a", o=1).broadcast_to([ap.shape[0], n, ap.shape[1]])


def two_batches(eng, turns, body):
    with eng.Fori(0, turns) as turn:
        for par in range(2):
            body(2 * turn + par, par)


class Stage:

    def __init__(self, nc, ctx, name, src, dst, consts):
        self.nc, self.ctx, self.name, self.src, self.dst, self.consts = nc, ctx, name, src, dst, consts
        self.NB = src.shape[0]
        self.sems = []
        assert self.NB % 2 == 0 and self.NB >= 4
        self.x_in = self.sb("x_in", [P, 2, J, D], F32)
        self.stats = self.sb("stats", [P, J, 6], F32)
        self.mean_var = self.sb("mean_var", [P, J, 2], F32)
        self.var_eps = self.sb("var_eps", [P, J], F32)
        self.rstd = self.sb("rstd", [P, J], F32)
        self.x_centred = self.sb("x_centred", [P, J, D], F32)
        self.x_hat = self.sb("x_hat", [P, J, D], F32)
        self.xT = self.sb("xT", [P, 2, T], F32)
        self.x_out = self.sb("x_out", [P, 2, J, D], F32)
        self.misc = self.ps("misc", [P, T], F32)
        self.x_loaded = [self.sem(f"x_loaded{par}") for par in range(2)]
        self.stats_done = self.sem("stats_done")
        self.mean_var_ready = self.sem("mean_var_ready")
        self.norm_step = self.sem("norm_step")
        self.x_hat_ready = self.sem("x_hat_ready")
        self.xT_in_psum = self.sem("xT_in_psum")
        self.xT_ready = self.sem("xT_ready")
        self.residual_free = self.sem("residual_free")
        self.x_out_free = [self.sem(f"x_out_free{par}") for par in range(2)]
        self.tick = self.sem("tick")
        self.weights_loaded = self.sem("weights_loaded")
        self.n_weights = 0

    def sb(self, name, shape, dt):
        return self.ctx.enter_context(self.nc.sbuf_tensor(f"{self.name}_{name}", shape, dt))

    def ps(self, name, shape, dt):
        return self.ctx.enter_context(self.nc.psum_tensor(f"{self.name}_{name}", shape, dt))

    def sem(self, name):
        self.sems.append(self.nc.alloc_semaphore(f"{self.name}_{name}"))
        return self.sems[-1]

    def finish(self):
        self.nc.clear_and_free_semaphores(self.sems)
        self.nc.all_engine_barrier()

    def load_weight(self, sp, dst, src):
        sp.dma_start(dst, src).then_inc(self.weights_loaded, 16)
        self.n_weights += 1

    def wait_weights(self, eng):
        eng.wait_ge(self.weights_loaded, 16 * self.n_weights)

    def load_x(self, sp, b, par):
        sp.dma_start(self.x_in[:, par], self.src[b].rearrange("(j p) d -> p j d", p=P)).then_inc(self.x_loaded[par], 16)

    def store_x(self, sp, b, par):
        sp.wait_ge(self.residual_free, b + 2)
        sp.dma_start(self.dst[b].rearrange("(j p) d -> p j d", p=P), self.x_out[:, par]).then_inc(self.x_out_free[par], 16)

    def stream(self, sp):
        for par in range(2):
            sp.sem_inc(self.x_out_free[par], 16)
        def body(b, par):
            self.store_x(sp, b, par)
            self.load_x(sp, b + 2, par)
        two_batches(sp, self.NB // 2 - 1, body)
        self.store_x(sp, self.NB - 2, 0)
        self.load_x(sp, 0, 0)
        self.store_x(sp, self.NB - 1, 1)
        for par in range(2):
            sp.wait_ge(self.x_out_free[par], 16 + 8 * self.NB)
        sp.wait_ge(self.x_loaded[0], 8 * self.NB + 16)

    def norm_stats(self, dve, b, par):
        nc = self.nc
        dve.wait_ge(self.x_loaded[par], 8 * (b - par) + 16)
        for j in range(J):
            last = nc.vector.bn_stats(self.stats[:, j, :], self.x_in[:, par, j, :])
        last.then_inc(self.stats_done, 1)
        dve.wait_ge(self.stats_done, b + 1)
        dve.sem_inc(self.tick, 1)
        for j in range(J):
            last = nc.vector.bn_aggr(self.mean_var[:, j, :], self.stats[:, j, :])
        last.then_inc(self.mean_var_ready, 1)

    def norm_apply(self, pool, b, par):
        nc, c = self.nc, self.consts
        pool.wait_ge(self.mean_var_ready, b + 1)
        nc.gpsimd.tensor_tensor(self.var_eps[:, :], self.mean_var[:, :, 1], c["eps"][:, 0:J], ALU.add)\
            .then_inc(self.norm_step, 1)
        nc.gpsimd.tensor_tensor(self.x_centred[:, :, :], self.x_in[:, par], along(self.mean_var[:, :, 0], D), ALU.subtract)\
            .then_inc(self.norm_step, 1)
        pool.wait_ge(self.norm_step, 3 * b + 2)
        nc.gpsimd.tensor_tensor(self.rstd[:, :], self.var_eps[:, :], c["minus_half"][:, 0:J], ALU.pow)\
            .then_inc(self.norm_step, 1)
        pool.wait_ge(self.norm_step, 3 * b + 3)
        nc.gpsimd.tensor_tensor(self.x_hat[:, :, :], self.x_centred[:, :, :],
                                along(self.rstd[:, :], D), ALU.mult).then_inc(self.x_hat_ready, 1)

    def norm_transpose(self, pe, b, first=False):
        pe.wait_ge(self.x_hat_ready, b + 1)
        if not first:
            pe.wait_ge(self.residual_free, b)
        for j in range(J):
            last = self.nc.tensor.transpose(self.misc[:, j * P:(j + 1) * P], self.x_hat[:, j, :], self.consts["ident"][:, :])
        last.then_inc(self.xT_in_psum, 1)

    def norm_store(self, act, b, par):
        act.wait_ge(self.xT_in_psum, b + 1)
        self.nc.scalar.activation(self.xT[:, par], self.misc[:, :], ACT.Copy).then_inc(self.xT_ready, 1)



def moe_top1_stage(nc, name, src, dst, consts, w):
    E, _, F = w["w1"].shape
    C = F // P
    with ExitStack() as ctx:
        st = Stage(nc, ctx, name, src, dst, consts)
        sb, ps, sem, misc, xT = st.sb, st.ps, st.sem, st.misc, st.xT
        w1 = sb("w1", [P, E, F], F32)
        w2 = sb("w2", [P, E, C, D], F32)
        b1 = sb("b1", [P, E, C], F32)
        b2 = sb("b2", [P, E], F32)
        gate_w = sb("gate_w", [P, E], F32)
        gate_b = sb("gate_b", [P, E], F32)
        expert_bias = sb("expert_bias", [P, E], F32)
        h = sb("h", [P, 2, C, T], F32)
        mask = sb("mask", [P, 2, T], F32)
        masked = sb("masked", [P, 2, T], F32)
        acc = sb("acc", [P, 2, T], F32)
        onehotT = sb("onehotT", [E, 2, T], BF16)
        onehot = sb("onehot", [P, J, E], BF16)
        logits_g = sb("logits_g", [P, J, E], F32)
        logits = sb("logits", [P, J, E], F32)
        at_max = sb("at_max", [P, J, E], F32)
        ranked = sb("ranked", [P, J, E], F32)
        best = sb("best", [P, J], F32)
        best_rank = sb("best_rank", [P, J], F32)
        h_psum = ps("h_psum", [P, C, T], F32)
        y_psum = ps("y_psum", [P, 2, T], F32)
        mask_psum = ps("mask_psum", [P, T], F32)
        pick, rank, ident, ident16 = consts["pick"], consts["rank"], consts["ident"], consts["ident16"]

        h_in_psum = sem("h_in_psum")
        h_ready = sem("h_ready")
        y_in_psum = sem("y_in_psum")
        y_free = sem("y_free")
        mask_in_psum = sem("mask_in_psum")
        mask_free = sem("mask_free")
        acc_step = sem("acc_step")
        acc_ready = sem("acc_ready")
        logits_in_psum = sem("logits_in_psum")
        gate_step = sem("gate_step")
        onehot_ready = sem("onehot_ready")
        onehotT_in_psum = sem("onehotT_in_psum")
        onehotT_ready = sem("onehotT_ready")
        out_in_psum = sem("out_in_psum")

        with nc.Block() as block:

            @block.sync
            def _(sp):
                st.load_x(sp, 0, 0)
                st.load_weight(sp, gate_w[:, :], w["gate_w"])
                st.load_weight(sp, gate_b[:, :], w["gate_b"].rearrange("(o e) -> o e", o=1).broadcast_to([P, E]))
                st.load_weight(sp, expert_bias[:, :],
                               w["expert_bias"].rearrange("(o e) -> o e", o=1).broadcast_to([P, E]))
                st.load_weight(sp, b1[:, :, :], w["b1"])
                st.load_weight(sp, b2[:, :], w["b2"])
                st.load_x(sp, 1, 1)
                for e in range(E):
                    st.load_weight(sp, w1[:, e, :], w["w1"][e])
                    st.load_weight(sp, w2[:, e, :, :], w["w2"][e].rearrange("(c p) d -> p c d", p=P))
                st.stream(sp)

            @block.gpsimd
            def _(pool):
                st.norm_apply(pool, 0, 0)
                two_batches(pool, st.NB // 2, lambda b, par: st.norm_apply(pool, b + 1, 1 - par))

            @block.tensor
            def _(pe):
                def hidden(b, par, e, first=False):
                    if e == 0:
                        pe.wait_ge(st.xT_ready, b + 1)
                    for c in range(C):
                        if not first:
                            pe.wait_ge(h_ready, C * E * b + C * (e - 1) + c + 1)
                        nc.tensor.matmul(h_psum[:, c, :], w1[:, e, c * P:(c + 1) * P], xT[:, par],
                                         start=True, stop=True).then_inc(h_in_psum, 1)

                def mask_row(b, par, e):
                    if e == 0:
                        pe.wait_ge(onehotT_ready, b + 1)
                    pe.wait_ge(mask_free, E * b + e + 1)
                    pe.sem_inc(st.tick, 1)
                    nc.tensor.matmul(mask_psum[:, :], pick[0:E, e, :], onehotT[:, par], start=True, stop=True)\
                        .then_inc(mask_in_psum, 1)

                def output(b, e):
                    pe.wait_ge(y_free, E * b + e + 1)
                    for c in range(C):
                        pe.wait_ge(h_ready, C * (E * b + e) + c + 1)
                        last = nc.tensor.matmul(y_psum[:, e % 2, :], w2[:, e, c, :], h[:, e % 2, c, :],
                                                start=(c == 0), stop=(c == C - 1))
                    last.then_inc(y_in_psum, 1)

                def gate(b, par):
                    pe.wait_ge(st.xT_ready, b + 1)
                    for j in range(J):
                        last = nc.tensor.matmul(misc[:, j * E:(j + 1) * E], xT[:, par, j * P:(j + 1) * P],
                                                gate_w[:, :], start=True, stop=True)
                    last.then_inc(logits_in_psum, 1)

                def turn_onehot(b):
                    pe.wait_ge(onehot_ready, b + 1)
                    for j in range(J):
                        last = nc.tensor.transpose(misc[0:E, j * P // 2:(j + 1) * P // 2].bitcast(BF16),
                                                   onehot[:, j, :], ident16[:, :])
                    last.then_inc(onehotT_in_psum, 1)

                def turn_out(b, par):
                    pe.wait_ge(acc_ready, b + 1)
                    for j in range(J):
                        last = nc.tensor.transpose(misc[:, j * P:(j + 1) * P], acc[:, par, j * P:(j + 1) * P],
                                                   ident[:, :])
                    last.then_inc(out_in_psum, 1)

                def body(b, par):
                    for e in range(1, E):
                        hidden(b, par, e)
                        mask_row(b, par, e)
                        if e == 3:
                            st.norm_transpose(pe, b + 1)
                        if e == 5:
                            gate(b + 1, 1 - par)
                        if e == 7:
                            turn_onehot(b + 1)
                        output(b, e - 1)
                    hidden(b + 1, 1 - par, 0)
                    output(b, E - 1)
                    mask_row(b + 1, 1 - par, 0)
                    turn_out(b, par)

                st.wait_weights(pe)
                st.norm_transpose(pe, 0, first=True)
                gate(0, 0)
                turn_onehot(0)
                hidden(0, 0, 0, first=True)
                mask_row(0, 0, 0)
                two_batches(pe, st.NB // 2, body)

            @block.scalar
            def _(act):
                def relus(b, e):
                    for c in range(C):
                        act.wait_ge(h_in_psum, C * (E * b + e) + c + 1)
                        nc.scalar.activation(h[:, e % 2, c, :], h_psum[:, c, :], ACT.Relu, bias=b1[:, e, c:c + 1])\
                            .then_inc(h_ready, 1)

                def copy_mask(b, e):
                    act.wait_ge(mask_in_psum, E * b + e + 1)
                    act.wait_ge(y_free, E * b + e + 1)
                    nc.scalar.activation(mask[:, e % 2, :], mask_psum[:, :], ACT.Copy).then_inc(mask_free, 1)

                def store_onehotT(b, par):
                    act.wait_ge(onehotT_in_psum, b + 1)
                    nc.scalar.activation(onehotT[:, par], misc[0:E, 0:T // 2].bitcast(BF16), ACT.Copy)\
                        .then_inc(onehotT_ready, 1)

                def body(b, par):
                    for e in range(1, E):
                        relus(b, e)
                        copy_mask(b, e)
                        if e == 3:
                            st.norm_store(act, b + 1, 1 - par)
                        if e == 7:
                            store_onehotT(b + 1, 1 - par)
                    relus(b + 1, 0)
                    copy_mask(b + 1, 0)

                st.wait_weights(act)
                act.sem_inc(mask_free, 1)
                st.norm_store(act, 0, 0)
                store_onehotT(0, 0)
                relus(0, 0)
                copy_mask(0, 0)
                two_batches(act, st.NB // 2, body)

            @block.vector
            def _(dve):
                gate_chain = Chain(dve, gate_step, 6)
                acc_chain = Chain(dve, acc_step, E - 2)

                def choose(b):
                    dve.wait_ge(logits_in_psum, b + 1)
                    gate_chain.start(b)
                    do = gate_chain.after
                    do(nc.vector.tensor_tensor(logits_g[:, :, :], misc[:, 0:J * E].rearrange("p (j e) -> p j e", j=J),
                                               over(gate_b[:, :], J), ALU.add))
                    do(nc.vector.tensor_tensor(logits[:, :, :], logits_g[:, :, :], over(expert_bias[:, :], J), ALU.add))
                    do(nc.vector.tensor_reduce(best[:, :], logits[:, :, :], AX.X, ALU.max))
                    do(nc.vector.tensor_tensor(at_max[:, :, :], logits[:, :, :], along(best[:, :], E), ALU.is_ge))
                    do(nc.vector.tensor_tensor(ranked[:, :, :], at_max[:, :, :], over(rank[:, 0:E], J), ALU.mult))
                    do(nc.vector.tensor_reduce(best_rank[:, :], ranked[:, :, :], AX.X, ALU.max))
                    gate_chain.end()
                    nc.vector.tensor_tensor(onehot[:, :, :], ranked[:, :, :], along(best_rank[:, :], E), ALU.is_equal)\
                        .then_inc(onehot_ready, 1)

                def add_output(b, par, e):
                    if e == 0:
                        acc_chain.start(b)
                    dve.wait_ge(y_in_psum, E * b + e + 1)
                    dve.wait_ge(mask_free, E * b + e + 2)
                    out = acc[:, par] if e == 0 else masked[:, e % 2, :]
                    nc.vector.scalar_tensor_tensor(out=out, in0=y_psum[:, e % 2, :], scalar=b2[:, e:e + 1],
                                                   in1=mask[:, e % 2, :], op0=ALU.add, op1=ALU.mult)\
                        .then_inc(y_free, 1)
                    if e > 0:
                        dve.wait_ge(y_free, E * b + e + 3)
                        ins = nc.vector.tensor_tensor(acc[:, par], acc[:, par], masked[:, e % 2, :], ALU.add)
                        if e == E - 1:
                            ins.then_inc(acc_ready, 1)
                        else:
                            acc_chain.after(ins)

                def add_residual(b, par):
                    dve.wait_ge(out_in_psum, b + 1)
                    dve.wait_ge(st.x_out_free[par], 8 * (b - par) + 16)
                    nc.vector.scalar_tensor_tensor(out=st.x_out[:, par].rearrange("p j d -> p (j d)"),
                                                   in0=misc[:, :], scalar=0.5,
                                                   in1=st.x_in[:, par].rearrange("p j d -> p (j d)"),
                                                   op0=ALU.mult, op1=ALU.add).then_inc(st.residual_free, 1)

                def body(b, par):
                    for e in range(1, E):
                        add_output(b, par, e - 1)
                        if e == 1:
                            st.norm_stats(dve, b + 1, 1 - par)
                        if e == 5:
                            choose(b + 1)
                    add_output(b, par, E - 1)
                    add_residual(b, par)

                dve.sem_inc(y_free, 2)
                dve.sem_inc(st.residual_free, 1)
                st.wait_weights(dve)
                st.norm_stats(dve, 0, 0)
                choose(0)
                two_batches(dve, st.NB // 2, body)

        st.finish()




def moe_top2_stage(nc, name, src, dst, consts, w):
    E = w["router"].shape[1] - 1
    K = w["gate"].shape[1]
    L = w["router"].shape[1]
    S = 32
    assert L == E + 1 and L <= S
    with ExitStack() as ctx:
        st = Stage(nc, ctx, name, src, dst, consts)
        sb, ps, sem, misc, xT = st.sb, st.ps, st.sem, st.misc, st.xT
        router = sb("router", [P, L], F32)
        w_gate = sb("w_gate", [P, K, P], F32)
        w_up = sb("w_up", [P, K, P], F32)
        w_down = sb("w_down", [P, K, D], F32)
        silu = sb("silu", [P, 2, T], F32)
        weight = sb("weight", [P, 2, T], F32)
        gated = sb("gated", [P, 2, T], F32)
        h = sb("h", [P, 2, T], F32)
        acc = sb("acc", [P, 2, T], F32)
        exp_in = sb("exp_in", [P, J, L], F32)
        exp_out = sb("exp_out", [P, J, L], F32)
        gates = sb("gates", [P, J, E], F32)
        gates_rest = sb("gates_rest", [P, J, E], F32)
        at_max = sb("at_max", [P, J, E], F32)
        ranked = sb("ranked", [P, J, E], F32)
        first = sb("first", [P, J, E], F32)
        second = sb("second", [P, J, E], F32)
        small = {n: sb(n, [P, J], F32) for n in
                 ("top", "total", "inv_total", "best", "rank1", "next_best", "rank2", "both", "inv_both", "shared_den")}
        token_w = sb("token_w", [P, J, L], F32)
        rest1 = sb("rest1", [P, J, L], F32)
        parts = sb("parts", [P, J, 3 * S], BF16)
        partsT = sb("partsT", [3 * S, 2, T], BF16)
        g_psum = ps("g_psum", [P, 2, T], F32)
        u_psum = ps("u_psum", [P, 2, T], F32)
        w_psum = ps("w_psum", [P, 2, T], F32)
        y_psum = ps("y_psum", [P, T], F32)
        spread, rank, ident, ident16 = consts["spread"], consts["rank"], consts["ident"], consts["ident16"]

        g_in_psum = sem("g_in_psum")
        u_in_psum = sem("u_in_psum")
        w_in_psum = sem("w_in_psum")
        silu_ready = sem("silu_ready")
        weight_ready = sem("weight_ready")
        gated_free = sem("gated_free")
        h_ready = sem("h_ready")
        h_free = sem("h_free")
        acc_ready = sem("acc_ready")
        parts_zeroed = sem("parts_zeroed")
        logits_in_psum = sem("logits_in_psum")
        exp_in_ready = sem("exp_in_ready")
        exp_ready = sem("exp_ready")
        gate_step = sem("gate_step")
        parts_ready = sem("parts_ready")
        partsT_in_psum = sem("partsT_in_psum")
        partsT_ready = sem("partsT_ready")
        out_in_psum = sem("out_in_psum")

        with nc.Block() as block:

            @block.sync
            def _(sp):
                st.load_x(sp, 0, 0)
                st.load_weight(sp, router[:, :], w["router"])
                st.load_weight(sp, w_gate[:, :, :], w["gate"])
                st.load_weight(sp, w_up[:, :, :], w["up"])
                st.load_x(sp, 1, 1)
                st.load_weight(sp, w_down[:, :, :], w["down"])
                st.stream(sp)

            @block.gpsimd
            def _(pool):
                nc.gpsimd.memset(parts[:, :, :], 0.0).then_inc(parts_zeroed, 1)
                st.norm_apply(pool, 0, 0)
                two_batches(pool, st.NB // 2, lambda b, par: st.norm_apply(pool, b + 1, 1 - par))

            @block.tensor
            def _(pe):
                def hidden(b, par, k, start=False):
                    n = K * b + k
                    if k == 0:
                        pe.wait_ge(st.xT_ready, b + 1)
                    if not start:
                        pe.wait_ge(silu_ready, n - 1)
                    nc.tensor.matmul(g_psum[:, k % 2, :], w_gate[:, k, :], xT[:, par], start=True, stop=True)\
                        .then_inc(g_in_psum, 1)
                    pe.wait_ge(gated_free, n + 1)
                    nc.tensor.matmul(u_psum[:, k % 2, :], w_up[:, k, :], xT[:, par], start=True, stop=True)\
                        .then_inc(u_in_psum, 1)
                    if k == 0:
                        pe.wait_ge(partsT_ready, b + 1)
                    if not start:
                        pe.wait_ge(weight_ready, n - 1)
                    pe.sem_inc(st.tick, 1)
                    nc.tensor.matmul(w_psum[:, k % 2, :], spread[:, k, :], partsT[:, par], start=True, stop=True)\
                        .then_inc(w_in_psum, 1)

                def down(b, k):
                    pe.wait_ge(h_ready, K * b + k + 1)
                    nc.tensor.matmul(y_psum[:, :], w_down[:, k, :], h[:, k % 2, :],
                                     start=(k == 0), stop=(k == K - 1)).then_inc(h_free, 1)

                def gate(b, par):
                    pe.wait_ge(st.xT_ready, b + 1)
                    for j in range(J):
                        last = nc.tensor.matmul(misc[:, j * L:(j + 1) * L], xT[:, par, j * P:(j + 1) * P],
                                                router[:, :], start=True, stop=True)
                    last.then_inc(logits_in_psum, 1)

                def turn_parts(b):
                    pe.wait_ge(parts_ready, b + 1)
                    for j in range(J):
                        last = nc.tensor.transpose(misc[0:3 * S, j * P // 2:(j + 1) * P // 2].bitcast(BF16),
                                                   parts[:, j, :], ident16[:, :])
                    last.then_inc(partsT_in_psum, 1)

                def turn_out(b, par):
                    pe.wait_ge(acc_ready, b + 1)
                    for j in range(J):
                        last = nc.tensor.transpose(misc[:, j * P:(j + 1) * P], acc[:, par, j * P:(j + 1) * P],
                                                   ident[:, :])
                    last.then_inc(out_in_psum, 1)

                def body(b, par):
                    for k in range(2, K):
                        hidden(b, par, k)
                        if k == 3:
                            st.norm_transpose(pe, b + 1)
                        if k == 5:
                            gate(b + 1, 1 - par)
                        if k == 9:
                            turn_parts(b + 1)
                        down(b, k - 2)
                    hidden(b + 1, 1 - par, 0)
                    down(b, K - 2)
                    hidden(b + 1, 1 - par, 1)
                    down(b, K - 1)
                    turn_out(b, par)

                st.wait_weights(pe)
                st.norm_transpose(pe, 0, first=True)
                gate(0, 0)
                turn_parts(0)
                hidden(0, 0, 0, start=True)
                hidden(0, 0, 1, start=True)
                two_batches(pe, st.NB // 2, body)

            @block.scalar
            def _(act):
                def chunk(b, k, start=False):
                    n = K * b + k
                    act.wait_ge(g_in_psum, n + 1)
                    act.wait_ge(gated_free, n + 1)
                    nc.scalar.activation(silu[:, k % 2, :], g_psum[:, k % 2, :], ACT.Silu).then_inc(silu_ready, 1)
                    act.wait_ge(w_in_psum, n + 1)
                    if not start:
                        act.wait_ge(h_ready, n - 1)
                    nc.scalar.activation(weight[:, k % 2, :], w_psum[:, k % 2, :], ACT.Copy).then_inc(weight_ready, 1)

                def exponentials(b):
                    act.wait_ge(exp_in_ready, b + 1)
                    nc.scalar.activation(exp_out[:, :, :], exp_in[:, :, :], ACT.Exp).then_inc(exp_ready, 1)

                def store_partsT(b, par):
                    act.wait_ge(partsT_in_psum, b + 1)
                    nc.scalar.activation(partsT[:, par], misc[0:3 * S, 0:T // 2].bitcast(BF16), ACT.Copy)\
                        .then_inc(partsT_ready, 1)

                def store_y(b, par):
                    act.wait_ge(h_free, K * b + K + 2)
                    nc.scalar.activation(acc[:, par], y_psum[:, :], ACT.Copy).then_inc(acc_ready, 1)

                def body(b, par):
                    for k in range(2, K):
                        chunk(b, k)
                        if k == 3:
                            st.norm_store(act, b + 1, 1 - par)
                        if k == 5:
                            exponentials(b + 1)
                        if k == 9:
                            store_partsT(b + 1, 1 - par)
                    chunk(b + 1, 0)
                    chunk(b + 1, 1)
                    store_y(b, par)

                st.wait_weights(act)
                st.norm_store(act, 0, 0)
                exponentials(0)
                store_partsT(0, 0)
                chunk(0, 0, start=True)
                chunk(0, 1, start=True)
                two_batches(act, st.NB // 2, body)

            @block.vector
            def _(dve):
                gate_chain = Chain(dve, gate_step, 25)

                def first_at(do, values, top, rank_of_top, onehot):
                    do(nc.vector.tensor_reduce(top[:, :], values[:, :, :], AX.X, ALU.max))
                    do(nc.vector.tensor_tensor(at_max[:, :, :], values[:, :, :], along(top[:, :], E), ALU.is_ge))
                    do(nc.vector.tensor_tensor(ranked[:, :, :], at_max[:, :, :], over(rank[:, 0:E], J), ALU.mult))
                    do(nc.vector.tensor_reduce(rank_of_top[:, :], ranked[:, :, :], AX.X, ALU.max))
                    do(nc.vector.tensor_tensor(onehot[:, :, :], ranked[:, :, :], along(rank_of_top[:, :], E),
                                               ALU.is_equal))

                def exp_inputs(b):
                    dve.wait_ge(logits_in_psum, b + 1)
                    gate_chain.start(b)
                    do = gate_chain.after
                    logits = misc[:, 0:J * L].rearrange("p (j e) -> p j e", j=J)
                    do(nc.vector.tensor_reduce(small["top"][:, :], logits[:, :, 0:E], AX.X, ALU.max))
                    nc.vector.tensor_tensor(exp_in[:, :, 0:E], logits[:, :, 0:E], along(small["top"][:, :], E),
                                            ALU.subtract)
                    nc.vector.tensor_scalar(exp_in[:, :, E], logits[:, :, E], -1.0, None, ALU.mult)\
                        .then_inc(exp_in_ready, 1)

                def token_weights(b):
                    do, s = gate_chain.after, small
                    dve.wait_ge(exp_ready, b + 1)
                    do(nc.vector.tensor_reduce(s["total"][:, :], exp_out[:, :, 0:E], AX.X, ALU.add))
                    do(nc.vector.reciprocal(s["inv_total"][:, :], s["total"][:, :]))
                    do(nc.vector.tensor_tensor(gates[:, :, :], exp_out[:, :, 0:E], along(s["inv_total"][:, :], E),
                                               ALU.mult))
                    first_at(do, gates, s["best"], s["rank1"], first)
                    do(nc.vector.scalar_tensor_tensor(out=gates_rest[:, :, :], in0=first[:, :, :], scalar=-4.0,
                                                      in1=gates[:, :, :], op0=ALU.mult, op1=ALU.add))
                    first_at(do, gates_rest, s["next_best"], s["rank2"], second)
                    do(nc.vector.tensor_tensor(s["both"][:, :], s["best"][:, :], s["next_best"][:, :], ALU.add))
                    do(nc.vector.reciprocal(s["inv_both"][:, :], s["both"][:, :]))
                    do(nc.vector.tensor_tensor(first[:, :, :], first[:, :, :], second[:, :, :], ALU.add))
                    do(nc.vector.tensor_tensor(first[:, :, :], first[:, :, :], gates[:, :, :], ALU.mult))
                    do(nc.vector.tensor_tensor(token_w[:, :, 0:E], first[:, :, :], along(s["inv_both"][:, :], E),
                                               ALU.mult))
                    do(nc.vector.tensor_scalar(s["shared_den"][:, :], exp_out[:, :, E], 1.0, None, ALU.add))
                    do(nc.vector.reciprocal(token_w[:, :, E], s["shared_den"][:, :]))
                    do(nc.vector.tensor_copy(parts[:, :, 0:L], token_w[:, :, :]))
                    do(nc.vector.tensor_tensor(rest1[:, :, :], token_w[:, :, :], parts[:, :, 0:L], ALU.subtract))
                    do(nc.vector.tensor_copy(parts[:, :, S:S + L], rest1[:, :, :]))
                    nc.vector.tensor_tensor(parts[:, :, 2 * S:2 * S + L], rest1[:, :, :], parts[:, :, S:S + L],
                                            ALU.subtract).then_inc(parts_ready, 1)
                    gate_chain.end()

                def chunk(b, k):
                    n = K * b + k
                    dve.wait_ge(silu_ready, n + 1)
                    dve.wait_ge(u_in_psum, n + 1)
                    nc.vector.tensor_tensor(gated[:, k % 2, :], silu[:, k % 2, :], u_psum[:, k % 2, :], ALU.mult)\
                        .then_inc(gated_free, 1)
                    dve.wait_ge(weight_ready, n + 1)
                    dve.wait_ge(gated_free, n + 3)
                    dve.wait_ge(h_free, n + 1)
                    nc.vector.tensor_tensor(h[:, k % 2, :], gated[:, k % 2, :], weight[:, k % 2, :], ALU.mult)\
                        .then_inc(h_ready, 1)

                def add_residual(b, par):
                    dve.wait_ge(out_in_psum, b + 1)
                    dve.wait_ge(st.x_out_free[par], 8 * (b - par) + 16)
                    nc.vector.scalar_tensor_tensor(out=st.x_out[:, par].rearrange("p j d -> p (j d)"),
                                                   in0=misc[:, :], scalar=0.5,
                                                   in1=st.x_in[:, par].rearrange("p j d -> p (j d)"),
                                                   op0=ALU.mult, op1=ALU.add).then_inc(st.residual_free, 1)

                def body(b, par):
                    for k in range(2, K):
                        chunk(b, k)
                        if k == 2:
                            st.norm_stats(dve, b + 1, 1 - par)
                        if k == 5:
                            exp_inputs(b + 1)
                        if k == 7:
                            token_weights(b + 1)
                    chunk(b + 1, 0)
                    chunk(b + 1, 1)
                    add_residual(b, par)

                dve.sem_inc(gated_free, 2)
                dve.sem_inc(h_free, 2)
                dve.sem_inc(st.residual_free, 1)
                dve.wait_ge(parts_zeroed, 1)
                st.wait_weights(dve)
                st.norm_stats(dve, 0, 0)
                exp_inputs(0)
                token_weights(0)
                chunk(0, 0)
                chunk(0, 1)
                two_batches(dve, st.NB // 2, body)

        st.finish()




class Bank:

    def __init__(self, full, free, lead_in, steps):
        self.full, self.free, self.lead_in, self.steps = full, free, lead_in, steps

    def number(self, b, step):
        return self.lead_in.index(step) if b is None else len(self.lead_in) + len(self.steps) * b + self.steps.index(step)

    def take(self, pe, b, step):
        pe.wait_ge(self.free, self.number(b, step) + 1)

    def filled(self, eng, b, step):
        eng.wait_ge(self.full, self.number(b, step) + 1)

    def emptied_last(self, eng, b):
        eng.wait_ge(self.free, len(self.lead_in) + len(self.steps) * b + 1)

    def emptied(self, eng, b, step):
        eng.wait_ge(self.free, self.number(b, step) + 2)


def attention_stage(nc, name, src, dst, consts, w):
    diff = "Wv" in w
    H = 16
    DH = 8
    maps = 2 if diff else 1
    VD = 16 if diff else 8
    WD = H * VD
    CW = WD // P
    G = maps * H // 4
    TERMS = 6
    HALF = TERMS * DH
    ROWS = 2 * HALF
    SCALE = float(1.0 / np.sqrt(DH))
    VP = 32
    width = lambda qt: (qt + 1) * P if diff else T
    start_q = lambda kt: kt * P if diff else 0
    units = []
    for qt in range(J):
        per = 4 if width(qt) <= T // 2 else 2
        units += [(qt, list(range(i, i + per)), 2 * T // per) for i in range(0, 4, per)]
    NU = len(units)
    LEAD = (7 * NU) // 4
    quota = lambda s: -(-NU * (s + 1) // 4) + LEAD
    tensors = [(c, q) for c in range(maps) for q in ("q", "k")]

    steps_at = {}
    for g in range(1, G + 1):
        steps_at[g, 1] = [("heads", g - 1)]
        steps_at[g, 2] = [("maxima", g + 1)]
    def at(g, kt, *steps):
        steps_at.setdefault((g, kt), []).extend(steps)
    if diff:
        at(2, 0, "xT")
        for n, t in enumerate(tensors):
            at(2 + n, 3, ("project", t))
        at(G, 2, ("values", 0))
        at(G, 3, ("values", 1), ("concat", 0), ("concat", 1), "out")
        values_steps = [("values", 0), ("values", 1)]
        prepare = ["xT"] + [("project", t) for t in tensors] + values_steps
        norm_at, load_at = (1, 0), (G, 3)
    else:
        at(2, 0, "xT")
        at(2, 3, ("project", (0, "q")), ("swapped", (0, "q")))
        at(3, 0, "latent")
        at(3, 3, ("project", (0, "k")), ("swapped", (0, "k")))
        at(G, 2, ("values", 0))
        at(G, 3, ("concat", 0), "out")
        values_steps = [("values", 0)]
        prepare = ["xT", ("project", (0, "q")), ("swapped", (0, "q")), "latent",
                   ("project", (0, "k")), ("swapped", (0, "k"))] + values_steps
        norm_at, load_at = (1, 0), (G, 3)
    slots = [(g, kt) for g in range(1, G + 1) for kt in range(J)]
    steps = [s for slot in slots for s in steps_at.get(slot, [])]
    lead_in = [(x, n) for n in range(2) for x in prepare] + [("maxima", 0), ("maxima", 1)]
    NT = len(tensors)

    with ExitStack() as ctx:
        st = Stage(nc, ctx, name, src, dst, consts)
        sb, ps, sem, misc, xT, NB = st.sb, st.ps, st.sem, st.misc, st.xT, st.NB
        x_res = sb("x_res", [P, 2, J, D], F32)
        if diff:
            w_qk = {t: sb(f"w_{t[1]}{t[0]}", [P, P], F32) for t in tensors}
            w_v = sb("w_v", [P, WD], F32)
            lam_in = sb("lam_in", [P, 4, H, DH], F32)
            lam_prod = sb("lam_prod", [P, 2, H, DH], F32)
            lam_sum = sb("lam_sum", [P, 2, H], F32)
            lam_exp = sb("lam_exp", [P, 2, H], F32)
            lam_diff = sb("lam_diff", [P, H], F32)
            lam = sb("lam", [P, H], F32)
            rms_scale = sb("rms_scale", [P, VD], F32)
            scale02 = sb("scale02", [P, VD], F32)
            map_out = sb("map_out", [P, 2, J, 4 * VD], F32)
            quad = sb("quad", [P, J, 4 * VD], F32)
            quad_sq = sb("quad_sq", [P, J, 4 * VD], F32)
            quad_ms = sb("quad_ms", [P, J * 4], F32)
            quad_mse = sb("quad_mse", [P, J * 4], F32)
            quad_rms = sb("quad_rms", [P, J * 4], F32)
            quad_n = sb("quad_n", [P, J, 4 * VD], F32)
            minus_half16 = sb("minus_half16", [P, J * 4], F32)
        else:
            w_q = sb("w_q", [P, 2, P], F32)
            w_k = sb("w_k", [32, 2, P], F32)
            w_v = sb("w_v", [32, WD], F32)
            w_down = sb("w_down", [P, 32], F32)
            b_q = sb("b_q", [P, 2], F32)
            b_k = sb("b_k", [P, 2], F32)
            b_v = sb("b_v", [P, WD], F32)
            b_down = sb("b_down", [32, 1], F32)
            b_out = sb("b_out", [P, D], F32)
            rope = sb("rope", [P, 2, T], F32)
            latent = sb("latent", [32, 2, T], F32)
            turned = sb("turned", [P, 2, T], F32)
            rotated = sb("rotated", [P, T], F32)
        w_o = sb("w_o", [P, CW, D], F32)
        qs = sb("qs", [P, 2, maps, H // 2, 2, T], BF16)
        ks = sb("ks", [P, 2, maps, H // 2, T], BF16)
        parts = sb("parts", [P, 2, 3, T], BF16)
        rest = sb("rest", [P, 2, T], F32)
        va = sb("va", [P, 2, J, H, VP], F32)
        row_max = sb("row_max", [P, 2, J * 4], F32)
        max_rest = sb("max_rest", [P, 2, J * 4], F32)
        max_parts = sb("max_parts", [P, 2, J, 3, 4], BF16)
        maxT = sb("maxT", [12, 2, T], BF16)
        prob = sb("prob", [P, 8, T], F32)
        oT = sb("oT", [P, 2, T], F32)
        inv_sum = sb("inv_sum", [P, J, 4], F32)
        inv_lam = sb("inv_lam", [P, J, 4], F32)
        o_all = sb("o_all", [P, J, WD], F32)
        o_allT = sb("o_allT", [P, CW, T], F32)
        zeros = sb("zeros", [P, J * 4], F32)
        s_psum = ps("s_psum", [P, 2, 2 * T], F32)
        sT_psum = ps("sT_psum", [P, 2, T], F32)
        pv_psum = ps("pv_psum", [P, T], F32)
        ident, ident16, causal_q, causal_k = (consts[k] for k in ("ident", "ident16", "causal_q", "causal_k"))
        scratch = nc.dram_tensor(f"{name}_stack", [2, maps, 2, 2, TERMS, DH, H // 2 * T], BF16, kind="Internal").ap()

        setup = sem("setup")
        setup_step = sem("setup_step")
        fixed_rows = sem("fixed_rows")
        res_loaded = [sem(f"res_loaded{i}") for i in range(2)]
        res_ready = sem("res_ready")
        hi_ready = sem("hi_ready")
        rest_ready = sem("rest_ready")
        mid_ready = sem("mid_ready")
        parts_ready = sem("parts_ready")
        rotated_ready = sem("rotated_ready")
        parts_written = [sem(f"parts_written{i}") for i in range(2)]
        stack_loaded = [sem(f"stack_loaded{i}") for i in range(2)]
        s_in_psum = sem("s_in_psum")
        s_free = sem("s_free")
        max_step = sem("max_step")
        max_parts_ready = sem("max_parts_ready")
        max_stored = [sem(f"max_stored{i}") for i in range(2)]
        sT_in_psum = sem("sT_in_psum")
        prob_ready = sem("prob_ready")
        pv_in_psum = sem("pv_in_psum")
        oT_ready = sem("oT_ready")
        post_step = sem("post_step")
        sq_ready = sem("sq_ready")
        mse_ready = sem("mse_ready")
        quad_step = sem("quad_step")
        ms_step = sem("ms_step")
        o_ready = sem("o_ready")
        bank = Bank(sem("misc_full"), sem("misc_free"), lead_in, steps)
        def head_of(g, i):
            c, quad_no = g % maps, g // maps
            return c, 2 * quad_no + i // 2, i % 2

        with nc.Block() as block:

            @block.sync
            def _(sp):
                def write_tensor(count, t, par):
                    c, q = t
                    k = tensors.index(t) % 2
                    sp.wait_ge(parts_ready, count + 1)
                    for g in range(2):
                        rows = parts[g * 64:(g + 1) * 64, k]
                        to = scratch[par, c, 0 if q == "q" else 1, g].rearrange("t d (i n) -> (d i) t n", n=T)
                        for t0, n in ((0, 3), (3, 2), (5, 1)):
                            if q == "q":
                                part = rows[:, 0:n, :]
                            else:
                                part = rows[:, 3 - n:4 - n, :].broadcast_to([64, n, T])
                            sp.dma_start(to[:, t0:t0 + n, :], part).then_inc(parts_written[k], 16)

                def load_stack(par, written):
                    for k in range(2):
                        sp.wait_ge(parts_written[k], written)
                    for c in range(maps):
                        for g in range(2):
                            rows = slice(g * HALF, (g + 1) * HALF)
                            sp.dma_start(qs[rows, par, c, :, g, :],
                                         scratch[par, c, 0, g].rearrange("t d (i n) -> (t d) i n", n=T))\
                                .then_inc(stack_loaded[par], 16)
                            sp.dma_start(ks[rows, par, c, :, :],
                                         scratch[par, c, 1, g].rearrange("t d (i n) -> (t d) i n", n=T))\
                                .then_inc(stack_loaded[par], 16)

                def store_max(b, par, arg):
                    g = arg % G
                    par = par if arg < G else 1 - par
                    c, pair, _ = head_of(g, 0)
                    bank.emptied(sp, b, ("maxima", arg))
                    for s in range(3):
                        to = qs[ROWS + s:ROWS + s + 1, par, c, pair:pair + 2, :, :].rearrange("o a b n -> o (a b) n")
                        sp.dma_start(to, maxT[4 * s:4 * s + 4, g % 2, :]).then_inc(max_stored[g % 2], 16)

                def load_x(b, par, index):
                    sp.dma_start(st.x_in[:, par], src[index].rearrange("(j p) d -> p j d", p=P))\
                        .then_inc(st.x_loaded[par], 16)

                def body(b, par, index=None):
                    for g, kt in slots:
                        if (g, kt) == (1, 0):
                            sp.wait_ge(st.x_hat_ready, b + 2)
                            sp.sem_inc(st.tick, 1)
                            load_x(b + 3, 1 - par, b + 3 if index is None else (index + 3) % NB)
                            bank.emptied_last(sp, b)
                            sp.sem_inc(st.tick, 1)
                            sp.dma_start(x_res[:, par], src[b].rearrange("(j p) d -> p j d", p=P))\
                                .then_inc(res_loaded[par], 16)
                        if kt == 2:
                            store_max(b, par, g + 1)
                        for s in steps_at.get((g, kt), []):
                            if s[0] == ("swapped" if not diff else "project"):
                                write_tensor(NT * (b + 2) + tensors.index(s[1]), s[1], par)
                        if (g, kt) == load_at:
                            sp.wait_ge(sT_in_psum, 16 * G * (b + 1))
                            sp.sem_inc(st.tick, 1)
                            load_stack(par, (NT // 2) * 96 * (b + 3))
                    bank.emptied(sp, b, "out")
                    sp.dma_start(dst[b].rearrange("(j p) d -> p j d", p=P), st.x_out[:, par])\
                        .then_inc(st.x_out_free[par], 16)

                for par in range(2):
                    sp.sem_inc(st.x_out_free[par], 16)
                load_x(0, 0, 0)
                load_x(1, 1, 1)
                if diff:
                    for n, t in enumerate(tensors):
                        st.load_weight(sp, w_qk[t][:, :], w[f"W{t[1]}{t[0]}"])
                    st.load_weight(sp, w_v[:, :], w["Wv"])
                    for n, k in enumerate(("lambda_q1", "lambda_k1", "lambda_q2", "lambda_k2")):
                        st.load_weight(sp, lam_in[:, n], w[k].rearrange("(o h) d -> o h d", o=1).broadcast_to([P, H, DH]))
                    st.load_weight(sp, rms_scale[:, :], w["rms_scale"].rearrange("(o h) -> o h", o=1).broadcast_to([P, VD]))
                else:
                    for to, k in ((w_q[:, :, :], "Wq"), (w_k[:, :, :], "Wk"), (w_v[:, :], "Wvalue"), (w_down[:, :], "Wdown"),
                                  (b_q[:, :], "bq"), (b_k[:, :], "bk"), (b_down[:, :], "bdown"),
                                  (rope[:, :, :], "rope")):
                        st.load_weight(sp, to, w[k])
                    st.load_weight(sp, b_v[:, :], w["bv"].rearrange("(o h) -> o h", o=1).broadcast_to([P, WD]))
                    st.load_weight(sp, b_out[:, :], w["bout"].rearrange("(o h) -> o h", o=1).broadcast_to([P, D]))
                st.load_weight(sp, w_o[:, :, :], w["Wo"])
                for par in range(2):
                    for c in range(maps):
                        sp.dma_start(ks[ROWS:ROWS + 3, par, c], w["minus_ones"]).then_inc(fixed_rows, 16)
                for n in range(2):
                    for t in tensors:
                        write_tensor(NT * n + tensors.index(t), t, n)
                    if n == 0:
                        sp.wait_ge(st.x_hat_ready, 1)
                        load_x(2, 0, 2)
                    sp.wait_ge(setup, 1)
                    load_stack(n, (NT // 2) * 96 * (n + 1))
                store_max(None, 0, 0)
                store_max(None, 0, 1)
                turns = NB // 2 - 2
                if turns > 0:
                    two_batches(sp, turns, body)
                for b in range(2 * max(turns, 0), NB):
                    body(b, b % 2, b)
                for par in range(2):
                    sp.wait_ge(st.x_out_free[par], 16 + 8 * NB)
                    sp.wait_ge(stack_loaded[par], 64 * maps * (NB // 2 + 1))
                sp.wait_ge(st.x_loaded[0], 16 * (NB // 2 + 2))
                sp.wait_ge(st.x_loaded[1], 16 * (NB // 2 + 1))
                for par in range(2):
                    sp.wait_ge(max_stored[par], 48 * (NB * G // 2 + 1))

            @block.gpsimd
            def _(pool):
                tt = nc.gpsimd.tensor_tensor
                maxc = Chain(pool, max_step, 3)

                def split_max(gg, g, last_unit):
                    k = g % 2
                    m, r = row_max[:, k], max_rest[:, k]
                    part = lambda i: max_parts[:, k, :, i, :]
                    pool.wait_ge(s_free, last_unit + 3)
                    maxc.start(gg)
                    v = lambda x: x.rearrange("p (j h) -> p j h", j=J)
                    maxc.after(tt(part(0), v(m), v(zeros[:, :]), ALU.add))
                    maxc.after(tt(v(r), v(m), part(0), ALU.subtract))
                    maxc.after(tt(part(1), v(r), v(zeros[:, :]), ALU.add))
                    tt(part(2), v(r), part(1), ALU.subtract).then_inc(max_parts_ready, 1)
                    maxc.end()

                def split_tensor(count, t, key):
                    k = tensors.index(t) % 2
                    if not diff:
                        bank.emptied(pool, *key)
                        tt(rotated[:, :], turned[:, 0], turned[:, 1], ALU.add).then_inc(rotated_ready, 1)
                        pool.wait_ge(hi_ready, count + 1)
                        tt(rest[:, k], rotated[:, :], parts[:, k, 0], ALU.subtract).then_inc(rest_ready, 1)
                    pool.wait_ge(mid_ready, count + 1)
                    tt(parts[:, k, 2], rest[:, k], parts[:, k, 1], ALU.subtract).then_inc(parts_ready, 1)

                def norm(b2, par):
                    st.norm_apply(pool, b2, par)

                def combine(qn, b, g):
                    bank.emptied(pool, b, ("heads", g))
                    tt(quad[:, :, :], map_out[:, 0], map_out[:, 1], ALU.subtract).then_inc(quad_step, 1)
                    pool.wait_ge(quad_step, 3 * qn + 1)
                    tt(quad_sq[:, :, :], quad[:, :, :], quad[:, :, :], ALU.mult).then_inc(sq_ready, 1)

                def rms(qn, quad_no):
                    pool.wait_ge(mse_ready, qn + 1)
                    tt(quad_rms[:, :], quad_mse[:, :], minus_half16[:, :], ALU.pow).then_inc(quad_step, 1)
                    pool.wait_ge(quad_step, 3 * qn + 2)
                    tt(quad_n[:, :, :].rearrange("p j (h d) -> p (j h) d", d=VD),
                       quad[:, :, :].rearrange("p j (h d) -> p (j h) d", d=VD), along(quad_rms[:, :], VD), ALU.mult)\
                        .then_inc(quad_step, 1)
                    pool.wait_ge(quad_step, 3 * qn + 3)
                    w4 = 4 * VD
                    heads = lambda x: x.rearrange("p j (h d) -> p j h d", d=VD)
                    scale = scale02[:, :].rearrange("p (a b d) -> p a b d", a=1, b=1).broadcast_to([P, J, 4, VD])
                    tt(heads(o_all[:, :, quad_no * w4:(quad_no + 1) * w4]), heads(quad_n[:, :, :]), scale, ALU.mult)\
                        .then_inc(o_ready, 1)

                def body(b, par):
                    for g, kt in slots:
                        if (g, kt) == norm_at:
                            norm(b + 2, par)
                            if not diff:
                                pool.wait_ge(res_loaded[par], 8 * (b - par) + 16)
                                tt(x_res[:, par], x_res[:, par], over(b_out[:, :], J), ALU.add).then_inc(res_ready, 1)
                        if kt == 2:
                            gg = G * b + g + 1
                            split_max(gg, g + 1, NU * (gg + 1) - 1)
                        if diff and kt == 2 and g % 2 == 0:
                            combine((G // 2) * b + g // 2 - 1, b, g - 1)
                        for s in steps_at.get((g, kt), []):
                            if s[0] == ("swapped" if not diff else "project"):
                                split_tensor(NT * (b + 2) + tensors.index(s[1]), s[1], (b, s))
                        if diff and kt == 3 and g % 2 == 0:
                            rms((G // 2) * b + g // 2 - 1, g // 2 - 1)

                nc.gpsimd.memset(qs[:, :, :, :, :, :].rearrange("p a b c d e -> p (a b c d e)").bitcast(F32), 0.0)
                nc.gpsimd.memset(zeros[:, :], 0.0)
                if diff:
                    nc.gpsimd.memset(minus_half16[:, :], -0.5)
                nc.gpsimd.memset(va[:, :, :, :, :], 0.0).then_inc(setup, 1)
                pool.wait_ge(setup, 1)
                nc.gpsimd.memset(va[:, :, :, :, VD:VD + 1].rearrange("p a j h o -> p (a j h) o"), 1.0).then_inc(setup, 1)
                st.wait_weights(pool)
                if diff:
                    pool.wait_ge(setup_step, 6)
                for n in range(2):
                    norm(n, n)
                    for t in tensors:
                        split_tensor(NT * n + tensors.index(t), t, (None, (("swapped", t), n)))
                split_max(0, 0, NU - 1)
                split_max(1, 1, 2 * NU - 1)
                two_batches(pool, NB // 2, body)

            @block.tensor
            def _(pe):
                mm = nc.tensor.matmul

                def max_unit(n, u, b_of, par, g):
                    qt, heads, pitch = units[u % NU]
                    W = width(qt)
                    if u % (NU * G) == 0:
                        pe.wait_ge(stack_loaded[par], 64 * maps * (b_of // 2 + 1) if isinstance(b_of, int)
                                   else 32 * maps * (b_of - par) + 64 * maps)
                    pe.wait_ge(s_free, n + 1)
                    pe.sem_inc(st.tick, 1)
                    for k, i in enumerate(heads):
                        c, pair, hp = head_of(g, i)
                        out = s_psum[:, u % 2, k * pitch:k * pitch + W]
                        last = mm(out, qs[0:ROWS, par, c, pair, hp, qt * P:(qt + 1) * P], ks[0:ROWS, par, c, pair, 0:W],
                                  start=True, stop=True)
                        if diff:
                            last = mm(out[:, W - P:W], ident16[:, :], causal_q[:, :], start=False, stop=True,
                                      skip_group_check=True)
                    last.then_inc(s_in_psum, 1)

                def score(n, par, g, kt, i, first=False):
                    c, pair, hp = head_of(g, i)
                    q0 = start_q(kt)
                    if not first:
                        pe.wait_ge(prob_ready, n - 1)
                        pe.sem_inc(st.tick, 1)
                    out = sT_psum[:, i % 2, q0:T]
                    last = mm(out, ks[0:ROWS + 3, par, c, pair, kt * P:(kt + 1) * P], qs[0:ROWS + 3, par, c, pair, hp, q0:T],
                              start=True, stop=True)
                    if diff:
                        last = mm(out[:, 0:P], ident16[:, :], causal_k[:, :], start=False, stop=True,
                                  skip_group_check=True)
                    last.then_inc(sT_in_psum, 1)

                def pv(gg, par, g, kt, first=False):
                    q0 = start_q(kt)
                    pe.wait_ge(prob_ready, 16 * gg + 4 * kt + 4)
                    if kt == 0 and not first:
                        pe.wait_ge(oT_ready, gg)
                    for i in range(4):
                        c, pair, hp = head_of(g, i)
                        last = mm(pv_psum[32 * i:32 * i + 32, q0:T], va[:, par, kt, 2 * pair + hp, :],
                                  prob[:, (4 * kt + i) % 8, q0:T], start=(kt == 0), stop=(kt == J - 1),
                                  skip_group_check=True)
                    if kt == J - 1:
                        last.then_inc(pv_in_psum, 1)

                def step(b, s, n=None, par=None, prep_par=None):
                    name_, arg = s if isinstance(s, tuple) else (s, None)
                    key = s if b is not None else ((s, n) if name_ != "maxima" else s)
                    bank.take(pe, b, key)
                    nb = (b + 2) if b is not None else n
                    pp = prep_par
                    if name_ == "xT":
                        pe.wait_ge(st.x_hat_ready, nb + 1)
                        for j in range(J):
                            last = nc.tensor.transpose(misc[:, j * P:(j + 1) * P], st.x_hat[:, j, :], ident[:, :])
                    elif name_ in ("project", "swapped"):
                        sw = int(name_ == "swapped")
                        if diff:
                            last = mm(misc[:, :], w_qk[arg][:, :], xT[:, pp], start=True, stop=True)
                        elif arg[1] == "q":
                            last = mm(misc[:, :], w_q[:, sw, :], xT[:, pp], start=True, stop=True)
                        else:
                            last = mm(misc[:, :], w_k[:, sw, :], latent[:, pp], start=True, stop=True)
                    elif name_ == "latent":
                        last = mm(misc[0:32, :], w_down[:, :], xT[:, pp], start=True, stop=True)
                    elif name_ == "values":
                        if diff:
                            for j in range(2):
                                tile = slice((2 * arg + j) * P, (2 * arg + j + 1) * P)
                                last = mm(misc[:, j * WD:(j + 1) * WD], xT[:, pp, tile], w_v[:, :], start=True, stop=True)
                        else:
                            for j in range(J):
                                last = mm(misc[:, j * WD:(j + 1) * WD], latent[:, pp, j * P:(j + 1) * P], w_v[:, :],
                                          start=True, stop=True)
                    elif name_ == "maxima":
                        gg = arg if b is None else G * b + arg
                        pe.wait_ge(max_parts_ready, gg + 1)
                        for j in range(J):
                            last = nc.tensor.transpose(misc[0:12, j * P // 2:(j + 1) * P // 2].bitcast(BF16),
                                                       max_parts[:, arg % 2, j].rearrange("p s h -> p (s h)"), ident16[:, :])
                    elif name_ == "heads":
                        pe.wait_ge(oT_ready, G * b + arg + 1)
                        for j in range(J):
                            last = nc.tensor.transpose(misc[:, j * P:(j + 1) * P], oT[:, arg % 2, j * P:(j + 1) * P], ident[:, :])
                    elif name_ == "concat":
                        if diff and arg == 0:
                            pe.wait_ge(o_ready, 4 * (b + 1))
                        for j in range(J):
                            last = nc.tensor.transpose(misc[:, j * P:(j + 1) * P], o_all[:, j, arg * P:(arg + 1) * P], ident[:, :])
                    elif name_ == "out":
                        for j in range(J):
                            for k in range(CW):
                                last = mm(misc[:, j * P:(j + 1) * P], o_allT[:, k, j * P:(j + 1) * P], w_o[:, k, :],
                                          start=(k == 0), stop=(k == CW - 1))
                    last.then_inc(bank.full, 1)

                def slot(b, par, s, g, kt, todo, first=False):
                    own, gm = (par, g) if g < G else (1 - par, 0)
                    n = 16 * G * b + 4 * s
                    if kt == 0:
                        pe.wait_ge(max_stored[g % 2], 24 * G * b + 48 * (g // 2 + 1))
                    for i in range(4):
                        score(n + i, own, gm, kt, i, first=first and kt == 0 and i < 2)
                        take = todo[i * len(todo) // 4:(i + 1) * len(todo) // 4]
                        for u in take:
                            over_b, ug = divmod(u // NU, G)
                            max_unit(NU * G * b + u, u, b + over_b, par if over_b % 2 == 0 else 1 - par, ug)

                def body(b, par):
                    for s, (g, kt) in enumerate(slots, start=4):
                        slot(b, par, s, g, kt, list(range(quota(s - 1), quota(s))))
                        if kt == 0:
                            pv(G * b + g - 1, par, g - 1, J - 1)
                        else:
                            pv(G * b + g, par if g < G else 1 - par, g % G, kt - 1)
                        for x in steps_at.get((g, kt), []):
                            step(b, x, par=par, prep_par=par)

                st.wait_weights(pe)
                pe.wait_ge(fixed_rows, 32 * maps)
                pe.wait_ge(setup, 2)
                for n in range(2):
                    for x in prepare:
                        step(None, x, n=n, prep_par=n)
                for u in range(LEAD):
                    if u == NU:
                        step(None, ("maxima", 0))
                    max_unit(u, u, 0, 0, u // NU)
                extra = list(range(LEAD, quota(3)))
                for u in extra:
                    max_unit(u, u, 0, 0, u // NU)
                step(None, ("maxima", 1))
                for kt in range(J):
                    slot(0, 0, kt, 0, kt, [], first=True)
                    if kt > 0:
                        pv(0, 0, 0, kt - 1, first=True)
                two_batches(pe, NB // 2, body)

            @block.scalar
            def _(act):
                def exps(n, kt):
                    q0 = start_q(kt)
                    for i in range(4):
                        act.wait_ge(sT_in_psum, n + i + 1)
                        nc.scalar.activation(prob[:, (4 * kt + i) % 8, q0:T], sT_psum[:, i % 2, q0:T], ACT.Exp, scale=SCALE)\
                            .then_inc(prob_ready, 1)

                def copy_heads(gg, g):
                    act.wait_ge(pv_in_psum, gg + 1)
                    nc.scalar.activation(oT[:, g % 2], pv_psum[:, :], ACT.Copy).then_inc(oT_ready, 1)

                def hi_mid(count, t, key):
                    k = tensors.index(t) % 2
                    if diff:
                        bank.emptied(act, *key)
                    else:
                        act.wait_ge(rotated_ready, count + 1)
                        nc.scalar.activation(parts[:, k, 0], rotated[:, :], ACT.Copy).then_inc(hi_ready, 1)
                        act.wait_ge(rest_ready, count + 1)
                    nc.scalar.activation(parts[:, k, 1], rest[:, k], ACT.Copy).then_inc(mid_ready, 1)

                def step(b, s, n=None, pp=None):
                    name_, arg = s if isinstance(s, tuple) else (s, None)
                    key = s if b is not None else ((s, n) if name_ != "maxima" else s)
                    if name_ == "xT":
                        bank.filled(act, b, key)
                        nc.scalar.activation(xT[:, pp], misc[:, :], ACT.Copy).then_inc(bank.free, 1)
                    elif name_ == "project" and diff:
                        k = tensors.index(arg) % 2
                        count = NT * (b + 2 if b is not None else n) + tensors.index(arg)
                        bank.filled(act, b, key)
                        if b is not None or n > 0 or tensors.index(arg) >= 2:
                            act.wait_ge(parts_written[k], 96 * (count // 2) if isinstance(count, int)
                                        else 96 * ((NT // 2) * (b + 2) + tensors.index(arg) // 2))
                        nc.scalar.activation(parts[:, k, 0], misc[:, :], ACT.Copy).then_inc(hi_ready, 1)
                        hi_mid(count, arg, (b, key))
                    elif name_ == "swapped":
                        k = tensors.index(arg) % 2
                        count = NT * (b + 2 if b is not None else n) + tensors.index(arg)
                        if b is not None or n > 0:
                            act.wait_ge(parts_written[k], 96 * (b + 2 if b is not None else n))
                        hi_mid(count, arg, (b, key))
                    elif name_ == "latent":
                        bank.filled(act, b, key)
                        nc.scalar.activation(latent[:, pp], misc[0:32, :], ACT.Identity, bias=b_down[:, 0:1])\
                            .then_inc(bank.free, 1)
                    elif name_ == "values" and diff:
                        bank.filled(act, b, key)
                        for j in range(2):
                            last = nc.scalar.activation(va[:, pp, 2 * arg + j, :, 0:VD],
                                                        misc[:, j * WD:(j + 1) * WD].rearrange("p (h d) -> p h d", d=VD), ACT.Copy)
                        last.then_inc(bank.free, 1)
                    elif name_ == "maxima":
                        bank.filled(act, b, key)
                        nc.scalar.activation(maxT[:, arg % 2, :], misc[0:12, 0:T // 2].bitcast(BF16), ACT.Copy)\
                            .then_inc(bank.free, 1)
                    elif name_ == "concat":
                        bank.filled(act, b, key)
                        nc.scalar.activation(o_allT[:, arg], misc[:, :], ACT.Copy).then_inc(bank.free, 1)

                def body(b, par):
                    for s, (g, kt) in enumerate(slots, start=4):
                        exps(16 * G * b + 4 * s, kt)
                        if kt == 0:
                            copy_heads(G * b + g - 1, g - 1)
                        for x in steps_at.get((g, kt), []):
                            step(b, x, pp=par)

                st.wait_weights(act)
                if diff:
                    act.wait_ge(setup_step, 2)
                    nc.scalar.activation(lam_exp[:, :, :], lam_sum[:, :, :], ACT.Exp).then_inc(setup_step, 1)
                for n in range(2):
                    for x in prepare:
                        step(None, x, n=n, pp=n)
                step(None, ("maxima", 0))
                step(None, ("maxima", 1))
                for kt in range(J):
                    exps(4 * kt, kt)
                two_batches(act, NB // 2, body)

            @block.vector
            def _(dve):
                post = Chain(dve, post_step, 1)

                def unit(n, u):
                    qt, heads, pitch = units[u % NU]
                    g = (u // NU) % G
                    dve.wait_ge(s_in_psum, n + 1)
                    scores = s_psum[:, u % 2, :].rearrange("p (k w) -> p k w", w=pitch)[:, :, 0:width(qt)]
                    nc.vector.tensor_reduce(row_max[:, g % 2, 4 * qt + heads[0]:4 * qt + heads[-1] + 1], scores, AX.X, ALU.max)\
                        .then_inc(s_free, 1)

                def step(b, s, n=None, pp=None):
                    name_, arg = s if isinstance(s, tuple) else (s, None)
                    key = s if b is not None else ((s, n) if name_ != "maxima" else s)
                    nb = b + 2 if b is not None else n
                    if name_ == "project" and diff:
                        k = tensors.index(arg) % 2
                        bank.filled(dve, b, key)
                        dve.wait_ge(hi_ready, NT * nb + tensors.index(arg) + 1)
                        nc.vector.tensor_tensor(rest[:, k], misc[:, :], parts[:, k, 0], ALU.subtract).then_inc(bank.free, 1)
                    elif name_ in ("project", "swapped"):
                        sw = int(name_ == "swapped")
                        bias = b_q if arg[1] == "q" else b_k
                        count = NT * nb + tensors.index(arg)
                        bank.filled(dve, b, key)
                        if not (isinstance(count, int) and count == 0):
                            dve.wait_ge(rotated_ready, count)
                        nc.vector.scalar_tensor_tensor(out=turned[:, sw], in0=misc[:, :], scalar=bias[:, sw:sw + 1],
                                                       in1=rope[:, sw], op0=ALU.add, op1=ALU.mult).then_inc(bank.free, 1)
                    elif name_ == "values" and not diff:
                        bank.filled(dve, b, key)
                        heads = lambda x: x.rearrange("p (j h d) -> p j h d", h=H, d=VD)
                        bias = b_v[:, :].rearrange("p (o h d) -> p o h d", o=1, d=VD).broadcast_to([P, J, H, VD])
                        nc.vector.tensor_tensor(va[:, pp, :, :, 0:VD], heads(misc[:, :]), bias, ALU.add).then_inc(bank.free, 1)
                    elif name_ == "heads":
                        c, quad_no = arg % maps, arg // maps
                        bank.filled(dve, b, key)
                        o = misc[:, :].rearrange("p (j h v) -> p j h v", h=4, v=VP)
                        post.start(post_no(b, arg))
                        post.after(nc.vector.reciprocal(inv_sum[:, :, :], o[:, :, :, VD]))
                        inv = inv_sum
                        if c == 1:
                            post.after(nc.vector.tensor_tensor(inv_lam[:, :, :], inv_sum[:, :, :],
                                                               over(lam[:, 4 * quad_no:4 * quad_no + 4], J), ALU.mult))
                            inv = inv_lam
                        to = map_out[:, c] if diff else o_all[:, :, quad_no * 4 * VD:(quad_no + 1) * 4 * VD]
                        inv = inv[:, :, :].rearrange("p j (h o) -> p j h o", o=1).broadcast_to([P, J, 4, VD])
                        nc.vector.tensor_tensor(to.rearrange("p j (h d) -> p j h d", d=VD), o[:, :, :, 0:VD], inv, ALU.mult)\
                            .then_inc(bank.free, 1)
                    elif name_ == "out":
                        bank.filled(dve, b, key)
                        if diff:
                            dve.wait_ge(res_loaded[pp], 8 * (b - pp) + 16)
                        else:
                            dve.wait_ge(res_ready, b + 1)
                        dve.wait_ge(st.x_out_free[pp], 8 * (b - pp) + 16)
                        nc.vector.tensor_tensor(st.x_out[:, pp].rearrange("p j d -> p (j d)"), misc[:, :],
                                                x_res[:, pp].rearrange("p j d -> p (j d)"), ALU.add).then_inc(bank.free, 1)

                def post_no(b, g):
                    post.per = 1
                    return G * b + g if not diff else 3 * (G // 2) * b + 3 * (g // 2) + g % 2

                def mean_square(qn):
                    dve.wait_ge(sq_ready, qn + 1)
                    nc.vector.tensor_reduce(quad_ms[:, :], quad_sq[:, :, :].rearrange("p j (h d) -> p (j h) d", d=VD), AX.X,
                                            ALU.add).then_inc(ms_step, 1)
                    dve.wait_ge(ms_step, qn + 1)
                    nc.vector.tensor_scalar(quad_mse[:, :], quad_ms[:, :], 1.0 / VD, EPS, ALU.mult, ALU.add)\
                        .then_inc(mse_ready, 1)

                def body(b, par):
                    for s, (g, kt) in enumerate(slots, start=4):
                        if (g, kt) == norm_at:
                            st.norm_stats(dve, b + 2, par)
                        for u in range(quota(s - 1), quota(s)):
                            unit(NU * G * b + u, u)
                        if diff and kt == 3 and g % 2 == 0:
                            mean_square((G // 2) * b + g // 2 - 1)
                        for x in steps_at.get((g, kt), []):
                            step(b, x, pp=par)

                dve.sem_inc(s_free, 2)
                dve.sem_inc(bank.free, 1)
                st.wait_weights(dve)
                if diff:
                    nc.vector.tensor_tensor(lam_prod[:, :, :, :], lam_in[:, 0:4:2], lam_in[:, 1:4:2], ALU.mult)\
                        .then_inc(setup_step, 1)
                    dve.wait_ge(setup_step, 1)
                    nc.vector.tensor_reduce(lam_sum[:, :, :], lam_prod[:, :, :, :], AX.X, ALU.add).then_inc(setup_step, 1)
                    dve.wait_ge(setup_step, 3)
                    nc.vector.tensor_tensor(lam_diff[:, :], lam_exp[:, 0], lam_exp[:, 1], ALU.subtract).then_inc(setup_step, 1)
                    dve.wait_ge(setup_step, 4)
                    nc.vector.tensor_scalar(lam[:, :], lam_diff[:, :], LAMBDA_INIT, None, ALU.add).then_inc(setup_step, 1)
                    nc.vector.tensor_scalar(scale02[:, :], rms_scale[:, :], 1.0 - LAMBDA_INIT, None, ALU.mult)\
                        .then_inc(setup_step, 1)
                for n in range(2):
                    st.norm_stats(dve, n, n)
                    for x in prepare:
                        step(None, x, n=n, pp=n)
                for u in range(quota(3)):
                    unit(u, u)
                two_batches(dve, NB // 2, body)

        st.finish()




def head_mixing_stage(nc, name, src, dst, consts, w):
    H, DH = 16, 8
    W = H * DH
    SCALE = float(1.0 / np.sqrt(DH))
    R = 32
    QW, KW = 2 * W, 3 * W
    with ExitStack() as ctx:
        st = Stage(nc, ctx, name, src, dst, consts)
        sb, ps, sem, misc, xT, NB = st.sb, st.ps, st.sem, st.misc, st.xT, st.NB
        w_q = sb("w_q", [P, QW], F32)
        w_kv = sb("w_kv", [R, KW], F32)
        w_down = sb("w_down", [P, R], F32)
        w_o = sb("w_o", [P, D], F32)
        b_qkv = sb("b_qkv", [P, QW + KW], F32)
        b_down = sb("b_down", [R, 1], F32)
        b_out = sb("b_out", [P, D], F32)
        rope = sb("rope", [P, J, 4 * W], F32)
        latent = sb("latent", [R, 2, T], F32)
        raw = sb("raw", [P, 2, QW + KW], F32)
        turned = sb("turned", [P, 2, 4 * W], F32)
        rotated = sb("rotated", [P, 2, 2 * W], F32)
        products = sb("products", [P, H * H * DH], F32)
        scores = sb("scores", [P, H, H], F32)
        top = sb("top", [P, H], F32)
        lowered = sb("lowered", [P, 2, H * H], F32)
        prob = sb("prob", [P, 2, H * H], F32)
        weighted = sb("weighted", [P, 2, H * DH * H], F32)
        total = sb("total", [P, H], F32)
        inv_total = sb("inv_total", [P, H], F32)
        mixed = sb("mixed", [P, W], F32)
        heads_out = sb("heads_out", [P, 2, W], F32)
        headsT = sb("headsT", [P, 2, P], F32)
        biased = sb("biased", [P, D], F32)
        q_psum = ps("q_psum", [P, 2, T], F32)
        kv_psum = ps("kv_psum", [P, 2, T], F32)
        latent_psum = ps("latent_psum", [P, T], F32)
        headsT_psum = ps("headsT_psum", [P, T], F32)
        out_psum = ps("out_psum", [P, T], F32)
        ident = consts["ident"]

        latent_in_psum = sem("latent_in_psum")
        latent_ready = sem("latent_ready")
        projected = sem("projected")
        raw_ready = sem("raw_ready")
        turned_ready = sem("turned_ready")
        rotated_ready = sem("rotated_ready")
        score_step = sem("score_step")
        lowered_ready = sem("lowered_ready")
        prob_ready = sem("prob_ready")
        weighted_ready = sem("weighted_ready")
        mix_step = sem("mix_step")
        heads_ready = sem("heads_ready")
        headsT_in_psum = sem("headsT_in_psum")
        headsT_ready = sem("headsT_ready")
        out_in_psum = sem("out_in_psum")
        out_free = sem("out_free")
        residual_step = sem("residual_step")

        with nc.Block() as block:

            @block.sync
            def _(sp):
                st.load_x(sp, 0, 0)
                for to, k in ((w_q[:, :], "Wq"), (w_kv[:, :], "Wkv"), (w_down[:, :], "Wdown"), (w_o[:, :], "Wo"),
                              (b_down[:, :], "bdown"), (rope[:, :, :], "rope")):
                    st.load_weight(sp, to, w[k])
                st.load_weight(sp, b_qkv[:, :], w["bqkv"].rearrange("(o h) -> o h", o=1).broadcast_to([P, QW + KW]))
                st.load_weight(sp, b_out[:, :], w["bout"].rearrange("(o h) -> o h", o=1).broadcast_to([P, D]))
                st.load_x(sp, 1, 1)
                st.stream(sp)

            @block.gpsimd
            def _(pool):
                tt = nc.gpsimd.tensor_tensor

                def rotate(n, k, j):
                    pool.wait_ge(raw_ready, n + 3)
                    tt(turned[:, k], raw[:, k, 0:4 * W], rope[:, j, :], ALU.mult).then_inc(turned_ready, 1)
                    pool.wait_ge(turned_ready, n + 1)
                    halves = turned[:, k].rearrange("p (x y w) -> p x y w", x=2, y=2)
                    tt(rotated[:, k].rearrange("p (x w) -> p x w", x=2), halves[:, :, 0, :], halves[:, :, 1, :], ALU.add)\
                        .then_inc(rotated_ready, 1)

                def weigh(n, k):
                    pool.wait_ge(prob_ready, n + 1)
                    p_ = prob[:, k].rearrange("p (h o g) -> p h o g", h=H, o=1).broadcast_to([P, H, DH, H])
                    v_ = raw[:, k, 4 * W:5 * W].rearrange("p (o g d) -> p o d g", o=1, d=DH).broadcast_to([P, H, DH, H])
                    tt(weighted[:, k].rearrange("p (h d g) -> p h d g", h=H, d=DH), p_, v_, ALU.mult)\
                        .then_inc(weighted_ready, 1)

                def body(b, par):
                    for j in range(J):
                        if j == 0:
                            st.norm_apply(pool, b + 1, 1 - par)
                        n = 4 * b + j
                        rotate(n + 3, (j + 3) % 2, (j + 3) % J)
                        weigh(n + 2, j % 2)

                st.wait_weights(pool)
                st.norm_apply(pool, 0, 0)
                for n in range(3):
                    rotate(n, n % 2, n)
                    if n > 0:
                        weigh(n - 1, (n - 1) % 2)
                two_batches(pool, NB // 2, body)

            @block.tensor
            def _(pe):
                mm = nc.tensor.matmul

                def project(n, k, b, par, j):
                    own = slice(j * P, (j + 1) * P)
                    if j == 0:
                        pe.wait_ge(st.xT_ready, b + 1)
                        mm(latent_psum[0:R, :], w_down[:, :], xT[:, par], start=True, stop=True).then_inc(latent_in_psum, 1)
                        pe.wait_ge(latent_ready, b + 1)
                    pe.wait_ge(raw_ready, n + 1)
                    mm(q_psum[:, k, 0:QW], xT[:, par, own], w_q[:, :], start=True, stop=True)
                    mm(kv_psum[:, k, 0:KW], latent[:, par, own], w_kv[:, :], start=True, stop=True).then_inc(projected, 1)

                def finish(n, k):
                    pe.wait_ge(heads_ready, n + 1)
                    nc.tensor.transpose(headsT_psum[:, 0:P], heads_out[:, k, :], ident[:, :]).then_inc(headsT_in_psum, 1)
                    pe.wait_ge(headsT_ready, n + 1)
                    pe.wait_ge(out_free, n + 1)
                    mm(out_psum[:, 0:D], headsT[:, k, :], w_o[:, :], start=True, stop=True).then_inc(out_in_psum, 1)

                def body(b, par):
                    for j in range(J):
                        n = 4 * b + j
                        finish(n, j % 2)
                        if j == 0:
                            project(n + 3, 1, b, par, 3)
                            st.norm_transpose(pe, b + 1)
                        else:
                            project(n + 3, (j + 3) % 2, b + 1, 1 - par, j - 1)

                st.wait_weights(pe)
                st.norm_transpose(pe, 0, first=True)
                for n in range(3):
                    project(n, n % 2, 0, 0, n)
                two_batches(pe, NB // 2, body)

            @block.scalar
            def _(act):
                def exps(n, k):
                    act.wait_ge(lowered_ready, n + 1)
                    nc.scalar.activation(prob[:, k], lowered[:, k], ACT.Exp, scale=SCALE).then_inc(prob_ready, 1)

                def store_latent(b, par):
                    act.wait_ge(latent_in_psum, b + 1)
                    nc.scalar.activation(latent[:, par], latent_psum[0:R, :], ACT.Identity, bias=b_down[:, 0:1])\
                        .then_inc(latent_ready, 1)

                def store_heads(n, k):
                    act.wait_ge(headsT_in_psum, n + 1)
                    nc.scalar.activation(headsT[:, k, :], headsT_psum[:, 0:P], ACT.Copy).then_inc(headsT_ready, 1)

                def body(b, par):
                    for j in range(J):
                        n = 4 * b + j
                        store_heads(n, j % 2)
                        if j == 0:
                            st.norm_store(act, b + 1, 1 - par)
                        if j == 1:
                            store_latent(b + 1, 1 - par)
                        exps(n + 2, j % 2)

                st.wait_weights(act)
                st.norm_store(act, 0, 0)
                store_latent(0, 0)
                exps(0, 0)
                exps(1, 1)
                two_batches(act, NB // 2, body)

            @block.vector
            def _(dve):
                score = Chain(dve, score_step, 3)
                mix = Chain(dve, mix_step, 3)

                def add_bias(n, k):
                    dve.wait_ge(projected, n + 1)
                    nc.vector.tensor_tensor(raw[:, k, 0:QW], q_psum[:, k, 0:QW], b_qkv[:, 0:QW], ALU.add)
                    nc.vector.tensor_tensor(raw[:, k, QW:QW + KW], kv_psum[:, k, 0:KW], b_qkv[:, QW:QW + KW], ALU.add)\
                        .then_inc(raw_ready, 1)

                def compare(n, k):
                    dve.wait_ge(rotated_ready, n + 1)
                    score.start(n)
                    q = rotated[:, k, 0:W].rearrange("p (h o d) -> p h o d", h=H, o=1).broadcast_to([P, H, H, DH])
                    key = rotated[:, k, W:2 * W].rearrange("p (o g d) -> p o g d", o=1, d=DH).broadcast_to([P, H, H, DH])
                    score.after(nc.vector.tensor_tensor(products[:, :].rearrange("p (h g d) -> p h g d", h=H, g=H), q, key,
                                                        ALU.mult))
                    score.after(nc.vector.tensor_reduce(scores[:, :, :].rearrange("p h g -> p (h g)"),
                                                        products[:, :].rearrange("p (x d) -> p x d", d=DH), AX.X, ALU.add))
                    score.after(nc.vector.tensor_reduce(top[:, :], scores[:, :, :], AX.X, ALU.max))
                    nc.vector.tensor_tensor(lowered[:, k].rearrange("p (h g) -> p h g", h=H), scores[:, :, :],
                                            along(top[:, :], H), ALU.subtract).then_inc(lowered_ready, 1)
                    score.end()

                def add_up(n, k):
                    dve.wait_ge(weighted_ready, n + 1)
                    mix.start(n)
                    mix.mark(nc.vector.tensor_reduce(total[:, :], prob[:, k].rearrange("p (h g) -> p h g", h=H), AX.X, ALU.add))
                    mix.after(nc.vector.tensor_reduce(mixed[:, :], weighted[:, k].rearrange("p (x g) -> p x g", g=H), AX.X,
                                                      ALU.add))
                    mix.after(nc.vector.reciprocal(inv_total[:, :], total[:, :]))
                    nc.vector.tensor_tensor(heads_out[:, k].rearrange("p (h d) -> p h d", d=DH),
                                            mixed[:, :].rearrange("p (h d) -> p h d", d=DH), along(inv_total[:, :], DH),
                                            ALU.mult).then_inc(heads_ready, 1)
                    mix.end()

                def add_residual(b, par, j):
                    n = 4 * b + j
                    dve.wait_ge(out_in_psum, n + 1)
                    nc.vector.tensor_tensor(biased[:, :], out_psum[:, 0:D], b_out[:, :], ALU.add).then_inc(out_free, 1)
                    if j == 0:
                        dve.wait_ge(st.x_out_free[par], 8 * (b - par) + 16)
                    dve.wait_ge(out_free, n + 2)
                    nc.vector.tensor_tensor(st.x_out[:, par, j, :], biased[:, :], st.x_in[:, par, j, :], ALU.add)\
                        .then_inc(st.residual_free if j == J - 1 else residual_step, 1)

                def body(b, par):
                    for j in range(J):
                        n = 4 * b + j
                        if j == 0:
                            st.norm_stats(dve, b + 1, 1 - par)
                        compare(n + 2, j % 2)
                        dve.wait_ge(weighted_ready, n + 2)
                        add_bias(n + 3, (j + 3) % 2)
                        add_up(n + 1, (j + 1) % 2)
                        add_residual(b, par, j)

                dve.sem_inc(raw_ready, 2)
                dve.sem_inc(out_free, 1)
                dve.sem_inc(st.residual_free, 1)
                st.wait_weights(dve)
                st.norm_stats(dve, 0, 0)
                add_bias(0, 0)
                add_bias(1, 1)
                compare(0, 0)
                compare(1, 1)
                dve.wait_ge(weighted_ready, 1)
                add_bias(2, 0)
                add_up(0, 0)
                two_batches(dve, NB // 2, body)

        st.finish()


def build(nc, t, out, stages):
    NB = t["X"].shape[0]
    with ExitStack() as ctx:
        def const(name, shape, dt):
            return ctx.enter_context(nc.sbuf_tensor(name, shape, dt))

        consts = {
            "eps": const("eps", [P, J], F32),
            "minus_half": const("minus_half", [P, J], F32),
            "ident": const("ident", [P, P], F32),
            "ident16": const("ident16", [P, P], BF16),
            "rank": const("rank", [P, 16], F32),
            "causal_q": const("causal_q", [P, P], BF16),
            "causal_k": const("causal_k", [P, P], BF16),
            "spread": const("spread", [96, 10, P], BF16),
            "pick": const("pick", [8, 8, P], BF16),
        }
        loaded = ctx.enter_context(nc.semaphore("consts_loaded"))
        with nc.Block() as block:
            @block.gpsimd
            def _(pool):
                nc.gpsimd.memset(consts["eps"][:, :], EPS)
                nc.gpsimd.memset(consts["minus_half"][:, :], -0.5)

            @block.sync
            def _(sp):
                for name in ("ident", "ident16", "rank", "pick", "spread", "causal_q", "causal_k"):
                    sp.dma_start(consts[name][:], t["c_" + name]).then_inc(loaded, 16)
                sp.wait_ge(loaded, 16 * 7)
        x = t["X"]
        for n, (kind, pre) in enumerate(stages):
            last = n == len(stages) - 1
            y = out if last else nc.dram_tensor(f"x_after_{n}", [NB, T, D], F32, kind="Internal").ap()
            w = {k[len(pre):]: v for k, v in t.items() if k.startswith(pre)}
            kind(nc, f"s{n}", x, y, consts, w)
            x = y


def lay_out(inputs):
    bf16 = mybir.dt.np(BF16)
    a = {k: np.ascontiguousarray(v) for k, v in inputs.items()}
    t = {k: v for k, v in a.items() if k != "L0_attn_X"}
    t["X"] = a["L0_attn_X"]
    t["L0_ffn_gate_w"] = np.ascontiguousarray(a["L0_ffn_gate_w"].T)
    t["L0_ffn_b1"] = np.ascontiguousarray(a["L0_ffn_b1"].reshape(8, -1, P).transpose(2, 0, 1))
    t["L0_ffn_b2"] = np.ascontiguousarray(a["L0_ffn_b2"].T)
    f = "L1_ffn_"
    for n in ("Wg", "Wsg", "We_gate", "We_up", "We_down", "Ws_gate", "Ws_up", "Ws_down"):
        del t[f + n]
    def chunks(rows):
        return np.ascontiguousarray(rows.reshape(-1, P, rows.shape[-1]).transpose(2, 0, 1))
    t[f + "router"] = np.ascontiguousarray(np.concatenate([a[f + "Wg"], a[f + "Wsg"]]).T)
    t[f + "gate"] = chunks(np.concatenate([a[f + "We_gate"].reshape(-1, D), a[f + "Ws_gate"]]))
    t[f + "up"] = chunks(np.concatenate([a[f + "We_up"].reshape(-1, D), a[f + "Ws_up"]]))
    down = np.concatenate([a[f + "We_down"].transpose(0, 2, 1).reshape(-1, D), a[f + "Ws_down"].T])
    t[f + "down"] = np.ascontiguousarray(down.reshape(-1, P, D).transpose(1, 0, 2))
    spread = np.zeros((3, 32, 10, P))
    for k in range(8):
        spread[:, 2 * k, k, :P // 2] = spread[:, 2 * k + 1, k, P // 2:] = 1
    spread[:, 16, 8:] = 1
    t["c_spread"] = spread.reshape(96, 10, P).astype(bf16)
    order = np.array([[2 * i + g, d] for g in range(2) for d in range(8) for i in range(8)])
    head, feat = order[:, 0], order[:, 1]
    f = "L0_attn_"
    for q in "qk":
        for c in range(2):
            t[f + f"W{q}{c}"] = np.ascontiguousarray(a[f + "W" + q][:, head * 16 + c * 8 + feat])
        del t[f + "W" + q]
    t[f + "Wo"] = np.ascontiguousarray(a[f + "Wo"].reshape(2, P, D).transpose(1, 0, 2))
    f = "L1_attn_"
    plain = np.arange(P)
    swap = plain // 8 * 8 + (plain + 4) % 8
    kv = lambda x: np.concatenate([x[..., i] for i in (plain // 8 * 16 + plain % 8, swap // 8 * 16 + swap % 8,
                                                       plain // 8 * 16 + 8 + plain % 8)], -1)
    t[f + "Wq"] = np.concatenate([a[f + "Wq"], a[f + "Wq"][:, swap]], 1)
    t[f + "Wkv"] = kv(a[f + "Wup"])
    t[f + "bqkv"] = np.concatenate([a[f + "bq"], a[f + "bq"][swap], kv(a[f + "bup"])])
    t[f + "bdown"] = a[f + "bdown"].reshape(-1, 1)
    t[f + "Wo"] = a[f + "Wout"]
    for n in ("Wup", "bup", "Wout", "bq"):
        del t[f + n]
    inv_freq = (1.0 / np.float32(10000.0) ** (np.arange(0, 8, 2, dtype=np.float32) / np.float32(8))).astype(np.float32)
    angle = (np.arange(T, dtype=np.float32)[:, None] * inv_freq[None, plain % 4]).astype(np.float32)
    sign = np.where(plain % 8 < 4, -1, 1)
    rope = np.concatenate([np.cos(angle), sign * np.sin(angle)] * 2, 1).astype(np.float32)
    t[f + "rope"] = np.ascontiguousarray(rope.reshape(J, P, 4 * P).transpose(1, 0, 2))
    for f in ("L0_attn_",):
        t[f + "minus_ones"] = np.full((3, 8, T), -1).astype(bf16)
    later = np.arange(P)[None, :] > np.arange(P)[:, None]
    t["c_causal_q"] = np.where(later, -1e30, 0).astype(bf16)
    t["c_causal_k"] = np.where(later.T, -1e30, 0).astype(bf16)
    t["c_ident"] = np.eye(P, dtype=np.float32)
    t["c_ident16"] = np.eye(P).astype(bf16)
    t["c_rank"] = np.tile(np.arange(16, 0, -1, dtype=np.float32), (P, 1))
    t["c_pick"] = np.repeat(np.eye(8), P, axis=1).reshape(8, 8, P).astype(bf16)
    return t


STAGES = [(moe_top1_stage, "L0_ffn_"), (attention_stage, "L0_attn_"), (moe_top1_stage, "L0_ffn_"),
          (moe_top2_stage, "L1_ffn_"), (head_mixing_stage, "L1_attn_"), (moe_top2_stage, "L1_ffn_")]


def kernel(**inputs):
    import concourse.bacc as bacc
    from concourse.bass_utils import run_bass_kernel_spmd

    arrays = lay_out(inputs)
    nc = bacc.Bacc("TRN2", target_bir_lowering=False, num_devices=1)
    t = {k: nc.dram_tensor("in_" + k, v.shape, mybir.dt.from_np(v.dtype), kind="ExternalInput").ap()
         for k, v in arrays.items()}
    out = nc.dram_tensor("out_0", arrays["X"].shape, F32, kind="ExternalOutput").ap()
    build(nc, t, out, STAGES)
    result = run_bass_kernel_spmd(nc, [{"in_" + k: v for k, v in arrays.items()}], core_ids=[0])
    return result.results[0]["out_0"]
```

```python
from contextlib import ExitStack

import numpy as np

import concourse.bass as bass
from concourse import mybir

F32 = mybir.dt.float32
BF16 = mybir.dt.bfloat16
I32 = mybir.dt.int32
ALU = mybir.AluOpType
ACT = mybir.ActivationFunctionType
AX = mybir.AxisListType

P = 128
D = 128
T = 512
J = T // P
EPS = 1e-5
LAMBDA_INIT = 0.8
ROWS = 256


class Chain:

    def __init__(self, eng, sem, per):
        self.eng, self.sem, self.per, self.base, self.n = eng, sem, per, 0, 0

    def start(self, b):
        self.base, self.n = b * self.per, 0

    def mark(self, ins):
        self.n += 1
        return ins.then_inc(self.sem, 1)

    def after(self, ins):
        self.mark(ins)
        self.eng.wait_ge(self.sem, self.base + self.n)

    def end(self):
        assert self.n == self.per, (self.n, self.per)


def along(ap, n):
    return ap.rearrange("p (a o) -> p a o", o=1).broadcast_to([ap.shape[0], ap.shape[1], n])


def over(ap, n):
    return ap.rearrange("p (o a) -> p o a", o=1).broadcast_to([ap.shape[0], n, ap.shape[1]])


def pick_tile(t, n):
    return t[:, n] if isinstance(n, int) else t[:, bass.ds(n, 1)].rearrange("p o d -> p (o d)")


def two_batches(eng, turns, body):
    with eng.Fori(0, turns) as turn:
        for par in range(2):
            body(2 * turn + par, par)


class Resources:

    def __init__(self, nc, ctx, name, src, dst, consts):
        self.nc, self.ctx, self.name, self.src, self.dst, self.consts = nc, ctx, name, src, dst, consts
        self.NB = src.shape[0]
        self.sems = []
        self.tick = self.sem("tick")
        self.weights_loaded = self.sem("weights_loaded")
        self.early_loaded = self.sem("early_loaded")
        self.n_weights = self.n_early = 0

    def sb(self, name, shape, dt):
        return self.ctx.enter_context(self.nc.sbuf_tensor(f"{self.name}_{name}", shape, dt))

    def ps(self, name, shape, dt):
        return self.ctx.enter_context(self.nc.psum_tensor(f"{self.name}_{name}", shape, dt))

    def sem(self, name):
        self.sems.append(self.nc.alloc_semaphore(f"{self.name}_{name}"))
        return self.sems[-1]

    def finish(self):
        self.nc.clear_and_free_semaphores(self.sems)
        self.nc.all_engine_barrier()

    def load_weight(self, sp, dst, src):
        sp.dma_start(dst, src).then_inc(self.weights_loaded, 16)
        self.n_weights += 1

    def load_early(self, sp, dst, src):
        sp.dma_start(dst, src).then_inc(self.early_loaded, 16)
        self.n_early += 1

    def wait_early(self, eng):
        eng.wait_ge(self.early_loaded, 16 * self.n_early)

    def wait_weights(self, eng):
        eng.wait_ge(self.weights_loaded, 16 * self.n_weights)


class Stage(Resources):

    def __init__(self, nc, ctx, name, src, dst, consts):
        super().__init__(nc, ctx, name, src, dst, consts)
        assert self.NB % 2 == 0 and self.NB >= 4
        self.x_in = self.sb("x_in", [P, 2, J, D], F32)
        self.stats = self.sb("stats", [P, J, 6], F32)
        self.mean_var = self.sb("mean_var", [P, J, 2], F32)
        self.var_eps = self.sb("var_eps", [P, J], F32)
        self.rstd = self.sb("rstd", [P, J], F32)
        self.x_centred = self.sb("x_centred", [P, J, D], F32)
        self.x_hat = self.sb("x_hat", [P, J, D], F32)
        self.xT = self.sb("xT", [P, 2, T], F32)
        self.x_out = self.sb("x_out", [P, 2, J, D], F32)
        self.misc = self.ps("misc", [P, T], F32)
        self.x_loaded = [self.sem(f"x_loaded{par}") for par in range(2)]
        self.stats_done = self.sem("stats_done")
        self.mean_var_ready = self.sem("mean_var_ready")
        self.norm_step = self.sem("norm_step")
        self.x_hat_ready = self.sem("x_hat_ready")
        self.xT_in_psum = self.sem("xT_in_psum")
        self.xT_ready = self.sem("xT_ready")
        self.residual_free = self.sem("residual_free")
        self.x_out_free = [self.sem(f"x_out_free{par}") for par in range(2)]

    def load_x(self, sp, b, par):
        sp.dma_start(self.x_in[:, par], self.src[b].rearrange("(j p) d -> p j d", p=P)).then_inc(self.x_loaded[par], 16)

    def store_x(self, sp, b, par):
        sp.wait_ge(self.residual_free, b + 2)
        sp.dma_start(self.dst[b].rearrange("(j p) d -> p j d", p=P), self.x_out[:, par]).then_inc(self.x_out_free[par], 16)

    def stream(self, sp):
        for par in range(2):
            sp.sem_inc(self.x_out_free[par], 16)
        def body(b, par):
            self.store_x(sp, b, par)
            self.load_x(sp, b + 2, par)
        two_batches(sp, self.NB // 2 - 1, body)
        self.store_x(sp, self.NB - 2, 0)
        self.load_x(sp, 0, 0)
        self.store_x(sp, self.NB - 1, 1)
        for par in range(2):
            sp.wait_ge(self.x_out_free[par], 16 + 8 * self.NB)
        sp.wait_ge(self.x_loaded[0], 8 * self.NB + 16)

    def norm_stats(self, dve, b, par):
        nc = self.nc
        dve.wait_ge(self.x_loaded[par], 8 * (b - par) + 16)
        for j in range(J):
            last = nc.vector.bn_stats(self.stats[:, j, :], self.x_in[:, par, j, :])
        last.then_inc(self.stats_done, 1)
        dve.wait_ge(self.stats_done, b + 1)
        dve.sem_inc(self.tick, 1)
        for j in range(J):
            last = nc.vector.bn_aggr(self.mean_var[:, j, :], self.stats[:, j, :])
        last.then_inc(self.mean_var_ready, 1)

    def norm_apply(self, pool, b, par):
        nc, c = self.nc, self.consts
        pool.wait_ge(self.mean_var_ready, b + 1)
        nc.gpsimd.tensor_tensor(self.var_eps[:, :], self.mean_var[:, :, 1], c["eps"][:, 0:J], ALU.add)\
            .then_inc(self.norm_step, 1)
        nc.gpsimd.tensor_tensor(self.x_centred[:, :, :], self.x_in[:, par], along(self.mean_var[:, :, 0], D), ALU.subtract)\
            .then_inc(self.norm_step, 1)
        pool.wait_ge(self.norm_step, 3 * b + 2)
        nc.gpsimd.tensor_tensor(self.rstd[:, :], self.var_eps[:, :], c["minus_half"][:, 0:J], ALU.pow)\
            .then_inc(self.norm_step, 1)
        pool.wait_ge(self.norm_step, 3 * b + 3)
        nc.gpsimd.tensor_tensor(self.x_hat[:, :, :], self.x_centred[:, :, :],
                                along(self.rstd[:, :], D), ALU.mult).then_inc(self.x_hat_ready, 1)

    def norm_transpose(self, pe, b, first=False):
        pe.wait_ge(self.x_hat_ready, b + 1)
        if not first:
            pe.wait_ge(self.residual_free, b)
        for j in range(J):
            last = self.nc.tensor.transpose(self.misc[:, j * P:(j + 1) * P], self.x_hat[:, j, :], self.consts["ident"][:, :])
        last.then_inc(self.xT_in_psum, 1)

    def norm_store(self, act, b, par):
        act.wait_ge(self.xT_in_psum, b + 1)
        self.nc.scalar.activation(self.xT[:, par], self.misc[:, :], ACT.Copy).then_inc(self.xT_ready, 1)




def moe_top1_stage(nc, name, src, dst, consts, w, scratch):
    E, _, F = w["w1"].shape
    C = F // P
    with ExitStack() as ctx:
        st = Resources(nc, ctx, name, src, dst, consts)
        sb, ps, sem, NB = st.sb, st.ps, st.sem, st.NB
        NT = NB * J
        TILES = NB * T // ROWS + E - 1
        FULL = NB * T // ROWS
        B = ROWS // P
        sorted_x, sorted_y = (s[0:TILES * ROWS, :] for s in scratch)
        w12 = sb("w12", [P, E, F + C * D], F32)
        w12_own = sb("w12_own", [P, 2, F + C * D], F32)
        b1 = sb("b1", [P, E, C], F32)
        b2 = sb("b2", [P, E], F32)
        gate_w = sb("gate_w", [P, E], F32)
        gate_b = sb("gate_b", [P, E], F32)
        expert_bias = sb("expert_bias", [P, E], F32)
        x = sb("x", [P, NT, D], F32)
        x_hat = sb("x_hat", [P, NT, D], F32)
        stats = sb("stats", [P, 2, J, 6], F32)
        mean_var = sb("mean_var", [P, 2, J, 2], F32)
        var_eps = sb("var_eps", [P, 2, J], F32)
        rstd = sb("rstd", [P, 2, J], F32)
        xT = sb("xT", [P, 2, T], F32)
        logits_g = sb("logits_g", [P, NT, E], F32)
        logits = sb("logits", [P, NT, E], F32)
        at_max = sb("at_max", [P, NT, E], F32)
        ranked = sb("ranked", [P, NT, E], F32)
        best = sb("best", [P, NT], F32)
        best_rank = sb("best_rank", [P, NT], F32)
        onehot = sb("onehot", [P, NT, E], BF16)
        running = sb("running", [P, 2, NT, E], F32)
        filled = sb("filled", [P, E, FULL], F32)
        rows = sb("rows", [P, E], F32)
        ends = sb("ends", [P, 4, E], F32)
        begins = sb("begins", [P, E], F32)
        place = sb("place", [P, 4, NT, E], F32)
        row_f = sb("row_f", [P, NT], F32)
        row = sb("row", [P, NT], I32)
        passed = sb("passed", [P, TILES, E], F32)
        expert_f = sb("expert_f", [P, 2, TILES], F32)
        expert = sb("expert", [P, TILES], I32)
        xs = sb("xs", [P, 2, B, D], F32)
        xsT = sb("xsT", [P, 2, ROWS], F32)
        h = sb("h", [P, 2, C, ROWS], F32)
        yT = sb("yT", [P, 2, ROWS], F32)
        ys = sb("ys", [P, 2, B, D], F32)
        turn_psum = ps("turn_psum", [P, 2, T], F32)
        h_psum = ps("h_psum", [P, C, T], F32)
        logits_psum = h_psum[:, 0, 0:NT * E].rearrange("p (t e) -> p t e", e=E)
        counts_psum = h_psum[:, 1, 0:2 * NT * E].rearrange("p (k t e) -> p k t e", k=2, e=E)
        y_psum = ps("y_psum", [P, T], F32)
        ys_psum = ps("ys_psum", [P, T], F32)
        rank, starts, ident = consts["rank"], consts["starts"], consts["ident"]

        x_loaded = [sem(f"x_loaded{par}") for par in range(2)]
        stats_done = sem("stats_done")
        mean_var_ready = sem("mean_var_ready")
        var_eps_ready = sem("var_eps_ready")
        rstd_ready = sem("rstd_ready")
        x_hat_ready = sem("x_hat_ready")
        xT_in_psum = sem("xT_in_psum")
        xT_ready = sem("xT_ready")
        logits_in_psum = sem("logits_in_psum")
        route_step = sem("route_step")
        onehot_ready = sem("onehot_ready")
        counts_in_psum = sem("counts_in_psum")
        row_ready = sem("row_ready")
        expert_ready = sem("expert_ready")
        w12_ready = sem("w12_ready")
        scattered = sem("scattered")
        xs_loaded = [sem(f"xs_loaded{par}") for par in range(2)]
        xsT_in_psum = sem("xsT_in_psum")
        xsT_ready = sem("xsT_ready")
        h_in_psum = sem("h_in_psum")
        h_ready = sem("h_ready")
        y_in_psum = sem("y_in_psum")
        yT_ready = sem("yT_ready")
        ys_in_psum = sem("ys_in_psum")
        ys_ready = sem("ys_ready")
        ys_stored = [sem(f"ys_stored{par}") for par in range(2)]
        gathered = [sem(f"gathered{b}") for b in range(NB)]
        residual_ready = sem("residual_ready")
        x_stored = sem("x_stored")

        def tiles(eng, body, lo=0):
            body(0, 0, True, False)
            middle = TILES - 2
            with eng.Fori(0, middle // 2) as turn:
                for k in range(2):
                    body(2 * turn + 1 + k, (1 + k) % 2, False, False)
            for i in range(1 + middle // 2 * 2, TILES):
                body(i, i % 2, False, i == TILES - 1)

        with nc.Block() as block:

            @block.sync
            def _(sp):
                def load_x(b, par):
                    if not (isinstance(b, int) and b < 2):
                        sp.wait_ge(x_loaded[par], 8 * (b - par))
                        sp.sem_inc(st.tick, 1)
                    sp.dma_start(x[:, 4 * b:4 * b + 4] if isinstance(b, int) else x[:, bass.ds(4 * b, 4)],
                                 src[b].rearrange("(j p) d -> p j d", p=P)).then_inc(x_loaded[par], 16)

                def load_xs(i, par):
                    sp.dma_start(xs[:, par], sorted_x[bass.ds(i * ROWS, ROWS), :].rearrange("(k p) d -> p k d", p=P))\
                        .then_inc(xs_loaded[par], 16)

                load_x(0, 0)
                load_x(1, 1)
                st.load_early(sp, gate_w[:, :], w["gate_w"])
                st.load_early(sp, gate_b[:, :], w["gate_b"].rearrange("(o e) -> o e", o=1).broadcast_to([P, E]))
                st.load_early(sp, expert_bias[:, :],
                               w["expert_bias"].rearrange("(o e) -> o e", o=1).broadcast_to([P, E]))
                st.load_weight(sp, b1[:, :, :], w["b1"])
                st.load_weight(sp, b2[:, :], w["b2"])
                with sp.Fori(1, NB // 2) as turn:
                    for par in range(2):
                        load_x(2 * turn + par, par)
                for e in range(E):
                    st.load_weight(sp, w12[:, e, 0:F], w["w1"][e])
                    st.load_weight(sp, w12[:, e, F:].rearrange("p (c d) -> p c d", d=D),
                                   w["w2"][e].rearrange("(c p) d -> p c d", p=P))
                for par in range(2):
                    sp.sem_inc(ys_stored[par], 16)
                sp.wait_ge(scattered, 16 * NT)
                load_xs(0, 0)
                load_xs(1, 1)

                def tile(i, par, first, last):
                    if not (isinstance(i, int) and i + 2 >= TILES):
                        sp.wait_ge(xsT_in_psum, i + 1)
                        sp.sem_inc(st.tick, 1)
                        load_xs(i + 2, par)
                    sp.wait_ge(ys_ready, i + 1)
                    sp.sem_inc(st.tick, 1)
                    sp.dma_start(sorted_y[bass.ds(i * ROWS, ROWS), :].rearrange("(k p) d -> p k d", p=P), ys[:, par])\
                        .then_inc(ys_stored[par], 16)

                tile(0, 0, True, False)
                middle = (TILES - 3) // 2
                with sp.Fori(0, middle) as turn:
                    for k in range(2):
                        tile(2 * turn + 1 + k, (1 + k) % 2, False, False)
                for i in range(2 * middle + 1, TILES):
                    tile(i, i % 2, False, i == TILES - 1)
                for b in range(NB):
                    sp.wait_ge(residual_ready, b + 1)
                    sp.dma_start(dst[b].rearrange("(j p) d -> p j d", p=P), x[:, b * J:(b + 1) * J]).then_inc(x_stored, 16)
                sp.wait_ge(x_stored, 16 * NB)

            @block.gpsimd
            def _(pool):
                def norm_scale(b, par):
                    pool.wait_ge(mean_var_ready, b + 1)
                    nc.gpsimd.tensor_tensor(var_eps[:, par], mean_var[:, par, :, 1], consts["eps"][:, 0:J], ALU.add)\
                        .then_inc(var_eps_ready, 1)
                    pool.wait_ge(var_eps_ready, b + 1)
                    nc.gpsimd.tensor_tensor(rstd[:, par], var_eps[:, par], consts["minus_half"][:, 0:J], ALU.pow)\
                        .then_inc(rstd_ready, 1)

                two_batches(pool, NB // 2, norm_scale)
                pool.wait_ge(row_ready, 1)
                for t in range(NT):
                    nc.gpsimd.indirect_dma_start(sorted_x, bass.IndirectOffsetOnAxis(row[:, t:t + 1], axis=0),
                                                 x_hat[:, t, :], None).then_inc(scattered, 16)
                pool.wait_ge(scattered, 16 * NT)
                for par in range(2):
                    pool.wait_ge(ys_stored[par], 16 + 16 * ((TILES + 1 - par) // 2))
                for t in range(NT):
                    nc.gpsimd.indirect_dma_start(x_hat[:, t, :], None, sorted_y,
                                                 bass.IndirectOffsetOnAxis(row[:, t:t + 1], axis=0))\
                        .then_inc(gathered[t // J], 16)

            @block.tensor
            def _(pe):
                mm = nc.tensor.matmul

                def turn_x(b, par):
                    pe.wait_ge(x_hat_ready, b + 1)
                    for j in range(J):
                        last = nc.tensor.transpose(turn_psum[:, par, j * P:(j + 1) * P], pick_tile(x_hat, 4 * b + j), ident[:, :])
                    last.then_inc(xT_in_psum, 1)

                def gate(b, par):
                    pe.wait_ge(xT_ready, b + 1)
                    for j in range(J):
                        last = mm(logits_psum[:, 4 * b + j], xT[:, par, j * P:(j + 1) * P], gate_w[:, :],
                                  start=True, stop=True)
                    last.then_inc(logits_in_psum, 1)

                def turn_in(i, par):
                    pe.wait_ge(xs_loaded[par], 8 * (i - par) + 16)
                    for k in range(B):
                        last = nc.tensor.transpose(turn_psum[:, par, k * P:(k + 1) * P], xs[:, par, k, :], ident[:, :])
                    last.then_inc(xsT_in_psum, 1)

                def hidden(i, par):
                    pe.wait_ge(w12_ready, i + 1)
                    pe.wait_ge(xsT_ready, i + 1)
                    for c in range(C):
                        mm(h_psum[:, c, 0:ROWS], w12_own[:, par, c * P:(c + 1) * P], xsT[:, par], start=True, stop=True)\
                            .then_inc(h_in_psum, 1)

                def output(i, par):
                    pe.wait_ge(h_ready, C * i + C)
                    for c in range(C):
                        last = mm(y_psum[:, 0:ROWS], w12_own[:, par, F + c * D:F + (c + 1) * D], h[:, par, c, :],
                                  start=(c == 0), stop=(c == C - 1))
                    last.then_inc(y_in_psum, 1)

                def turn_out(i, par):
                    pe.wait_ge(yT_ready, i + 1)
                    if not (isinstance(i, int) and i == 0):
                        pe.wait_ge(ys_ready, i)
                    for k in range(B):
                        last = nc.tensor.transpose(ys_psum[:, k * P:(k + 1) * P], yT[:, par, k * P:(k + 1) * P], ident[:, :])
                    last.then_inc(ys_in_psum, 1)

                def tile(i, par, first, last):
                    if not last:
                        turn_in(i + 1, 1 - par)
                    if not first:
                        turn_out(i - 1, 1 - par)
                    output(i, par)
                    if not last:
                        hidden(i + 1, 1 - par)

                turn_x(0, 0)
                st.wait_early(pe)
                turn_x(1, 1)
                gate(0, 0)
                for b in range(2, NB):
                    turn_x(b, b % 2)
                    gate(b - 1, 1 - b % 2)
                gate(NB - 1, 1)
                pe.wait_ge(onehot_ready, 1)
                flat = onehot[:, :, :].rearrange("p t e -> p (t e)")
                for k, m in enumerate((consts["earlier"], consts["ones"])):
                    last = mm(counts_psum[:, k].rearrange("p t e -> p (t e)"), m[:, :], flat, start=True, stop=True)
                last.then_inc(counts_in_psum, 1)
                pe.wait_ge(expert_ready, 1)
                turn_in(0, 0)
                hidden(0, 0)
                tiles(pe, tile)
                turn_out(TILES - 1, (TILES - 1) % 2)

            @block.scalar
            def _(act):
                def store_xT(b, par):
                    act.wait_ge(xT_in_psum, b + 1)
                    nc.scalar.activation(xT[:, par], turn_psum[:, par], ACT.Copy).then_inc(xT_ready, 1)

                def store_xsT(i, par):
                    act.wait_ge(xsT_in_psum, i + 1)
                    nc.scalar.activation(xsT[:, par], turn_psum[:, par, 0:ROWS], ACT.Copy).then_inc(xsT_ready, 1)

                def relus(i, par):
                    e = act.value_load(expert[0:1, bass.ds(i, 1)], min_val=0, max_val=E - 1)
                    for c in range(C):
                        act.wait_ge(h_in_psum, C * i + c + 1)
                        act.sem_inc(st.tick, 1)
                        nc.scalar.activation(h[:, par, c, :], h_psum[:, c, 0:ROWS], ACT.Relu,
                                             bias=b1[:, bass.ds(e, 1), c:c + 1].rearrange("p e c -> p (e c)")).then_inc(h_ready, 1)

                def add_b2(i, par):
                    e = act.value_load(expert[0:1, bass.ds(i, 1)], min_val=0, max_val=E - 1)
                    act.wait_ge(y_in_psum, i + 1)
                    act.sem_inc(st.tick, 1)
                    nc.scalar.activation(yT[:, par], y_psum[:, 0:ROWS], ACT.Identity, bias=b2[:, bass.ds(e, 1)]).then_inc(yT_ready, 1)

                def tile(i, par, first, last):
                    if not last:
                        store_xsT(i + 1, 1 - par)
                    add_b2(i, par)
                    if not last:
                        relus(i + 1, 1 - par)

                two_batches(act, NB // 2, store_xT)
                st.wait_weights(act)
                act.wait_ge(expert_ready, 1)
                store_xsT(0, 0)
                relus(0, 0)
                tiles(act, tile)

            @block.vector
            def _(dve):
                tt, reduce = nc.vector.tensor_tensor, nc.vector.tensor_reduce
                SPAN = [1 << k for k in range(16) if 1 << k < NT]
                SPAN_E = [1 << k for k in range(16) if 1 << k < E]
                route = Chain(dve, route_step, 0)

                def norm_stats(b, par):
                    dve.wait_ge(x_loaded[par], 8 * (b - par) + 16)
                    dve.sem_inc(st.tick, 1)
                    for j in range(J):
                        last = nc.vector.bn_stats(stats[:, par, j, :], pick_tile(x, 4 * b + j))
                    last.then_inc(stats_done, 1)
                    dve.wait_ge(stats_done, b + 1)
                    dve.sem_inc(st.tick, 1)
                    for j in range(J):
                        last = nc.vector.bn_aggr(mean_var[:, par, j, :], stats[:, par, j, :])
                    last.then_inc(mean_var_ready, 1)

                def norm_apply(b, par):
                    dve.wait_ge(rstd_ready, b + 1)
                    dve.sem_inc(st.tick, 1)
                    for j in range(J):
                        last = nc.vector.tensor_scalar(pick_tile(x_hat, 4 * b + j), pick_tile(x, 4 * b + j),
                                                       mean_var[:, par, j, 0:1], rstd[:, par, j:j + 1],
                                                       ALU.subtract, ALU.mult)
                    last.then_inc(x_hat_ready, 1)

                def fetch_w12(i, par):
                    e = dve.value_load(expert[0:1, bass.ds(i, 1)], min_val=0, max_val=E - 1)
                    if not (isinstance(i, int) and i < 2):
                        dve.wait_ge(y_in_psum, i - 1)
                        dve.sem_inc(st.tick, 1)
                    nc.vector.tensor_copy(w12_own[:, par], pick_tile(w12, e)).then_inc(w12_ready, 1)

                def copy_out(i, par):
                    dve.wait_ge(ys_in_psum, i + 1)
                    dve.wait_ge(ys_stored[par], 8 * (i - par) + 16)
                    nc.vector.tensor_copy(ys[:, par].rearrange("p k d -> p (k d)"), ys_psum[:, 0:ROWS]).then_inc(ys_ready, 1)

                def tile(i, par, first, last):
                    if not first:
                        copy_out(i - 1, 1 - par)
                    if not last:
                        fetch_w12(i + 1, 1 - par)

                norm_stats(0, 0)
                with dve.Fori(0, NB // 2 - 1) as turn:
                    for par in range(2):
                        norm_stats(2 * turn + 1 + par, 1 - par)
                        norm_apply(2 * turn + par, par)
                norm_stats(NB - 1, 1)
                norm_apply(NB - 2, 0)
                norm_apply(NB - 1, 1)

                do = route.after
                st.wait_early(dve)
                dve.wait_ge(logits_in_psum, NB)
                do(tt(logits_g[:, :, :], logits_psum, over(gate_b[:, :], NT), ALU.add))
                do(tt(logits[:, :, :], logits_g[:, :, :], over(expert_bias[:, :], NT), ALU.add))
                do(reduce(best[:, :], logits[:, :, :], AX.X, ALU.max))
                do(tt(at_max[:, :, :], logits[:, :, :], along(best[:, :], E), ALU.is_ge))
                do(tt(ranked[:, :, :], at_max[:, :, :], over(rank[:, 0:E], NT), ALU.mult))
                do(reduce(best_rank[:, :], ranked[:, :, :], AX.X, ALU.max))
                tt(onehot[:, :, :], ranked[:, :, :], along(best_rank[:, :], E), ALU.is_equal).then_inc(onehot_ready, 1)

                dve.wait_ge(counts_in_psum, 1)
                before, in_tile = counts_psum[:, 0], counts_psum[:, 1]
                do(nc.vector.tensor_copy(running[:, 1], in_tile))
                now = running[:, 1]
                for k, s in enumerate(SPAN):
                    to = running[:, k % 2]
                    route.mark(nc.vector.tensor_copy(to[:, 0:s, :], now[:, 0:s, :]))
                    do(tt(to[:, s:NT, :], now[:, s:NT, :], now[:, 0:NT - s, :], ALU.add))
                    now = to
                do(tt(filled[:, :, :], along(now[:, NT - 1, :], FULL), over(starts[:, 0:FULL], E), ALU.is_gt))
                do(reduce(rows[:, :], filled[:, :, :], AX.X, ALU.add))
                do(nc.vector.tensor_scalar(ends[:, 0], rows[:, :], float(ROWS), None, ALU.mult))
                end = ends[:, 0]
                for k, s in enumerate(SPAN_E):
                    to = ends[:, k + 1]
                    route.mark(nc.vector.tensor_copy(to[:, 0:s], end[:, 0:s]))
                    do(tt(to[:, s:E], end[:, s:E], end[:, 0:E - s], ALU.add))
                    end = to
                route.mark(tt(begins[:, :], end, ends[:, 0], ALU.subtract))
                do(tt(place[:, 0], now, in_tile, ALU.subtract))
                do(tt(place[:, 1], place[:, 0], before, ALU.add))
                do(tt(place[:, 2], place[:, 1], over(begins[:, :], NT), ALU.add))
                do(tt(place[:, 3], place[:, 2], onehot[:, :, :], ALU.mult))
                do(reduce(row_f[:, :], place[:, 3], AX.X, ALU.add))
                nc.vector.tensor_copy(row[:, :], row_f[:, :]).then_inc(row_ready, 1)
                do(tt(passed[:, :, :], over(end, TILES), along(starts[:, 0:TILES], E), ALU.is_le))
                do(reduce(expert_f[:, 0], passed[:, :, :], AX.X, ALU.add))
                do(nc.vector.tensor_scalar(expert_f[:, 1], expert_f[:, 0], float(E - 1), None, ALU.min))
                nc.vector.tensor_copy(expert[:, :], expert_f[:, 1]).then_inc(expert_ready, 1)

                dve.wait_ge(expert_ready, 1)
                st.wait_weights(dve)
                fetch_w12(0, 0)
                tiles(dve, tile)
                copy_out(TILES - 1, (TILES - 1) % 2)
                for b in range(NB):
                    dve.wait_ge(gathered[b], 16 * J)
                    own = slice(b * J, (b + 1) * J)
                    flat = lambda a: a[:, own].rearrange("p j d -> p (j d)")
                    nc.vector.scalar_tensor_tensor(out=flat(x), in0=flat(x_hat), scalar=0.5, in1=flat(x),
                                                   op0=ALU.mult, op1=ALU.add).then_inc(residual_ready, 1)

        st.finish()




def moe_top2_stage(nc, name, src, dst, consts, w, scratch):
    E = w["router"].shape[1] - 1
    K = w["gate"].shape[1]
    L = w["router"].shape[1]
    S = 32
    assert L == E + 1 and L <= S
    with ExitStack() as ctx:
        st = Stage(nc, ctx, name, src, dst, consts)
        sb, ps, sem, misc, xT = st.sb, st.ps, st.sem, st.misc, st.xT
        router = sb("router", [P, L], F32)
        w_gate = sb("w_gate", [P, K, P], F32)
        w_up = sb("w_up", [P, K, P], F32)
        w_down = sb("w_down", [P, K, D], F32)
        silu = sb("silu", [P, 2, T], F32)
        weight = sb("weight", [P, 2, T], F32)
        gated = sb("gated", [P, 2, T], F32)
        h = sb("h", [P, 2, T], F32)
        acc = sb("acc", [P, 2, T], F32)
        exp_in = sb("exp_in", [P, J, L], F32)
        exp_out = sb("exp_out", [P, J, L], F32)
        gates = sb("gates", [P, J, E], F32)
        gates_rest = sb("gates_rest", [P, J, E], F32)
        at_max = sb("at_max", [P, J, E], F32)
        ranked = sb("ranked", [P, J, E], F32)
        first = sb("first", [P, J, E], F32)
        second = sb("second", [P, J, E], F32)
        small = {n: sb(n, [P, J], F32) for n in
                 ("top", "total", "inv_total", "best", "rank1", "next_best", "rank2", "both", "inv_both", "shared_den")}
        token_w = sb("token_w", [P, J, L], F32)
        rest1 = sb("rest1", [P, J, L], F32)
        parts = sb("parts", [P, J, 3 * S], BF16)
        partsT = sb("partsT", [3 * S, 2, T], BF16)
        g_psum = ps("g_psum", [P, 2, T], F32)
        u_psum = ps("u_psum", [P, 2, T], F32)
        w_psum = ps("w_psum", [P, 2, T], F32)
        y_psum = ps("y_psum", [P, T], F32)
        spread, rank, ident, ident16 = consts["spread"], consts["rank"], consts["ident"], consts["ident16"]

        g_in_psum = sem("g_in_psum")
        u_in_psum = sem("u_in_psum")
        w_in_psum = sem("w_in_psum")
        silu_ready = sem("silu_ready")
        weight_ready = sem("weight_ready")
        gated_free = sem("gated_free")
        h_ready = sem("h_ready")
        h_free = sem("h_free")
        acc_ready = sem("acc_ready")
        parts_zeroed = sem("parts_zeroed")
        logits_in_psum = sem("logits_in_psum")
        exp_in_ready = sem("exp_in_ready")
        exp_ready = sem("exp_ready")
        gate_step = sem("gate_step")
        parts_ready = sem("parts_ready")
        partsT_in_psum = sem("partsT_in_psum")
        partsT_ready = sem("partsT_ready")
        out_in_psum = sem("out_in_psum")

        with nc.Block() as block:

            @block.sync
            def _(sp):
                st.load_x(sp, 0, 0)
                st.load_weight(sp, router[:, :], w["router"])
                st.load_weight(sp, w_gate[:, :, :], w["gate"])
                st.load_weight(sp, w_up[:, :, :], w["up"])
                st.load_x(sp, 1, 1)
                st.load_weight(sp, w_down[:, :, :], w["down"])
                st.stream(sp)

            @block.gpsimd
            def _(pool):
                nc.gpsimd.memset(parts[:, :, :], 0.0).then_inc(parts_zeroed, 1)
                st.norm_apply(pool, 0, 0)
                two_batches(pool, st.NB // 2, lambda b, par: st.norm_apply(pool, b + 1, 1 - par))

            @block.tensor
            def _(pe):
                def hidden(b, par, k, start=False):
                    n = K * b + k
                    if k == 0:
                        pe.wait_ge(st.xT_ready, b + 1)
                    if not start:
                        pe.wait_ge(silu_ready, n - 1)
                    nc.tensor.matmul(g_psum[:, k % 2, :], w_gate[:, k, :], xT[:, par], start=True, stop=True)\
                        .then_inc(g_in_psum, 1)
                    pe.wait_ge(gated_free, n + 1)
                    nc.tensor.matmul(u_psum[:, k % 2, :], w_up[:, k, :], xT[:, par], start=True, stop=True)\
                        .then_inc(u_in_psum, 1)
                    if k == 0:
                        pe.wait_ge(partsT_ready, b + 1)
                    if not start:
                        pe.wait_ge(weight_ready, n - 1)
                    pe.sem_inc(st.tick, 1)
                    nc.tensor.matmul(w_psum[:, k % 2, :], spread[:, k, :], partsT[:, par], start=True, stop=True)\
                        .then_inc(w_in_psum, 1)

                def down(b, k):
                    pe.wait_ge(h_ready, K * b + k + 1)
                    nc.tensor.matmul(y_psum[:, :], w_down[:, k, :], h[:, k % 2, :],
                                     start=(k == 0), stop=(k == K - 1)).then_inc(h_free, 1)

                def gate(b, par):
                    pe.wait_ge(st.xT_ready, b + 1)
                    for j in range(J):
                        last = nc.tensor.matmul(misc[:, j * L:(j + 1) * L], xT[:, par, j * P:(j + 1) * P],
                                                router[:, :], start=True, stop=True)
                    last.then_inc(logits_in_psum, 1)

                def turn_parts(b):
                    pe.wait_ge(parts_ready, b + 1)
                    for j in range(J):
                        last = nc.tensor.transpose(misc[0:3 * S, j * P // 2:(j + 1) * P // 2].bitcast(BF16),
                                                   parts[:, j, :], ident16[:, :])
                    last.then_inc(partsT_in_psum, 1)

                def turn_out(b, par):
                    pe.wait_ge(acc_ready, b + 1)
                    for j in range(J):
                        last = nc.tensor.transpose(misc[:, j * P:(j + 1) * P], acc[:, par, j * P:(j + 1) * P],
                                                   ident[:, :])
                    last.then_inc(out_in_psum, 1)

                def body(b, par):
                    for k in range(2, K):
                        hidden(b, par, k)
                        if k == 3:
                            st.norm_transpose(pe, b + 1)
                        if k == 5:
                            gate(b + 1, 1 - par)
                        if k == 9:
                            turn_parts(b + 1)
                        down(b, k - 2)
                    hidden(b + 1, 1 - par, 0)
                    down(b, K - 2)
                    hidden(b + 1, 1 - par, 1)
                    down(b, K - 1)
                    turn_out(b, par)

                st.wait_weights(pe)
                st.norm_transpose(pe, 0, first=True)
                gate(0, 0)
                turn_parts(0)
                hidden(0, 0, 0, start=True)
                hidden(0, 0, 1, start=True)
                two_batches(pe, st.NB // 2, body)

            @block.scalar
            def _(act):
                def chunk(b, k, start=False):
                    n = K * b + k
                    act.wait_ge(g_in_psum, n + 1)
                    act.wait_ge(gated_free, n + 1)
                    nc.scalar.activation(silu[:, k % 2, :], g_psum[:, k % 2, :], ACT.Silu).then_inc(silu_ready, 1)
                    act.wait_ge(w_in_psum, n + 1)
                    if not start:
                        act.wait_ge(h_ready, n - 1)
                    nc.scalar.activation(weight[:, k % 2, :], w_psum[:, k % 2, :], ACT.Copy).then_inc(weight_ready, 1)

                def exponentials(b):
                    act.wait_ge(exp_in_ready, b + 1)
                    nc.scalar.activation(exp_out[:, :, :], exp_in[:, :, :], ACT.Exp).then_inc(exp_ready, 1)

                def store_partsT(b, par):
                    act.wait_ge(partsT_in_psum, b + 1)
                    nc.scalar.activation(partsT[:, par], misc[0:3 * S, 0:T // 2].bitcast(BF16), ACT.Copy)\
                        .then_inc(partsT_ready, 1)

                def store_y(b, par):
                    act.wait_ge(h_free, K * b + K + 2)
                    nc.scalar.activation(acc[:, par], y_psum[:, :], ACT.Copy).then_inc(acc_ready, 1)

                def body(b, par):
                    for k in range(2, K):
                        chunk(b, k)
                        if k == 3:
                            st.norm_store(act, b + 1, 1 - par)
                        if k == 5:
                            exponentials(b + 1)
                        if k == 9:
                            store_partsT(b + 1, 1 - par)
                    chunk(b + 1, 0)
                    chunk(b + 1, 1)
                    store_y(b, par)

                st.wait_weights(act)
                st.norm_store(act, 0, 0)
                exponentials(0)
                store_partsT(0, 0)
                chunk(0, 0, start=True)
                chunk(0, 1, start=True)
                two_batches(act, st.NB // 2, body)

            @block.vector
            def _(dve):
                gate_chain = Chain(dve, gate_step, 25)

                def first_at(do, values, top, rank_of_top, onehot):
                    do(nc.vector.tensor_reduce(top[:, :], values[:, :, :], AX.X, ALU.max))
                    do(nc.vector.tensor_tensor(at_max[:, :, :], values[:, :, :], along(top[:, :], E), ALU.is_ge))
                    do(nc.vector.tensor_tensor(ranked[:, :, :], at_max[:, :, :], over(rank[:, 0:E], J), ALU.mult))
                    do(nc.vector.tensor_reduce(rank_of_top[:, :], ranked[:, :, :], AX.X, ALU.max))
                    do(nc.vector.tensor_tensor(onehot[:, :, :], ranked[:, :, :], along(rank_of_top[:, :], E),
                                               ALU.is_equal))

                def exp_inputs(b):
                    dve.wait_ge(logits_in_psum, b + 1)
                    gate_chain.start(b)
                    do = gate_chain.after
                    logits = misc[:, 0:J * L].rearrange("p (j e) -> p j e", j=J)
                    do(nc.vector.tensor_reduce(small["top"][:, :], logits[:, :, 0:E], AX.X, ALU.max))
                    nc.vector.tensor_tensor(exp_in[:, :, 0:E], logits[:, :, 0:E], along(small["top"][:, :], E),
                                            ALU.subtract)
                    nc.vector.tensor_scalar(exp_in[:, :, E], logits[:, :, E], -1.0, None, ALU.mult)\
                        .then_inc(exp_in_ready, 1)

                def token_weights(b):
                    do, s = gate_chain.after, small
                    dve.wait_ge(exp_ready, b + 1)
                    do(nc.vector.tensor_reduce(s["total"][:, :], exp_out[:, :, 0:E], AX.X, ALU.add))
                    do(nc.vector.reciprocal(s["inv_total"][:, :], s["total"][:, :]))
                    do(nc.vector.tensor_tensor(gates[:, :, :], exp_out[:, :, 0:E], along(s["inv_total"][:, :], E),
                                               ALU.mult))
                    first_at(do, gates, s["best"], s["rank1"], first)
                    do(nc.vector.scalar_tensor_tensor(out=gates_rest[:, :, :], in0=first[:, :, :], scalar=-4.0,
                                                      in1=gates[:, :, :], op0=ALU.mult, op1=ALU.add))
                    first_at(do, gates_rest, s["next_best"], s["rank2"], second)
                    do(nc.vector.tensor_tensor(s["both"][:, :], s["best"][:, :], s["next_best"][:, :], ALU.add))
                    do(nc.vector.reciprocal(s["inv_both"][:, :], s["both"][:, :]))
                    do(nc.vector.tensor_tensor(first[:, :, :], first[:, :, :], second[:, :, :], ALU.add))
                    do(nc.vector.tensor_tensor(first[:, :, :], first[:, :, :], gates[:, :, :], ALU.mult))
                    do(nc.vector.tensor_tensor(token_w[:, :, 0:E], first[:, :, :], along(s["inv_both"][:, :], E),
                                               ALU.mult))
                    do(nc.vector.tensor_scalar(s["shared_den"][:, :], exp_out[:, :, E], 1.0, None, ALU.add))
                    do(nc.vector.reciprocal(token_w[:, :, E], s["shared_den"][:, :]))
                    do(nc.vector.tensor_copy(parts[:, :, 0:L], token_w[:, :, :]))
                    do(nc.vector.tensor_tensor(rest1[:, :, :], token_w[:, :, :], parts[:, :, 0:L], ALU.subtract))
                    do(nc.vector.tensor_copy(parts[:, :, S:S + L], rest1[:, :, :]))
                    nc.vector.tensor_tensor(parts[:, :, 2 * S:2 * S + L], rest1[:, :, :], parts[:, :, S:S + L],
                                            ALU.subtract).then_inc(parts_ready, 1)
                    gate_chain.end()

                def chunk(b, k):
                    n = K * b + k
                    dve.wait_ge(silu_ready, n + 1)
                    dve.wait_ge(u_in_psum, n + 1)
                    nc.vector.tensor_tensor(gated[:, k % 2, :], silu[:, k % 2, :], u_psum[:, k % 2, :], ALU.mult)\
                        .then_inc(gated_free, 1)
                    dve.wait_ge(weight_ready, n + 1)
                    dve.wait_ge(gated_free, n + 3)
                    dve.wait_ge(h_free, n + 1)
                    nc.vector.tensor_tensor(h[:, k % 2, :], gated[:, k % 2, :], weight[:, k % 2, :], ALU.mult)\
                        .then_inc(h_ready, 1)

                def add_residual(b, par):
                    dve.wait_ge(out_in_psum, b + 1)
                    dve.wait_ge(st.x_out_free[par], 8 * (b - par) + 16)
                    nc.vector.scalar_tensor_tensor(out=st.x_out[:, par].rearrange("p j d -> p (j d)"),
                                                   in0=misc[:, :], scalar=0.5,
                                                   in1=st.x_in[:, par].rearrange("p j d -> p (j d)"),
                                                   op0=ALU.mult, op1=ALU.add).then_inc(st.residual_free, 1)

                def body(b, par):
                    for k in range(2, K):
                        chunk(b, k)
                        if k == 2:
                            st.norm_stats(dve, b + 1, 1 - par)
                        if k == 5:
                            exp_inputs(b + 1)
                        if k == 7:
                            token_weights(b + 1)
                    chunk(b + 1, 0)
                    chunk(b + 1, 1)
                    add_residual(b, par)

                dve.sem_inc(gated_free, 2)
                dve.sem_inc(h_free, 2)
                dve.sem_inc(st.residual_free, 1)
                dve.wait_ge(parts_zeroed, 1)
                st.wait_weights(dve)
                st.norm_stats(dve, 0, 0)
                exp_inputs(0)
                token_weights(0)
                chunk(0, 0)
                chunk(0, 1)
                two_batches(dve, st.NB // 2, body)

        st.finish()




class Bank:

    def __init__(self, full, free, lead_in, steps):
        self.full, self.free, self.lead_in, self.steps = full, free, lead_in, steps

    def number(self, b, step):
        return self.lead_in.index(step) if b is None else len(self.lead_in) + len(self.steps) * b + self.steps.index(step)

    def take(self, pe, b, step):
        pe.wait_ge(self.free, self.number(b, step) + 1)

    def filled(self, eng, b, step):
        eng.wait_ge(self.full, self.number(b, step) + 1)

    def emptied_last(self, eng, b):
        eng.wait_ge(self.free, len(self.lead_in) + len(self.steps) * b + 1)

    def emptied(self, eng, b, step):
        eng.wait_ge(self.free, self.number(b, step) + 2)


def attention_stage(nc, name, src, dst, consts, w, scratch):
    H = 16
    DH = 8
    maps = 2
    VD = 16
    WD = H * VD
    CW = WD // P
    G = maps * H // 4
    TERMS = 6
    HALF = TERMS * DH
    ROWS = 2 * HALF
    SCALE = float(1.0 / np.sqrt(DH))
    VP = 32
    width = lambda qt: (qt + 1) * P
    start_q = lambda kt: kt * P
    units = []
    for qt in range(J):
        per = {1: 4, 2: 2}.get(qt + 1, 1)
        units += [(qt, list(range(i, i + per)), T // per) for i in range(0, 4, per)]
    NU = len(units)
    LEAD = (7 * NU) // 4
    quota = lambda s: -(-NU * (s + 1) // 4) + LEAD
    tensors = [(c, q) for c in range(maps) for q in ("q", "k")]

    steps_at, mid_at = {}, {}
    for g in range(1, G + 1):
        mid_at[g, 1] = [("maxima", g + 1)]
        steps_at[g, 1] = [("heads", g - 1)]
    def at(g, kt, *steps):
        steps_at.setdefault((g, kt), []).extend(steps)
    at(2, 0, "xT")
    for n, t in enumerate(tensors):
        at(2 + n, 3, ("project", t))
    at(G, 2, ("values", 0))
    at(6, 0, ("concat", 0))
    at(G, 3, ("values", 1), ("concat", 1), "out")
    values_steps = [("values", 0), ("values", 1)]
    prepare = ["xT"] + [("project", t) for t in tensors] + values_steps
    norm_at, load_at = (1, 0), (G, 3)
    slots = [(g, kt) for g in range(1, G + 1) for kt in range(J)]
    steps = [s for slot in slots for s in mid_at.get(slot, []) + steps_at.get(slot, [])]
    lead_in = [(x, n) for n in range(2) for x in prepare] + [("maxima", 0), ("maxima", 1)]
    NT = len(tensors)

    with ExitStack() as ctx:
        st = Stage(nc, ctx, name, src, dst, consts)
        sb, ps, sem, misc, xT, NB = st.sb, st.ps, st.sem, st.misc, st.xT, st.NB
        x_res = sb("x_res", [P, 2, J, D], F32)
        w_qk = {t: sb(f"w_{t[1]}{t[0]}", [P, P], F32) for t in tensors}
        w_v = sb("w_v", [P, WD], F32)
        lam_in = sb("lam_in", [P, 4, H, DH], F32)
        lam_prod = sb("lam_prod", [P, 2, H, DH], F32)
        lam_sum = sb("lam_sum", [P, 2, H], F32)
        lam_exp = sb("lam_exp", [P, 2, H], F32)
        lam_diff = sb("lam_diff", [P, H], F32)
        lam = sb("lam", [P, H], F32)
        rms_scale = sb("rms_scale", [P, VD], F32)
        scale02 = sb("scale02", [P, VD], F32)
        map_out = sb("map_out", [P, 2, J, 4 * VD], F32)
        quad = sb("quad", [P, J, 4 * VD], F32)
        quad_sq = sb("quad_sq", [P, J, 4 * VD], F32)
        quad_ms = sb("quad_ms", [P, J * 4], F32)
        quad_mse = sb("quad_mse", [P, J * 4], F32)
        quad_rms = sb("quad_rms", [P, J * 4], F32)
        quad_n = sb("quad_n", [P, J, 4 * VD], F32)
        minus_half16 = sb("minus_half16", [P, J * 4], F32)
        w_o = sb("w_o", [P, CW, D], F32)
        qs = sb("qs", [P, 2, maps, H // 2, 2, T], BF16)
        ks = sb("ks", [P, 2, maps, H // 2, T], BF16)
        parts = sb("parts", [P, 2, 3, T], BF16)
        rest = sb("rest", [P, 2, T], F32)
        va = sb("va", [P, 2, J, H, VP], F32)
        row_max = sb("row_max", [P, 2, J * 4], F32)
        max_rest = sb("max_rest", [P, 2, J * 4], F32)
        max_parts = sb("max_parts", [P, 2, J, 3, 4], BF16)
        maxT = sb("maxT", [12, 2, T], BF16)
        prob = sb("prob", [P, 8, T], F32)
        oT = sb("oT", [P, 2, T], F32)
        inv_sum = sb("inv_sum", [P, J, 4], F32)
        inv_lam = sb("inv_lam", [P, J, 4], F32)
        o_all = sb("o_all", [P, J, WD], F32)
        o_allT = sb("o_allT", [P, CW, T], F32)
        zeros = sb("zeros", [P, J * 4], F32)
        s_psum = ps("s_psum", [P, 2, T], F32)
        sT_psum = ps("sT_psum", [P, 4, T], F32)
        pv_psum = ps("pv_psum", [P, T], F32)
        ident, ident16, causal_q, causal_k = (consts[k] for k in ("ident", "ident16", "causal_q", "causal_k"))
        scratch = nc.dram_tensor(f"{name}_stack", [2, maps, 2, 2, TERMS, DH, H // 2 * T], BF16, kind="Internal").ap()

        setup = sem("setup")
        setup_step = sem("setup_step")
        fixed_rows = sem("fixed_rows")
        res_loaded = [sem(f"res_loaded{i}") for i in range(2)]
        hi_ready = sem("hi_ready")
        mid_ready = sem("mid_ready")
        parts_ready = sem("parts_ready")
        parts_written = [sem(f"parts_written{i}") for i in range(2)]
        stack_loaded = [sem(f"stack_loaded{i}") for i in range(2)]
        s_in_psum = sem("s_in_psum")
        s_free = sem("s_free")
        max_step = sem("max_step")
        max_parts_ready = sem("max_parts_ready")
        max_stored = [sem(f"max_stored{i}") for i in range(2)]
        sT_in_psum = sem("sT_in_psum")
        prob_ready = sem("prob_ready")
        pv_in_psum = sem("pv_in_psum")
        oT_ready = sem("oT_ready")
        post_step = sem("post_step")
        sq_ready = sem("sq_ready")
        mse_ready = sem("mse_ready")
        quad_step = sem("quad_step")
        ms_step = sem("ms_step")
        o_ready = sem("o_ready")
        bank = Bank(sem("misc_full"), sem("misc_free"), lead_in, steps)
        def head_of(g, i):
            c, quad_no = g % maps, g // maps
            return c, 2 * quad_no + i // 2, i % 2

        with nc.Block() as block:

            @block.sync
            def _(sp):
                def write_tensor(count, t, par):
                    c, q = t
                    k = tensors.index(t) % 2
                    sp.wait_ge(parts_ready, count + 1)
                    for g in range(2):
                        rows = parts[g * 64:(g + 1) * 64, k]
                        to = scratch[par, c, 0 if q == "q" else 1, g].rearrange("t d (i n) -> (d i) t n", n=T)
                        for t0, n in ((0, 3), (3, 2), (5, 1)):
                            if q == "q":
                                part = rows[:, 0:n, :]
                            else:
                                part = rows[:, 3 - n:4 - n, :].broadcast_to([64, n, T])
                            sp.dma_start(to[:, t0:t0 + n, :], part).then_inc(parts_written[k], 16)

                def load_stack(par, written):
                    for k in range(2):
                        sp.wait_ge(parts_written[k], written)
                    for c in range(maps):
                        for g in range(2):
                            rows = slice(g * HALF, (g + 1) * HALF)
                            sp.dma_start(qs[rows, par, c, :, g, :],
                                         scratch[par, c, 0, g].rearrange("t d (i n) -> (t d) i n", n=T))\
                                .then_inc(stack_loaded[par], 16)
                            sp.dma_start(ks[rows, par, c, :, :],
                                         scratch[par, c, 1, g].rearrange("t d (i n) -> (t d) i n", n=T))\
                                .then_inc(stack_loaded[par], 16)

                def store_max(b, par, arg):
                    g = arg % G
                    par = par if arg < G else 1 - par
                    c, pair, _ = head_of(g, 0)
                    bank.emptied(sp, b, ("maxima", arg))
                    for s in range(3):
                        to = qs[ROWS + s:ROWS + s + 1, par, c, pair:pair + 2, :, :].rearrange("o a b n -> o (a b) n")
                        sp.dma_start(to, maxT[4 * s:4 * s + 4, g % 2, :]).then_inc(max_stored[g % 2], 16)

                def load_x(b, par, index):
                    sp.dma_start(st.x_in[:, par], src[index].rearrange("(j p) d -> p j d", p=P))\
                        .then_inc(st.x_loaded[par], 16)

                def body(b, par, index=None):
                    for g, kt in slots:
                        if (g, kt) == (1, 0):
                            sp.wait_ge(st.x_hat_ready, b + 2)
                            sp.sem_inc(st.tick, 1)
                            load_x(b + 3, 1 - par, b + 3 if index is None else (index + 3) % NB)
                            bank.emptied_last(sp, b)
                            sp.sem_inc(st.tick, 1)
                            sp.dma_start(x_res[:, par], src[b].rearrange("(j p) d -> p j d", p=P))\
                                .then_inc(res_loaded[par], 16)
                        if kt == 1:
                            store_max(b, par, g + 1)
                        for s in steps_at.get((g, kt), []):
                            if s[0] == "project":
                                write_tensor(NT * (b + 2) + tensors.index(s[1]), s[1], par)
                        if (g, kt) == load_at:
                            sp.wait_ge(sT_in_psum, 16 * G * (b + 1))
                            sp.sem_inc(st.tick, 1)
                            load_stack(par, (NT // 2) * 96 * (b + 3))
                    bank.emptied(sp, b, "out")
                    sp.dma_start(dst[b].rearrange("(j p) d -> p j d", p=P), st.x_out[:, par])\
                        .then_inc(st.x_out_free[par], 16)

                for par in range(2):
                    sp.sem_inc(st.x_out_free[par], 16)
                load_x(0, 0, 0)
                load_x(1, 1, 1)
                for n, t in enumerate(tensors):
                    st.load_weight(sp, w_qk[t][:, :], w[f"W{t[1]}{t[0]}"])
                st.load_weight(sp, w_v[:, :], w["Wv"])
                for n, k in enumerate(("lambda_q1", "lambda_k1", "lambda_q2", "lambda_k2")):
                    st.load_weight(sp, lam_in[:, n], w[k].rearrange("(o h) d -> o h d", o=1).broadcast_to([P, H, DH]))
                st.load_weight(sp, rms_scale[:, :], w["rms_scale"].rearrange("(o h) -> o h", o=1).broadcast_to([P, VD]))
                st.load_weight(sp, w_o[:, :, :], w["Wo"])
                for par in range(2):
                    for c in range(maps):
                        sp.dma_start(ks[ROWS:ROWS + 3, par, c], w["minus_ones"]).then_inc(fixed_rows, 16)
                for n in range(2):
                    for t in tensors:
                        write_tensor(NT * n + tensors.index(t), t, n)
                    if n == 0:
                        sp.wait_ge(st.x_hat_ready, 1)
                        load_x(2, 0, 2)
                    sp.wait_ge(setup, 1)
                    load_stack(n, (NT // 2) * 96 * (n + 1))
                store_max(None, 0, 0)
                store_max(None, 0, 1)
                turns = NB // 2 - 2
                if turns > 0:
                    two_batches(sp, turns, body)
                for b in range(2 * max(turns, 0), NB):
                    body(b, b % 2, b)
                for par in range(2):
                    sp.wait_ge(st.x_out_free[par], 16 + 8 * NB)
                    sp.wait_ge(stack_loaded[par], 64 * maps * (NB // 2 + 1))
                sp.wait_ge(st.x_loaded[0], 16 * (NB // 2 + 2))
                sp.wait_ge(st.x_loaded[1], 16 * (NB // 2 + 1))
                for par in range(2):
                    sp.wait_ge(max_stored[par], 48 * (NB * G // 2 + 1))

            @block.gpsimd
            def _(pool):
                tt = nc.gpsimd.tensor_tensor
                maxc = Chain(pool, max_step, 3)

                def split_max(gg, g, last_unit):
                    k = g % 2
                    m, r = row_max[:, k], max_rest[:, k]
                    part = lambda i: max_parts[:, k, :, i, :]
                    pool.wait_ge(s_free, last_unit + 3)
                    maxc.start(gg)
                    v = lambda x: x.rearrange("p (j h) -> p j h", j=J)
                    maxc.after(tt(part(0), v(m), v(zeros[:, :]), ALU.add))
                    maxc.after(tt(v(r), v(m), part(0), ALU.subtract))
                    maxc.after(tt(part(1), v(r), v(zeros[:, :]), ALU.add))
                    tt(part(2), v(r), part(1), ALU.subtract).then_inc(max_parts_ready, 1)
                    maxc.end()

                def split_tensor(count, t, key):
                    k = tensors.index(t) % 2
                    pool.wait_ge(mid_ready, count + 1)
                    tt(parts[:, k, 2], rest[:, k], parts[:, k, 1], ALU.subtract).then_inc(parts_ready, 1)

                def norm(b2, par):
                    st.norm_apply(pool, b2, par)

                def combine(qn, b, g):
                    bank.emptied(pool, b, ("heads", g))
                    tt(quad[:, :, :], map_out[:, 0], map_out[:, 1], ALU.subtract).then_inc(quad_step, 1)
                    pool.wait_ge(quad_step, 3 * qn + 1)
                    tt(quad_sq[:, :, :], quad[:, :, :], quad[:, :, :], ALU.mult).then_inc(sq_ready, 1)

                def rms(qn, quad_no):
                    pool.wait_ge(mse_ready, qn + 1)
                    tt(quad_rms[:, :], quad_mse[:, :], minus_half16[:, :], ALU.pow).then_inc(quad_step, 1)
                    pool.wait_ge(quad_step, 3 * qn + 2)
                    tt(quad_n[:, :, :].rearrange("p j (h d) -> p (j h) d", d=VD),
                       quad[:, :, :].rearrange("p j (h d) -> p (j h) d", d=VD), along(quad_rms[:, :], VD), ALU.mult)\
                        .then_inc(quad_step, 1)
                    pool.wait_ge(quad_step, 3 * qn + 3)
                    w4 = 4 * VD
                    heads = lambda x: x.rearrange("p j (h d) -> p j h d", d=VD)
                    scale = scale02[:, :].rearrange("p (a b d) -> p a b d", a=1, b=1).broadcast_to([P, J, 4, VD])
                    tt(heads(o_all[:, :, quad_no * w4:(quad_no + 1) * w4]), heads(quad_n[:, :, :]), scale, ALU.mult)\
                        .then_inc(o_ready, 1)

                def body(b, par):
                    for g, kt in slots:
                        if (g, kt) == norm_at:
                            norm(b + 2, par)
                        if kt == 1:
                            gg = G * b + g + 1
                            split_max(gg, g + 1, NU * (gg + 1) - 1)
                        if kt == 2 and g % 2 == 0:
                            combine((G // 2) * b + g // 2 - 1, b, g - 1)
                        if kt == 3 and g % 2 == 0:
                            rms((G // 2) * b + g // 2 - 1, g // 2 - 1)
                        for s in steps_at.get((g, kt), []):
                            if s[0] == "project":
                                split_tensor(NT * (b + 2) + tensors.index(s[1]), s[1], (b, s))

                nc.gpsimd.memset(qs[:, :, :, :, :, :].rearrange("p a b c d e -> p (a b c d e)").bitcast(F32), 0.0)
                nc.gpsimd.memset(zeros[:, :], 0.0)
                nc.gpsimd.memset(minus_half16[:, :], -0.5)
                nc.gpsimd.memset(va[:, :, :, :, :], 0.0).then_inc(setup, 1)
                pool.wait_ge(setup, 1)
                nc.gpsimd.memset(va[:, :, :, :, VD:VD + 1].rearrange("p a j h o -> p (a j h) o"), 1.0).then_inc(setup, 1)
                st.wait_weights(pool)
                pool.wait_ge(setup_step, 6)
                for n in range(2):
                    norm(n, n)
                    for t in tensors:
                        split_tensor(NT * n + tensors.index(t), t, (None, (("project", t), n)))
                split_max(0, 0, NU - 1)
                split_max(1, 1, 2 * NU - 1)
                two_batches(pool, NB // 2, body)

            @block.tensor
            def _(pe):
                mm = nc.tensor.matmul

                def max_unit(n, u, b_of, par, g):
                    qt, heads, pitch = units[u % NU]
                    W = width(qt)
                    if u % (NU * G) == 0:
                        pe.wait_ge(stack_loaded[par], 64 * maps * (b_of // 2 + 1) if isinstance(b_of, int)
                                   else 32 * maps * (b_of - par) + 64 * maps)
                    pe.wait_ge(s_free, n + 1)
                    pe.sem_inc(st.tick, 1)
                    for k, i in enumerate(heads):
                        c, pair, hp = head_of(g, i)
                        out = s_psum[:, u % 2, k * pitch:k * pitch + W]
                        last = mm(out, qs[0:ROWS, par, c, pair, hp, qt * P:(qt + 1) * P], ks[0:ROWS, par, c, pair, 0:W],
                                  start=True, stop=True)
                        last = mm(out[:, W - P:W], ident16[:, :], causal_q[:, :], start=False, stop=True,
                                  skip_group_check=True)
                    last.then_inc(s_in_psum, 1)

                def score(n, par, g, kt, i, first=False):
                    c, pair, hp = head_of(g, i)
                    q0 = start_q(kt)
                    if not first:
                        pe.wait_ge(prob_ready, n - 3)
                        pe.sem_inc(st.tick, 1)
                    out = sT_psum[:, i, q0:T]
                    last = mm(out, ks[0:ROWS + 3, par, c, pair, kt * P:(kt + 1) * P], qs[0:ROWS + 3, par, c, pair, hp, q0:T],
                              start=True, stop=True)
                    last = mm(out[:, 0:P], ident16[:, :], causal_k[:, :], start=False, stop=True,
                              skip_group_check=True)
                    last.then_inc(sT_in_psum, 1)

                def pv(gg, par, g, kt, first=False):
                    q0 = start_q(kt)
                    pe.wait_ge(prob_ready, 16 * gg + 4 * kt + 4)
                    if kt == 0 and not first:
                        pe.wait_ge(oT_ready, gg)
                    for i in range(4):
                        c, pair, hp = head_of(g, i)
                        last = mm(pv_psum[32 * i:32 * i + 32, q0:T], va[:, par, kt, 2 * pair + hp, :],
                                  prob[:, (4 * kt + i) % 8, q0:T], start=(kt == 0), stop=(kt == J - 1),
                                  skip_group_check=True)
                    if kt == J - 1:
                        last.then_inc(pv_in_psum, 1)

                def step(b, s, n=None, par=None, prep_par=None):
                    name_, arg = s if isinstance(s, tuple) else (s, None)
                    key = s if b is not None else ((s, n) if name_ != "maxima" else s)
                    bank.take(pe, b, key)
                    nb = (b + 2) if b is not None else n
                    pp = prep_par
                    if name_ == "xT":
                        pe.wait_ge(st.x_hat_ready, nb + 1)
                        for j in range(J):
                            last = nc.tensor.transpose(misc[:, j * P:(j + 1) * P], st.x_hat[:, j, :], ident[:, :])
                    elif name_ == "project":
                        last = mm(misc[:, :], w_qk[arg][:, :], xT[:, pp], start=True, stop=True)
                    elif name_ == "values":
                        for j in range(2):
                            tile = slice((2 * arg + j) * P, (2 * arg + j + 1) * P)
                            last = mm(misc[:, j * WD:(j + 1) * WD], xT[:, pp, tile], w_v[:, :], start=True, stop=True)
                    elif name_ == "maxima":
                        gg = arg if b is None else G * b + arg
                        pe.wait_ge(max_parts_ready, gg + 1)
                        for j in range(J):
                            last = nc.tensor.transpose(misc[0:12, j * P // 2:(j + 1) * P // 2].bitcast(BF16),
                                                       max_parts[:, arg % 2, j].rearrange("p s h -> p (s h)"), ident16[:, :])
                    elif name_ == "heads":
                        pe.wait_ge(oT_ready, G * b + arg + 1)
                        for j in range(J):
                            last = nc.tensor.transpose(misc[:, j * P:(j + 1) * P], oT[:, arg % 2, j * P:(j + 1) * P], ident[:, :])
                    elif name_ == "concat":
                        pe.wait_ge(o_ready, 4 * b + 2 * (arg + 1))
                        for j in range(J):
                            last = nc.tensor.transpose(misc[:, j * P:(j + 1) * P], o_all[:, j, arg * P:(arg + 1) * P], ident[:, :])
                    elif name_ == "out":
                        for j in range(J):
                            for k in range(CW):
                                last = mm(misc[:, j * P:(j + 1) * P], o_allT[:, k, j * P:(j + 1) * P], w_o[:, k, :],
                                          start=(k == 0), stop=(k == CW - 1))
                    last.then_inc(bank.full, 1)

                def slot(b, par, s, g, kt, todo, first=False):
                    own, gm = (par, g) if g < G else (1 - par, 0)
                    n = 16 * G * b + 4 * s
                    if kt == 0:
                        pe.wait_ge(max_stored[g % 2], 24 * G * b + 48 * (g // 2 + 1))
                    for i in range(4):
                        score(n + i, own, gm, kt, i, first=first and kt == 0)
                        take = todo[i * len(todo) // 4:(i + 1) * len(todo) // 4]
                        for u in take:
                            over_b, ug = divmod(u // NU, G)
                            max_unit(NU * G * b + u, u, b + over_b, par if over_b % 2 == 0 else 1 - par, ug)

                def body(b, par):
                    for s, (g, kt) in enumerate(slots, start=4):
                        slot(b, par, s, g, kt, list(range(quota(s - 1), quota(s))))
                        for x in mid_at.get((g, kt), []):
                            step(b, x, par=par, prep_par=par)
                        if kt == 0:
                            pv(G * b + g - 1, par, g - 1, J - 1)
                        else:
                            pv(G * b + g, par if g < G else 1 - par, g % G, kt - 1)
                        for x in steps_at.get((g, kt), []):
                            step(b, x, par=par, prep_par=par)

                st.wait_weights(pe)
                pe.wait_ge(fixed_rows, 32 * maps)
                pe.wait_ge(setup, 2)
                for n in range(2):
                    for x in prepare:
                        step(None, x, n=n, prep_par=n)
                for u in range(LEAD):
                    if u == NU:
                        step(None, ("maxima", 0))
                    max_unit(u, u, 0, 0, u // NU)
                extra = list(range(LEAD, quota(3)))
                for u in extra:
                    max_unit(u, u, 0, 0, u // NU)
                step(None, ("maxima", 1))
                for kt in range(J):
                    slot(0, 0, kt, 0, kt, [], first=True)
                    if kt > 0:
                        pv(0, 0, 0, kt - 1, first=True)
                two_batches(pe, NB // 2, body)

            @block.scalar
            def _(act):
                def exps(n, kt):
                    q0 = start_q(kt)
                    for i in range(4):
                        act.wait_ge(sT_in_psum, n + i + 1)
                        nc.scalar.activation(prob[:, (4 * kt + i) % 8, q0:T], sT_psum[:, i, q0:T], ACT.Exp, scale=SCALE)\
                            .then_inc(prob_ready, 1)

                def copy_heads(gg, g):
                    act.wait_ge(pv_in_psum, gg + 1)
                    nc.scalar.activation(oT[:, g % 2], pv_psum[:, :], ACT.Copy).then_inc(oT_ready, 1)

                def hi_mid(count, t, key):
                    k = tensors.index(t) % 2
                    bank.emptied(act, *key)
                    nc.scalar.activation(parts[:, k, 1], rest[:, k], ACT.Copy).then_inc(mid_ready, 1)

                def step(b, s, n=None, pp=None):
                    name_, arg = s if isinstance(s, tuple) else (s, None)
                    key = s if b is not None else ((s, n) if name_ != "maxima" else s)
                    if name_ == "xT":
                        bank.filled(act, b, key)
                        nc.scalar.activation(xT[:, pp], misc[:, :], ACT.Copy).then_inc(bank.free, 1)
                    elif name_ == "project":
                        k = tensors.index(arg) % 2
                        count = NT * (b + 2 if b is not None else n) + tensors.index(arg)
                        bank.filled(act, b, key)
                        if b is not None or n > 0 or tensors.index(arg) >= 2:
                            act.wait_ge(parts_written[k], 96 * (count // 2) if isinstance(count, int)
                                        else 96 * ((NT // 2) * (b + 2) + tensors.index(arg) // 2))
                        nc.scalar.activation(parts[:, k, 0], misc[:, :], ACT.Copy).then_inc(hi_ready, 1)
                        hi_mid(count, arg, (b, key))
                    elif name_ == "values":
                        bank.filled(act, b, key)
                        for j in range(2):
                            last = nc.scalar.activation(va[:, pp, 2 * arg + j, :, 0:VD],
                                                        misc[:, j * WD:(j + 1) * WD].rearrange("p (h d) -> p h d", d=VD), ACT.Copy)
                        last.then_inc(bank.free, 1)
                    elif name_ == "maxima":
                        bank.filled(act, b, key)
                        nc.scalar.activation(maxT[:, arg % 2, :], misc[0:12, 0:T // 2].bitcast(BF16), ACT.Copy)\
                            .then_inc(bank.free, 1)
                    elif name_ == "concat":
                        bank.filled(act, b, key)
                        nc.scalar.activation(o_allT[:, arg], misc[:, :], ACT.Copy).then_inc(bank.free, 1)

                def body(b, par):
                    for s, (g, kt) in enumerate(slots, start=4):
                        exps(16 * G * b + 4 * s, kt)
                        if kt == 0:
                            copy_heads(G * b + g - 1, g - 1)
                        for x in mid_at.get((g, kt), []) + steps_at.get((g, kt), []):
                            step(b, x, pp=par)

                st.wait_weights(act)
                act.wait_ge(setup_step, 2)
                nc.scalar.activation(lam_exp[:, :, :], lam_sum[:, :, :], ACT.Exp).then_inc(setup_step, 1)
                for n in range(2):
                    for x in prepare:
                        step(None, x, n=n, pp=n)
                step(None, ("maxima", 0))
                step(None, ("maxima", 1))
                for kt in range(J):
                    exps(4 * kt, kt)
                two_batches(act, NB // 2, body)

            @block.vector
            def _(dve):
                post = Chain(dve, post_step, 1)

                def unit(n, u):
                    qt, heads, pitch = units[u % NU]
                    g = (u // NU) % G
                    dve.wait_ge(s_in_psum, n + 1)
                    scores = s_psum[:, u % 2, :].rearrange("p (k w) -> p k w", w=pitch)[:, :, 0:width(qt)]
                    nc.vector.tensor_reduce(row_max[:, g % 2, 4 * qt + heads[0]:4 * qt + heads[-1] + 1], scores, AX.X, ALU.max)\
                        .then_inc(s_free, 1)

                def step(b, s, n=None, pp=None):
                    name_, arg = s if isinstance(s, tuple) else (s, None)
                    key = s if b is not None else ((s, n) if name_ != "maxima" else s)
                    nb = b + 2 if b is not None else n
                    if name_ == "project":
                        k = tensors.index(arg) % 2
                        bank.filled(dve, b, key)
                        dve.wait_ge(hi_ready, NT * nb + tensors.index(arg) + 1)
                        nc.vector.tensor_tensor(rest[:, k], misc[:, :], parts[:, k, 0], ALU.subtract).then_inc(bank.free, 1)
                    elif name_ == "heads":
                        c, quad_no = arg % maps, arg // maps
                        bank.filled(dve, b, key)
                        o = misc[:, :].rearrange("p (j h v) -> p j h v", h=4, v=VP)
                        post.start(post_no(b, arg))
                        post.after(nc.vector.reciprocal(inv_sum[:, :, :], o[:, :, :, VD]))
                        inv = inv_sum
                        if c == 1:
                            post.after(nc.vector.tensor_tensor(inv_lam[:, :, :], inv_sum[:, :, :],
                                                               over(lam[:, 4 * quad_no:4 * quad_no + 4], J), ALU.mult))
                            inv = inv_lam
                        to = map_out[:, c]
                        inv = inv[:, :, :].rearrange("p j (h o) -> p j h o", o=1).broadcast_to([P, J, 4, VD])
                        nc.vector.tensor_tensor(to.rearrange("p j (h d) -> p j h d", d=VD), o[:, :, :, 0:VD], inv, ALU.mult)\
                            .then_inc(bank.free, 1)
                    elif name_ == "out":
                        bank.filled(dve, b, key)
                        dve.wait_ge(res_loaded[pp], 8 * (b - pp) + 16)
                        dve.wait_ge(st.x_out_free[pp], 8 * (b - pp) + 16)
                        nc.vector.tensor_tensor(st.x_out[:, pp].rearrange("p j d -> p (j d)"), misc[:, :],
                                                x_res[:, pp].rearrange("p j d -> p (j d)"), ALU.add).then_inc(bank.free, 1)

                def post_no(b, g):
                    post.per = 1
                    return 3 * (G // 2) * b + 3 * (g // 2) + g % 2

                def mean_square(qn):
                    dve.wait_ge(sq_ready, qn + 1)
                    nc.vector.tensor_reduce(quad_ms[:, :], quad_sq[:, :, :].rearrange("p j (h d) -> p (j h) d", d=VD), AX.X,
                                            ALU.add).then_inc(ms_step, 1)
                    dve.wait_ge(ms_step, qn + 1)
                    nc.vector.tensor_scalar(quad_mse[:, :], quad_ms[:, :], 1.0 / VD, EPS, ALU.mult, ALU.add)\
                        .then_inc(mse_ready, 1)

                def body(b, par):
                    for s, (g, kt) in enumerate(slots, start=4):
                        if (g, kt) == norm_at:
                            st.norm_stats(dve, b + 2, par)
                        for u in range(quota(s - 1), quota(s)):
                            unit(NU * G * b + u, u)
                        if kt == 2 and g % 2 == 0:
                            mean_square((G // 2) * b + g // 2 - 1)
                        for x in steps_at.get((g, kt), []):
                            step(b, x, pp=par)

                dve.sem_inc(s_free, 2)
                dve.sem_inc(bank.free, 1)
                st.wait_weights(dve)
                nc.vector.tensor_tensor(lam_prod[:, :, :, :], lam_in[:, 0:4:2], lam_in[:, 1:4:2], ALU.mult)\
                    .then_inc(setup_step, 1)
                dve.wait_ge(setup_step, 1)
                nc.vector.tensor_reduce(lam_sum[:, :, :], lam_prod[:, :, :, :], AX.X, ALU.add).then_inc(setup_step, 1)
                dve.wait_ge(setup_step, 3)
                nc.vector.tensor_tensor(lam_diff[:, :], lam_exp[:, 0], lam_exp[:, 1], ALU.subtract).then_inc(setup_step, 1)
                dve.wait_ge(setup_step, 4)
                nc.vector.tensor_scalar(lam[:, :], lam_diff[:, :], LAMBDA_INIT, None, ALU.add).then_inc(setup_step, 1)
                nc.vector.tensor_scalar(scale02[:, :], rms_scale[:, :], 1.0 - LAMBDA_INIT, None, ALU.mult)\
                    .then_inc(setup_step, 1)
                for n in range(2):
                    st.norm_stats(dve, n, n)
                    for x in prepare:
                        step(None, x, n=n, pp=n)
                for u in range(quota(3)):
                    unit(u, u)
                two_batches(dve, NB // 2, body)

        st.finish()




def head_mixing_stage(nc, name, src, dst, consts, w, scratch):
    H, DH = 16, 8
    W = H * DH
    SCALE = float(1.0 / np.sqrt(DH))
    R = 32
    QW, KW = 2 * W, 3 * W
    with ExitStack() as ctx:
        st = Stage(nc, ctx, name, src, dst, consts)
        sb, ps, sem, misc, xT, NB = st.sb, st.ps, st.sem, st.misc, st.xT, st.NB
        w_q = sb("w_q", [P, QW], F32)
        w_kv = sb("w_kv", [R, KW], F32)
        w_down = sb("w_down", [P, R], F32)
        w_o = sb("w_o", [P, D], F32)
        b_qkv = sb("b_qkv", [P, QW + KW], F32)
        b_down = sb("b_down", [R, 1], F32)
        b_out = sb("b_out", [P, D], F32)
        rope = sb("rope", [P, J, 4 * W], F32)
        latent = sb("latent", [R, 2, T], F32)
        raw = sb("raw", [P, 2, QW + KW], F32)
        turned = sb("turned", [P, 2, 4 * W], F32)
        rotated = sb("rotated", [P, 2, 2 * W], F32)
        products = sb("products", [P, H * H * DH], F32)
        scores = sb("scores", [P, H, H], F32)
        top = sb("top", [P, H], F32)
        lowered = sb("lowered", [P, 2, H * H], F32)
        prob = sb("prob", [P, 2, H * H], F32)
        weighted = sb("weighted", [P, 2, H * DH * H], F32)
        total = sb("total", [P, H], F32)
        inv_total = sb("inv_total", [P, H], F32)
        mixed = sb("mixed", [P, W], F32)
        heads_out = sb("heads_out", [P, 2, W], F32)
        headsT = sb("headsT", [P, 2, P], F32)
        biased = sb("biased", [P, D], F32)
        q_psum = ps("q_psum", [P, 2, T], F32)
        kv_psum = ps("kv_psum", [P, 2, T], F32)
        latent_psum = ps("latent_psum", [P, T], F32)
        headsT_psum = ps("headsT_psum", [P, T], F32)
        out_psum = ps("out_psum", [P, T], F32)
        ident = consts["ident"]

        latent_in_psum = sem("latent_in_psum")
        latent_ready = sem("latent_ready")
        projected = sem("projected")
        raw_ready = sem("raw_ready")
        turned_ready = sem("turned_ready")
        rotated_ready = sem("rotated_ready")
        score_step = sem("score_step")
        lowered_ready = sem("lowered_ready")
        prob_ready = sem("prob_ready")
        weighted_ready = sem("weighted_ready")
        mix_step = sem("mix_step")
        heads_ready = sem("heads_ready")
        headsT_in_psum = sem("headsT_in_psum")
        headsT_ready = sem("headsT_ready")
        out_in_psum = sem("out_in_psum")
        out_free = sem("out_free")
        residual_step = sem("residual_step")

        with nc.Block() as block:

            @block.sync
            def _(sp):
                st.load_x(sp, 0, 0)
                for to, k in ((w_q[:, :], "Wq"), (w_kv[:, :], "Wkv"), (w_down[:, :], "Wdown"), (w_o[:, :], "Wo"),
                              (b_down[:, :], "bdown"), (rope[:, :, :], "rope")):
                    st.load_weight(sp, to, w[k])
                st.load_weight(sp, b_qkv[:, :], w["bqkv"].rearrange("(o h) -> o h", o=1).broadcast_to([P, QW + KW]))
                st.load_weight(sp, b_out[:, :], w["bout"].rearrange("(o h) -> o h", o=1).broadcast_to([P, D]))
                st.load_x(sp, 1, 1)
                st.stream(sp)

            @block.gpsimd
            def _(pool):
                tt = nc.gpsimd.tensor_tensor

                def rotate(n, k, j):
                    pool.wait_ge(raw_ready, n + 3)
                    tt(turned[:, k], raw[:, k, 0:4 * W], rope[:, j, :], ALU.mult).then_inc(turned_ready, 1)
                    pool.wait_ge(turned_ready, n + 1)
                    halves = turned[:, k].rearrange("p (x y w) -> p x y w", x=2, y=2)
                    tt(rotated[:, k].rearrange("p (x w) -> p x w", x=2), halves[:, :, 0, :], halves[:, :, 1, :], ALU.add)\
                        .then_inc(rotated_ready, 1)

                def weigh(n, k):
                    pool.wait_ge(prob_ready, n + 1)
                    p_ = prob[:, k].rearrange("p (h o g) -> p h o g", h=H, o=1).broadcast_to([P, H, DH, H])
                    v_ = raw[:, k, 4 * W:5 * W].rearrange("p (o g d) -> p o d g", o=1, d=DH).broadcast_to([P, H, DH, H])
                    tt(weighted[:, k].rearrange("p (h d g) -> p h d g", h=H, d=DH), p_, v_, ALU.mult)\
                        .then_inc(weighted_ready, 1)

                def body(b, par):
                    for j in range(J):
                        if j == 0:
                            st.norm_apply(pool, b + 1, 1 - par)
                        n = 4 * b + j
                        rotate(n + 3, (j + 3) % 2, (j + 3) % J)
                        weigh(n + 2, j % 2)

                st.wait_weights(pool)
                st.norm_apply(pool, 0, 0)
                for n in range(3):
                    rotate(n, n % 2, n)
                    if n > 0:
                        weigh(n - 1, (n - 1) % 2)
                two_batches(pool, NB // 2, body)

            @block.tensor
            def _(pe):
                mm = nc.tensor.matmul

                def project(n, k, b, par, j):
                    own = slice(j * P, (j + 1) * P)
                    if j == 0:
                        pe.wait_ge(st.xT_ready, b + 1)
                        mm(latent_psum[0:R, :], w_down[:, :], xT[:, par], start=True, stop=True).then_inc(latent_in_psum, 1)
                        pe.wait_ge(latent_ready, b + 1)
                    pe.wait_ge(raw_ready, n + 1)
                    mm(q_psum[:, k, 0:QW], xT[:, par, own], w_q[:, :], start=True, stop=True)
                    mm(kv_psum[:, k, 0:KW], latent[:, par, own], w_kv[:, :], start=True, stop=True).then_inc(projected, 1)

                def finish(n, k):
                    pe.wait_ge(heads_ready, n + 1)
                    nc.tensor.transpose(headsT_psum[:, 0:P], heads_out[:, k, :], ident[:, :]).then_inc(headsT_in_psum, 1)
                    pe.wait_ge(headsT_ready, n + 1)
                    pe.wait_ge(out_free, n + 1)
                    mm(out_psum[:, 0:D], headsT[:, k, :], w_o[:, :], start=True, stop=True).then_inc(out_in_psum, 1)

                def body(b, par):
                    for j in range(J):
                        n = 4 * b + j
                        finish(n, j % 2)
                        if j == 0:
                            project(n + 3, 1, b, par, 3)
                            st.norm_transpose(pe, b + 1)
                        else:
                            project(n + 3, (j + 3) % 2, b + 1, 1 - par, j - 1)

                st.wait_weights(pe)
                st.norm_transpose(pe, 0, first=True)
                for n in range(3):
                    project(n, n % 2, 0, 0, n)
                two_batches(pe, NB // 2, body)

            @block.scalar
            def _(act):
                def exps(n, k):
                    act.wait_ge(lowered_ready, n + 1)
                    nc.scalar.activation(prob[:, k], lowered[:, k], ACT.Exp, scale=SCALE).then_inc(prob_ready, 1)

                def store_latent(b, par):
                    act.wait_ge(latent_in_psum, b + 1)
                    nc.scalar.activation(latent[:, par], latent_psum[0:R, :], ACT.Identity, bias=b_down[:, 0:1])\
                        .then_inc(latent_ready, 1)

                def store_heads(n, k):
                    act.wait_ge(headsT_in_psum, n + 1)
                    nc.scalar.activation(headsT[:, k, :], headsT_psum[:, 0:P], ACT.Copy).then_inc(headsT_ready, 1)

                def body(b, par):
                    for j in range(J):
                        n = 4 * b + j
                        store_heads(n, j % 2)
                        if j == 0:
                            st.norm_store(act, b + 1, 1 - par)
                        if j == 1:
                            store_latent(b + 1, 1 - par)
                        exps(n + 2, j % 2)

                st.wait_weights(act)
                st.norm_store(act, 0, 0)
                store_latent(0, 0)
                exps(0, 0)
                exps(1, 1)
                two_batches(act, NB // 2, body)

            @block.vector
            def _(dve):
                score = Chain(dve, score_step, 3)
                mix = Chain(dve, mix_step, 3)

                def add_bias(n, k):
                    dve.wait_ge(projected, n + 1)
                    nc.vector.tensor_tensor(raw[:, k, 0:QW], q_psum[:, k, 0:QW], b_qkv[:, 0:QW], ALU.add)
                    nc.vector.tensor_tensor(raw[:, k, QW:QW + KW], kv_psum[:, k, 0:KW], b_qkv[:, QW:QW + KW], ALU.add)\
                        .then_inc(raw_ready, 1)

                def compare(n, k):
                    dve.wait_ge(rotated_ready, n + 1)
                    score.start(n)
                    q = rotated[:, k, 0:W].rearrange("p (h o d) -> p h o d", h=H, o=1).broadcast_to([P, H, H, DH])
                    key = rotated[:, k, W:2 * W].rearrange("p (o g d) -> p o g d", o=1, d=DH).broadcast_to([P, H, H, DH])
                    score.after(nc.vector.tensor_tensor(products[:, :].rearrange("p (h g d) -> p h g d", h=H, g=H), q, key,
                                                        ALU.mult))
                    score.after(nc.vector.tensor_reduce(scores[:, :, :].rearrange("p h g -> p (h g)"),
                                                        products[:, :].rearrange("p (x d) -> p x d", d=DH), AX.X, ALU.add))
                    score.after(nc.vector.tensor_reduce(top[:, :], scores[:, :, :], AX.X, ALU.max))
                    nc.vector.tensor_tensor(lowered[:, k].rearrange("p (h g) -> p h g", h=H), scores[:, :, :],
                                            along(top[:, :], H), ALU.subtract).then_inc(lowered_ready, 1)
                    score.end()

                def add_up(n, k):
                    dve.wait_ge(weighted_ready, n + 1)
                    mix.start(n)
                    mix.mark(nc.vector.tensor_reduce(total[:, :], prob[:, k].rearrange("p (h g) -> p h g", h=H), AX.X, ALU.add))
                    mix.after(nc.vector.tensor_reduce(mixed[:, :], weighted[:, k].rearrange("p (x g) -> p x g", g=H), AX.X,
                                                      ALU.add))
                    mix.after(nc.vector.reciprocal(inv_total[:, :], total[:, :]))
                    nc.vector.tensor_tensor(heads_out[:, k].rearrange("p (h d) -> p h d", d=DH),
                                            mixed[:, :].rearrange("p (h d) -> p h d", d=DH), along(inv_total[:, :], DH),
                                            ALU.mult).then_inc(heads_ready, 1)
                    mix.end()

                def add_residual(b, par, j):
                    n = 4 * b + j
                    dve.wait_ge(out_in_psum, n + 1)
                    nc.vector.tensor_tensor(biased[:, :], out_psum[:, 0:D], b_out[:, :], ALU.add).then_inc(out_free, 1)
                    if j == 0:
                        dve.wait_ge(st.x_out_free[par], 8 * (b - par) + 16)
                    dve.wait_ge(out_free, n + 2)
                    nc.vector.tensor_tensor(st.x_out[:, par, j, :], biased[:, :], st.x_in[:, par, j, :], ALU.add)\
                        .then_inc(st.residual_free if j == J - 1 else residual_step, 1)

                def body(b, par):
                    for j in range(J):
                        n = 4 * b + j
                        if j == 0:
                            st.norm_stats(dve, b + 1, 1 - par)
                        compare(n + 2, j % 2)
                        dve.wait_ge(weighted_ready, n + 2)
                        add_bias(n + 3, (j + 3) % 2)
                        add_up(n + 1, (j + 1) % 2)
                        add_residual(b, par, j)

                dve.sem_inc(raw_ready, 2)
                dve.sem_inc(out_free, 1)
                dve.sem_inc(st.residual_free, 1)
                st.wait_weights(dve)
                st.norm_stats(dve, 0, 0)
                add_bias(0, 0)
                add_bias(1, 1)
                compare(0, 0)
                compare(1, 1)
                dve.wait_ge(weighted_ready, 1)
                add_bias(2, 0)
                add_up(0, 0)
                two_batches(dve, NB // 2, body)

        st.finish()


def build(nc, t, out, stages):
    NB = t["X"].shape[0]
    with ExitStack() as ctx:
        def const(name, shape, dt):
            return ctx.enter_context(nc.sbuf_tensor(name, shape, dt))

        consts = {
            "eps": const("eps", [P, J], F32),
            "minus_half": const("minus_half", [P, J], F32),
            "ident": const("ident", [P, P], F32),
            "ident16": const("ident16", [P, P], BF16),
            "rank": const("rank", [P, 16], F32),
            "causal_q": const("causal_q", [P, P], BF16),
            "causal_k": const("causal_k", [P, P], BF16),
            "spread": const("spread", [96, 10, P], BF16),
            "starts": const("starts", [P, 32], F32),
            "earlier": const("earlier", [P, P], BF16),
            "ones": const("ones", [P, P], BF16),
            "zeros": const("zeros", [P, D], F32),
        }
        loaded = ctx.enter_context(nc.semaphore("consts_loaded"))
        zeroed = ctx.enter_context(nc.semaphore("zeroed"))
        BLOCKS = NB * T // P + 8 * ROWS // P
        scratch = [nc.dram_tensor(n, [BLOCKS * P, D], F32, kind="Internal").ap() for n in ("sorted_x", "sorted_y")]
        with nc.Block() as block:
            @block.gpsimd
            def _(pool):
                nc.gpsimd.memset(consts["zeros"][:, :], 0.0).then_inc(zeroed, 1)
                nc.gpsimd.memset(consts["eps"][:, :], EPS)
                nc.gpsimd.memset(consts["minus_half"][:, :], -0.5)

            @block.sync
            def _(sp):
                for name in ("ident", "ident16", "rank", "starts", "earlier", "ones", "spread", "causal_q", "causal_k"):
                    sp.dma_start(consts[name][:], t["c_" + name]).then_inc(loaded, 16)
                sp.wait_ge(zeroed, 1)
                sp.dma_start(scratch[0].rearrange("(n p) d -> p n d", p=P),
                             over(consts["zeros"][:, :], BLOCKS)).then_inc(loaded, 16)
                sp.wait_ge(loaded, 16 * 10)
        x = t["X"]
        for n, (kind, pre) in enumerate(stages):
            last = n == len(stages) - 1
            y = out if last else nc.dram_tensor(f"x_after_{n}", [NB, T, D], F32, kind="Internal").ap()
            w = {k[len(pre):]: v for k, v in t.items() if k.startswith(pre)}
            kind(nc, f"s{n}", x, y, consts, w, scratch)
            x = y


def lay_out(inputs):
    bf16 = mybir.dt.np(BF16)
    a = {k: np.ascontiguousarray(v) for k, v in inputs.items()}
    t = {k: v for k, v in a.items() if k != "L0_attn_X"}
    t["X"] = a["L0_attn_X"]
    t["L0_ffn_gate_w"] = np.ascontiguousarray(a["L0_ffn_gate_w"].T)
    t["L0_ffn_b1"] = np.ascontiguousarray(a["L0_ffn_b1"].reshape(8, -1, P).transpose(2, 0, 1))
    t["L0_ffn_b2"] = np.ascontiguousarray(a["L0_ffn_b2"].T)
    f = "L1_ffn_"
    for n in ("Wg", "Wsg", "We_gate", "We_up", "We_down", "Ws_gate", "Ws_up", "Ws_down"):
        del t[f + n]
    def chunks(rows):
        return np.ascontiguousarray(rows.reshape(-1, P, rows.shape[-1]).transpose(2, 0, 1))
    t[f + "router"] = np.ascontiguousarray(np.concatenate([a[f + "Wg"], a[f + "Wsg"]]).T)
    t[f + "gate"] = chunks(np.concatenate([a[f + "We_gate"].reshape(-1, D), a[f + "Ws_gate"]]))
    t[f + "up"] = chunks(np.concatenate([a[f + "We_up"].reshape(-1, D), a[f + "Ws_up"]]))
    down = np.concatenate([a[f + "We_down"].transpose(0, 2, 1).reshape(-1, D), a[f + "Ws_down"].T])
    t[f + "down"] = np.ascontiguousarray(down.reshape(-1, P, D).transpose(1, 0, 2))
    spread = np.zeros((3, 32, 10, P))
    for k in range(8):
        spread[:, 2 * k, k, :P // 2] = spread[:, 2 * k + 1, k, P // 2:] = 1
    spread[:, 16, 8:] = 1
    t["c_spread"] = spread.reshape(96, 10, P).astype(bf16)
    order = np.array([[2 * i + g, d] for g in range(2) for d in range(8) for i in range(8)])
    head, feat = order[:, 0], order[:, 1]
    f = "L0_attn_"
    for q in "qk":
        for c in range(2):
            t[f + f"W{q}{c}"] = np.ascontiguousarray(a[f + "W" + q][:, head * 16 + c * 8 + feat])
        del t[f + "W" + q]
    t[f + "Wo"] = np.ascontiguousarray(a[f + "Wo"].reshape(2, P, D).transpose(1, 0, 2))
    f = "L1_attn_"
    plain = np.arange(P)
    swap = plain // 8 * 8 + (plain + 4) % 8
    kv = lambda x: np.concatenate([x[..., i] for i in (plain // 8 * 16 + plain % 8, swap // 8 * 16 + swap % 8,
                                                       plain // 8 * 16 + 8 + plain % 8)], -1)
    t[f + "Wq"] = np.concatenate([a[f + "Wq"], a[f + "Wq"][:, swap]], 1)
    t[f + "Wkv"] = kv(a[f + "Wup"])
    t[f + "bqkv"] = np.concatenate([a[f + "bq"], a[f + "bq"][swap], kv(a[f + "bup"])])
    t[f + "bdown"] = a[f + "bdown"].reshape(-1, 1)
    t[f + "Wo"] = a[f + "Wout"]
    for n in ("Wup", "bup", "Wout", "bq"):
        del t[f + n]
    inv_freq = (1.0 / np.float32(10000.0) ** (np.arange(0, 8, 2, dtype=np.float32) / np.float32(8))).astype(np.float32)
    angle = (np.arange(T, dtype=np.float32)[:, None] * inv_freq[None, plain % 4]).astype(np.float32)
    sign = np.where(plain % 8 < 4, -1, 1)
    rope = np.concatenate([np.cos(angle), sign * np.sin(angle)] * 2, 1).astype(np.float32)
    t[f + "rope"] = np.ascontiguousarray(rope.reshape(J, P, 4 * P).transpose(1, 0, 2))
    for f in ("L0_attn_",):
        t[f + "minus_ones"] = np.full((3, 8, T), -1).astype(bf16)
    later = np.arange(P)[None, :] > np.arange(P)[:, None]
    t["c_causal_q"] = np.where(later, -1e30, 0).astype(bf16)
    t["c_causal_k"] = np.where(later.T, -1e30, 0).astype(bf16)
    t["c_ident"] = np.eye(P, dtype=np.float32)
    t["c_ident16"] = np.eye(P).astype(bf16)
    t["c_rank"] = np.tile(np.arange(16, 0, -1, dtype=np.float32), (P, 1))
    t["c_starts"] = np.tile(ROWS * np.arange(32, dtype=np.float32), (P, 1))
    t["c_earlier"] = np.triu(np.ones((P, P)), 1).astype(bf16)
    t["c_ones"] = np.ones((P, P)).astype(bf16)
    return t


STAGES = [(moe_top1_stage, "L0_ffn_"), (attention_stage, "L0_attn_"), (moe_top1_stage, "L0_ffn_"),
          (moe_top2_stage, "L1_ffn_"), (head_mixing_stage, "L1_attn_"), (moe_top2_stage, "L1_ffn_")]


def kernel(**inputs):
    import concourse.bacc as bacc
    from concourse.bass_utils import run_bass_kernel_spmd

    arrays = lay_out(inputs)
    nc = bacc.Bacc("TRN2", target_bir_lowering=False, num_devices=1)
    t = {k: nc.dram_tensor("in_" + k, v.shape, mybir.dt.from_np(v.dtype), kind="ExternalInput").ap()
         for k, v in arrays.items()}
    out = nc.dram_tensor("out_0", arrays["X"].shape, F32, kind="ExternalOutput").ap()
    build(nc, t, out, STAGES)
    result = run_bass_kernel_spmd(nc, [{"in_" + k: v for k, v in arrays.items()}], core_ids=[0])
    return result.results[0]["out_0"]
```
